# Optimizing a Trainium2 kernel written in Bass

```python
import numpy as np
import jax
import jax.numpy as jnp

def _softmax(x, axis=-1):
    return jax.nn.softmax(x, axis=axis)

def _gelu(x):
    return jax.nn.gelu(x, approximate=True)

def _silu(x):
    return jax.nn.silu(x)

def _sigmoid(x):
    return jax.nn.sigmoid(x)

def _layernorm(x, axis=-1, eps=1e-05):
    m = jnp.mean(x, axis=axis, keepdims=True)
    v = jnp.var(x, axis=axis, keepdims=True)
    return (x - m) / jnp.sqrt(v + eps)

def _scatter_add(tgt, idx, src, axis=0):
    return tgt.at[idx].add(src)

def _segment_sum(src, seg, n):
    return jax.ops.segment_sum(src, seg, n)
kernel_name = 'mk_prb_d1_jaxref_r8_91c94c'

def setup_inputs(seed: int=0):
    np.random.seed(seed)
    _w = jnp.asarray

    def _L0_attn_setup():
        import jax, jax.numpy as jnp
        import numpy as np
        from jax import lax
        D_MODEL = 128
        N_HEADS = 8
        D_HEAD = 64
        D_INNER = N_HEADS * D_HEAD
        B, T = (4, 512)
        LN_EPS = 1e-05
        NORM_EPS = 1e-12
        key = jax.random.key(seed)
        ks = jax.random.split(key, 6)
        s_proj = (2.0 / (D_MODEL + D_INNER)) ** 0.5
        x = jax.random.normal(ks[0], (B, T, D_MODEL), jnp.float32)
        Wq = jax.random.normal(ks[1], (D_MODEL, D_INNER), jnp.float32) * s_proj
        Wk = jax.random.normal(ks[2], (D_MODEL, D_INNER), jnp.float32) * s_proj
        Wv = jax.random.normal(ks[3], (D_MODEL, D_INNER), jnp.float32) * s_proj
        Wa = jax.random.normal(ks[4], (D_MODEL, D_INNER), jnp.float32) * s_proj
        ba = jnp.full((D_INNER,), 3.0, jnp.float32)
        Wo = jax.random.normal(ks[5], (D_INNER, D_MODEL), jnp.float32) * s_proj
        gamma = jnp.ones((D_MODEL,), jnp.float32)
        beta = jnp.zeros((D_MODEL,), jnp.float32)
        return {'x': x, 'Wq': Wq, 'Wk': Wk, 'Wv': Wv, 'Wa': Wa, 'ba': ba, 'Wo': Wo, 'gamma': gamma, 'beta': beta}
    _L0_attn_in = _L0_attn_setup()

    def _L0_ffn_setup():
        import jax, jax.numpy as jnp
        import numpy as np
        DIM = 128
        DEPTH = 6
        HEADS = 16
        DIM_HEAD = 64
        WINDOW = 32
        INNER = HEADS * DIM_HEAD
        DIM_INNER = int(DIM * 4 * 2 / 3)
        QK_SCALE = 8.0

        def shift_tokens(t):
            a, s = jnp.split(t, 2, -1)
            s = jnp.pad(s, ((0, 0), (1, 0), (0, 0)))[:, :-1]
            return jnp.concatenate([a, s], -1)

        def l2norm(t):
            return t / jnp.maximum(jnp.linalg.norm(t, axis=-1, keepdims=True), 1e-12)

        def rotate_half(x):
            x1, x2 = jnp.split(x, 2, -1)
            return jnp.concatenate([-x2, x1], -1)

        def rotary_tables(n):
            half = jnp.arange(0, DIM_HEAD, 2, dtype=jnp.float32)
            inv_freq = 1.0 / 10000.0 ** (half / DIM_HEAD)
            t = jnp.arange(n, dtype=jnp.float32)
            freqs = t[:, None] * inv_freq[None, :]
            freqs = jnp.concatenate([freqs, freqs], -1)
            base_scale = (half + 0.4 * DIM_HEAD) / (1.4 * DIM_HEAD)
            power = (t - n // 2) / (WINDOW // 2)
            scale = base_scale[None, :] ** power[:, None]
            scale = jnp.concatenate([scale, scale], -1)
            return (freqs, scale)

        def local_attention(q, k, v):
            b, h, n, d = q.shape
            w = WINDOW
            nw = n // w
            bq = q.reshape(b, h, nw, w, d)
            bk = k.reshape(b, h, nw, w, d)
            bv = v.reshape(b, h, nw, w, d)

            def look(t):
                p = jnp.pad(t, ((0, 0), (0, 0), (1, 0), (0, 0), (0, 0)))
                return jnp.concatenate([p[:, :, :nw], p[:, :, 1:]], axis=3)
            bk2, bv2 = (look(bk), look(bv))
            seq = jnp.arange(n).reshape(nw, w)
            seq_p = jnp.pad(seq, ((1, 0), (0, 0)), constant_values=-1)
            jt = jnp.concatenate([seq_p[:nw], seq_p[1:]], axis=1)
            it = seq[:, :, None]
            jb = jt[:, None, :]
            mask = (it < jb) | (it > jb + w) | (jb == -1)
            sim = jnp.einsum('bhwie,bhwje->bhwij', bq, bk2) * QK_SCALE
            sim = jnp.where(mask, -jnp.finfo(sim.dtype).max, sim)
            attn = jax.nn.softmax(sim, -1)
            out = jnp.einsum('bhwij,bhwje->bhwie', attn, bv2)
            return out.reshape(b, h, n, d)

        def attn_layer(x, Wqkv, qs, ksc, Wo):
            b, n, _ = x.shape
            qkv = x @ Wqkv
            q, k, v = jnp.split(qkv, 3, -1)
            sh = lambda t: t.reshape(b, n, HEADS, DIM_HEAD).transpose(0, 2, 1, 3)
            q, k, v = (sh(q), sh(k), sh(v))
            q = l2norm(q) * qs
            k = l2norm(k) * ksc
            freqs, scale = rotary_tables(n)
            cos, sin = (jnp.cos(freqs), jnp.sin(freqs))
            q = q * cos * scale + rotate_half(q) * sin * scale
            inv = 1.0 / scale
            k = k * cos * inv + rotate_half(k) * sin * inv
            out = local_attention(q, k, v)
            out = out.transpose(0, 2, 1, 3).reshape(b, n, INNER)
            return out @ Wo

        def ffn_layer(x, g, bln, W1, b1, W2, b2):
            mu = x.mean(-1, keepdims=True)
            var = ((x - mu) ** 2).mean(-1, keepdims=True)
            xn = (x - mu) / jnp.sqrt(var + 1e-05) * g + bln
            hg = xn @ W1 + b1
            a, gate = jnp.split(hg, 2, -1)
            return a * jax.nn.gelu(gate, approximate=False) @ W2 + b2
        key = jax.random.key(seed)
        ks = jax.random.split(key, 8)
        B, N = (2, 256)
        init = lambda k, shape: jax.random.normal(k, shape, jnp.float32) * 0.02
        return {'x': jax.random.normal(ks[0], (B, N, DIM), jnp.float32), 'Wqkv': init(ks[1], (DEPTH, DIM, 3 * INNER)), 'q_scale': jnp.ones((DEPTH, DIM_HEAD), jnp.float32), 'k_scale': jnp.ones((DEPTH, DIM_HEAD), jnp.float32), 'Wo': init(ks[2], (DEPTH, INNER, DIM)), 'ln_g': jnp.ones((DEPTH, DIM), jnp.float32), 'ln_b': jnp.zeros((DEPTH, DIM), jnp.float32), 'W1': init(ks[3], (DEPTH, DIM, 2 * DIM_INNER)), 'b1': jnp.zeros((DEPTH, 2 * DIM_INNER), jnp.float32), 'W2': init(ks[4], (DEPTH, DIM_INNER, DIM)), 'b2': jnp.zeros((DEPTH, DIM), jnp.float32)}
    _L0_ffn_in = _L0_ffn_setup()
    _d = {'L0_attn_x': _L0_attn_in['x'], 'L0_attn_Wq': _L0_attn_in['Wq'], 'L0_attn_Wk': _L0_attn_in['Wk'], 'L0_attn_Wv': _L0_attn_in['Wv'], 'L0_attn_Wa': _L0_attn_in['Wa'], 'L0_attn_ba': _L0_attn_in['ba'], 'L0_attn_Wo': _L0_attn_in['Wo'], 'L0_attn_gamma': _L0_attn_in['gamma'], 'L0_attn_beta': _L0_attn_in['beta'], 'L0_ffn_Wqkv': _L0_ffn_in['Wqkv'], 'L0_ffn_q_scale': _L0_ffn_in['q_scale'], 'L0_ffn_k_scale': _L0_ffn_in['k_scale'], 'L0_ffn_Wo': _L0_ffn_in['Wo'], 'L0_ffn_ln_g': _L0_ffn_in['ln_g'], 'L0_ffn_ln_b': _L0_ffn_in['ln_b'], 'L0_ffn_W1': _L0_ffn_in['W1'], 'L0_ffn_b1': _L0_ffn_in['b1'], 'L0_ffn_W2': _L0_ffn_in['W2'], 'L0_ffn_b2': _L0_ffn_in['b2']}
    _x0 = _d['L0_attn_x']
    _d['L0_attn_x'] = jax.random.normal(jax.random.fold_in(jax.random.key(seed), 1), (8, 512, 128), dtype=_x0.dtype)
    del _x0
    return _d

def reference(L0_attn_x, L0_attn_Wq, L0_attn_Wk, L0_attn_Wv, L0_attn_Wa, L0_attn_ba, L0_attn_Wo, L0_attn_gamma, L0_attn_beta, L0_ffn_Wqkv, L0_ffn_q_scale, L0_ffn_k_scale, L0_ffn_Wo, L0_ffn_ln_g, L0_ffn_ln_b, L0_ffn_W1, L0_ffn_b1, L0_ffn_W2, L0_ffn_b2):

    def _L0_attn_ref(x, Wq, Wk, Wv, Wa, ba, Wo, gamma, beta):
        import jax, jax.numpy as jnp
        import numpy as np
        from jax import lax
        D_MODEL = 128
        N_HEADS = 8
        D_HEAD = 64
        D_INNER = N_HEADS * D_HEAD
        B, T = (4, 512)
        LN_EPS = 1e-05
        NORM_EPS = 1e-12
        Bx, Tx, _ = x.shape
        residual = x
        mu = jnp.mean(x, axis=-1, keepdims=True)
        var = jnp.var(x, axis=-1, keepdims=True)
        xn = (x - mu) / jnp.sqrt(var + LN_EPS) * gamma + beta

        def heads(y):
            return jnp.moveaxis(y.reshape(Bx, Tx, N_HEADS, D_HEAD), 1, 0)
        q = heads(xn @ Wq)
        k = heads(xn @ Wk)
        v = heads(xn @ Wv)
        alpha = jax.nn.sigmoid(heads(xn @ Wa + ba))
        knorm = jnp.linalg.norm(k, axis=-1, keepdims=True)
        k = k / jnp.maximum(knorm, NORM_EPS)

        def step(S, inp):
            q_t, k_t, v_t, a_t = inp
            S = a_t[..., None] * S + k_t[..., None] * v_t[..., None, :]
            o_t = jnp.einsum('bhji,bhj->bhi', S, q_t)
            return (S, o_t)
        S0 = jnp.zeros((Bx, N_HEADS, D_HEAD, D_HEAD), x.dtype)
        _, outs = lax.scan(step, S0, (q, k, v, alpha))
        out = jnp.moveaxis(outs, 0, 1).reshape(Bx, Tx, D_INNER) @ Wo
        return out + residual

    def _L0_ffn_ref(x, Wqkv, q_scale, k_scale, Wo, ln_g, ln_b, W1, b1, W2, b2):
        import jax, jax.numpy as jnp
        import numpy as np
        DIM = 128
        DEPTH = 6
        HEADS = 16
        DIM_HEAD = 64
        WINDOW = 32
        INNER = HEADS * DIM_HEAD
        DIM_INNER = int(DIM * 4 * 2 / 3)
        QK_SCALE = 8.0

        def shift_tokens(t):
            a, s = jnp.split(t, 2, -1)
            s = jnp.pad(s, ((0, 0), (1, 0), (0, 0)))[:, :-1]
            return jnp.concatenate([a, s], -1)

        def l2norm(t):
            return t / jnp.maximum(jnp.linalg.norm(t, axis=-1, keepdims=True), 1e-12)

        def rotate_half(x):
            x1, x2 = jnp.split(x, 2, -1)
            return jnp.concatenate([-x2, x1], -1)

        def rotary_tables(n):
            half = jnp.arange(0, DIM_HEAD, 2, dtype=jnp.float32)
            inv_freq = 1.0 / 10000.0 ** (half / DIM_HEAD)
            t = jnp.arange(n, dtype=jnp.float32)
            freqs = t[:, None] * inv_freq[None, :]
            freqs = jnp.concatenate([freqs, freqs], -1)
            base_scale = (half + 0.4 * DIM_HEAD) / (1.4 * DIM_HEAD)
            power = (t - n // 2) / (WINDOW // 2)
            scale = base_scale[None, :] ** power[:, None]
            scale = jnp.concatenate([scale, scale], -1)
            return (freqs, scale)

        def local_attention(q, k, v):
            b, h, n, d = q.shape
            w = WINDOW
            nw = n // w
            bq = q.reshape(b, h, nw, w, d)
            bk = k.reshape(b, h, nw, w, d)
            bv = v.reshape(b, h, nw, w, d)

            def look(t):
                p = jnp.pad(t, ((0, 0), (0, 0), (1, 0), (0, 0), (0, 0)))
                return jnp.concatenate([p[:, :, :nw], p[:, :, 1:]], axis=3)
            bk2, bv2 = (look(bk), look(bv))
            seq = jnp.arange(n).reshape(nw, w)
            seq_p = jnp.pad(seq, ((1, 0), (0, 0)), constant_values=-1)
            jt = jnp.concatenate([seq_p[:nw], seq_p[1:]], axis=1)
            it = seq[:, :, None]
            jb = jt[:, None, :]
            mask = (it < jb) | (it > jb + w) | (jb == -1)
            sim = jnp.einsum('bhwie,bhwje->bhwij', bq, bk2) * QK_SCALE
            sim = jnp.where(mask, -jnp.finfo(sim.dtype).max, sim)
            attn = jax.nn.softmax(sim, -1)
            out = jnp.einsum('bhwij,bhwje->bhwie', attn, bv2)
            return out.reshape(b, h, n, d)

        def attn_layer(x, Wqkv, qs, ksc, Wo):
            b, n, _ = x.shape
            qkv = x @ Wqkv
            q, k, v = jnp.split(qkv, 3, -1)
            sh = lambda t: t.reshape(b, n, HEADS, DIM_HEAD).transpose(0, 2, 1, 3)
            q, k, v = (sh(q), sh(k), sh(v))
            q = l2norm(q) * qs
            k = l2norm(k) * ksc
            freqs, scale = rotary_tables(n)
            cos, sin = (jnp.cos(freqs), jnp.sin(freqs))
            q = q * cos * scale + rotate_half(q) * sin * scale
            inv = 1.0 / scale
            k = k * cos * inv + rotate_half(k) * sin * inv
            out = local_attention(q, k, v)
            out = out.transpose(0, 2, 1, 3).reshape(b, n, INNER)
            return out @ Wo

        def ffn_layer(x, g, bln, W1, b1, W2, b2):
            mu = x.mean(-1, keepdims=True)
            var = ((x - mu) ** 2).mean(-1, keepdims=True)
            xn = (x - mu) / jnp.sqrt(var + 1e-05) * g + bln
            hg = xn @ W1 + b1
            a, gate = jnp.split(hg, 2, -1)
            return a * jax.nn.gelu(gate, approximate=False) @ W2 + b2
        for i in range(DEPTH):
            x = attn_layer(shift_tokens(x), Wqkv[i], q_scale[i], k_scale[i], Wo[i]) + x
            x = ffn_layer(shift_tokens(x), ln_g[i], ln_b[i], W1[i], b1[i], W2[i], b2[i]) + x
        return x
    x = L0_attn_x
    xn = _layernorm(x, axis=-1)
    x = x + _L0_attn_ref(xn, L0_attn_Wq, L0_attn_Wk, L0_attn_Wv, L0_attn_Wa, L0_attn_ba, L0_attn_Wo, L0_attn_gamma, L0_attn_beta) + _L0_ffn_ref(xn, L0_ffn_Wqkv, L0_ffn_q_scale, L0_ffn_k_scale, L0_ffn_Wo, L0_ffn_ln_g, L0_ffn_ln_b, L0_ffn_W1, L0_ffn_b1, L0_ffn_W2, L0_ffn_b2)
    return x

_drawn_inputs = setup_inputs


def setup_inputs(seed=0):
    import zlib

    import numpy as np

    out = dict(_drawn_inputs(seed))
    spreads = {'L0_attn_ba': (3.0, 0.6),
     'L0_attn_gamma': (1.0, 0.581),
     'L0_attn_beta': (0.0, 0.8),
     'L0_ffn_q_scale': (1.0, 0.6),
     'L0_ffn_k_scale': (1.0, 0.6),
     'L0_ffn_ln_g': (1.0, 0.6),
     'L0_ffn_ln_b': (0.0, 0.8),
     'L0_ffn_b1': (0.0, 0.8),
     'L0_ffn_b2': (0.0, 0.556)}
    factors = {'L0_ffn_W1': 6.981, 'L0_ffn_W2': 6.857, 'L0_attn_Wa': 7.511}
    for name, (base, spread) in spreads.items():
        noise = np.random.default_rng([zlib.crc32(name.encode()), seed]).standard_normal(out[name].shape)
        drawn = base * np.exp(spread * noise) if base else spread * noise
        out[name] = jnp.asarray(drawn.astype(out[name].dtype))
    for name, factor in factors.items():
        out[name] = (out[name] * factor).astype(out[name].dtype)
    return out
```

```python
import concourse.bass as bass
from concourse import mybir
from contextlib import ExitStack

F32 = mybir.dt.float32
BF16 = mybir.dt.bfloat16
ALU = mybir.AluOpType
ACT = mybir.ActivationFunctionType
AX_X = mybir.AxisListType.X

SEQS, T, D = 8, 512, 128
P = 128
BLKS = T // P
LN_EPS = 1e-5
NORM_MIN2 = 1e-24

RH, RD = 8, 64
RHP = RH // 2
RI = RH * RD
LEVELS = 7
HALF = P // 2

DEPTH, AH, AD, WIN = 6, 16, 64, 32
AI = AH * AD
AHP = AH // 2
GROUPS = 2
GH = AH // GROUPS
GHP = GH // 2
UNITS = BLKS * GROUPS
WPB = P // WIN
QK_SCALE = 8.0
FF = int(D * 4 * 2 / 3)
FT = [(0, 128), (128, 128), (256, FF - 256)]
MASKED = -1e30


class Signal:

    def __init__(self, sem, per):
        self.sem, self.per = sem, per

    def upto(self, turn, n):
        return turn * self.per + n


def settle(engine, sem):
    engine.sem_inc(sem, 1)


class Chain:

    def __init__(self, counter, engine, turn):
        self.counter, self.engine, self.turn, self.n = counter, engine, turn, 0

    def link(self, instruction):
        self.n += 1
        instruction.then_inc(self.counter.sem, 1)
        self.engine.wait_ge(self.counter.sem, self.counter.upto(self.turn, self.n))

    def close(self):
        assert self.n == self.counter.per, (self.n, self.counter.per)


def bcast(ap, axis, n):
    ap = ap.unsqueeze(axis)
    shape = list(ap.shape)
    shape[axis] = n
    return ap.to_broadcast(shape)


def refine_rsqrt(nc, link, tmp, x, r0, out):
    link(nc.vector.tensor_tensor(tmp, r0, r0, ALU.mult))
    link(nc.vector.scalar_tensor_tensor(tmp, x, -0.5, tmp, ALU.mult, ALU.mult))
    link(nc.vector.scalar_tensor_tensor(out, tmp, 1.5, r0, ALU.add, ALU.mult))


def build(nc, a):
    with ExitStack() as ctx:
        def sb(name, shape, dt=F32):
            return ctx.enter_context(nc.sbuf_tensor(name, shape, dt))

        xst = sb("xst", [P, SEQS, T])
        acc = sb("acc", [P, SEQS, T])
        ident = sb("ident", [P, P])
        recurrence(nc, a, xst, acc, ident)
        layers(nc, a, xst, ident)
        combine(nc, a, xst, acc, ident)


def recurrence(nc, a, xst, acc, ident):
    ctx = ExitStack()
    with ctx:
        def sb(name, shape, dt=F32):
            return ctx.enter_context(nc.sbuf_tensor("r_" + name, shape, dt))

        def sig(name, per=1):
            return Signal(ctx.enter_context(nc.semaphore("r_" + name)), per)

        x_in = sb("x_in", [P, BLKS, D])
        xh = sb("xh", [P, BLKS, D])
        xh2 = sb("xh2", [P, BLKS, D])
        xsum = sb("xsum", [P, BLKS, D])
        stats = sb("stats", [P, BLKS, 6])
        mv = sb("mv", [P, BLKS, 2])
        mv2 = sb("mv2", [P, BLKS, 2])
        var = sb("var", [P, 2, BLKS])
        lnv = sb("lnv", [P, RH])
        r0 = sb("r0", [P, RH])
        tmp = sb("tmp", [P, RH])
        rstd = sb("rstd", [P, RH])
        xnT = sb("xnT", [P, T])
        wq, wk, wv, wa = (sb(n, [P, RI]) for n in ("wq", "wk", "wv", "wa"))
        wo = sb("wo", [P, RHP, D])
        vecs = sb("vecs", [P, RHP + 2])
        ba, gamma, beta = vecs[:, 0:RHP], vecs[:, RHP:RHP + 1], vecs[:, RHP + 1:RHP + 2]
        masks = sb("masks", [P, LEVELS, P])
        zeros = sb("zeros", [P, T], BF16)
        Q = sb("Q", [P, RHP, T + 4])
        K = sb("K", [P, RHP, T])
        decay = [sb(f"decay{i}", [P, RHP, T >> i]) for i in range(LEVELS + 1)]
        ksq = sb("ksq", [P, RI])
        kn2 = sb("kn2", [P, RH])
        ktok = sb("ktok", [P, RI])
        Vc = sb("Vc", [P, BLKS, RI])
        xleft = sb("xleft", [P, 2, 2, P])
        Kl = sb("Kl", [P, 2, BLKS * HALF])
        Vl = sb("Vl", [P, 2, 2, RI])
        PM = sb("PM", [P, 2, 2, 2, P])
        Kd = sb("Kd", [P, BLKS, P])
        S = sb("S", [P, RHP, BLKS + 1, RD])
        oT = sb("oT", [P, RHP, T + 4])

        pb = [ctx.enter_context(nc.psum_tensor(f"r_p{i}", [P, T], F32)) for i in range(6)]
        po, pv, pm = pb[0:4], pb[4], pb[5]
        pscores = ctx.enter_context(nc.psum_tensor("r_pscores", [P, 2, T], F32))
        psc = [pscores[:, 0, :], pscores[:, 1, :]]

        loaded = sig("loaded")
        x_loaded = sig("x_loaded", 16)
        x_used = sig("x_used")
        var_ready = sig("var_ready", 2 + BLKS)
        r0_ready = sig("r0_ready", 2 + BLKS)
        act_chain = sig("act_chain", 2 + BLKS)
        normed = sig("normed", 3)
        turned = sig("turned", 3)
        turned_out = sig("turned_out", 3)
        proj = sig("proj", 2 * RHP)
        proj_out = sig("proj_out", 2 * RHP)
        kproj = sig("kproj", BLKS)
        ksquares = sig("ksquares", BLKS)
        knormed = sig("knormed", BLKS)
        kturned = sig("kturned", BLKS)
        k_out = sig("k_out", BLKS)
        vproj = sig("vproj", BLKS + 2 * LEVELS)
        v_out = sig("v_out", BLKS + 2 * LEVELS)
        scored = sig("scored", 2 * LEVELS * RHP)
        masked = sig("masked", 2 * LEVELS * RHP)
        decayed = sig("decayed", LEVELS * RHP)
        summed = sig("summed", LEVELS * RHP)
        kd_turned = sig("kd_turned", RHP)
        kd_out = sig("kd_out", RHP)
        ds_ready = sig("ds_ready", RHP)
        state_ready = sig("state_ready", RHP)
        o_ready = sig("o_ready", RHP)
        o_out = sig("o_out", RHP + 1)
        y_ready = sig("y_ready")
        y_added = sig("y_added")
        lefts = sig("lefts", LEVELS)
        packed = sig("packed", LEVELS * RHP)
        chain_len = 2 * (3 * BLKS + 2) + 4 * BLKS + 2 * LEVELS * RHP + RHP * (BLKS - 1)
        chain = sig("chain", chain_len)
        set_up = sig("set_up")
        settled = sig("settled", 0)

        xin_d = a["L0_attn_x"].rearrange("s (b p) d -> s p b d", p=P)

        block = ctx.enter_context(nc.Block())

        @block.sync
        def _(sp):
            n = 0
            for dst, src in ((wq, a["L0_attn_Wq"]), (wk, a["L0_attn_Wk"]), (wv, a["L0_attn_Wv"]),
                             (wa, a["L0_attn_Wa"]), (ident, a["ident"]), (masks, a["level_masks"]),
                             (vecs, a["r_vectors"]),
                             (wo, a["L0_attn_Wo"].rearrange("(h p) d -> p h d", p=P))):
                sp.dma_start(dst[:], src).then_inc(loaded.sem, 16)
                n += 1
            assert n == 8
            with sp.Fori(0, SEQS) as b:
                sp.wait_ge(x_used.sem, x_used.upto(b, 1))
                sp.dma_start(x_in[:], xin_d[b]).then_inc(x_loaded.sem, 16)

        LOADED = 128

        @block.vector
        def _(dve):
            nc.vector.memset(zeros[:], 0.0)
            nc.vector.memset(Q[:], 0.0)
            nc.vector.memset(S[:], 0.0).then_inc(set_up.sem, 1)
            dve.wait_ge(set_up.sem, 1)
            dve.sem_inc(x_used.sem, 1)
            dve.wait_ge(loaded.sem, LOADED)
            with dve.Fori(0, SEQS) as b:
                ch = Chain(chain, dve, b)
                link = ch.link

                def normalise(src, mv_, out, which, signal, n):
                    for i in range(BLKS):
                        link(nc.vector.bn_stats(stats[:, i, :], src[:, i, :]))
                        settle(dve, settled.sem)
                        link(nc.vector.bn_aggr(mv_[:, i, :], stats[:, i, :]))
                    nc.vector.tensor_scalar(var[:, which, :], mv_[:, :, 1], LN_EPS, None, ALU.add).then_inc(var_ready.sem, 1)
                    dve.wait_ge(r0_ready.sem, r0_ready.upto(b, which + 1))
                    refine_rsqrt(nc, link, tmp[:, 0:BLKS], var[:, which, :], r0[:, 0:BLKS], rstd[:, 0:BLKS])
                    for i in range(BLKS - 1):
                        link(nc.vector.tensor_scalar(out[:, i, :], src[:, i, :], mv_[:, i, 0:1], rstd[:, i:i + 1],
                                                     ALU.subtract, ALU.mult))
                    i = BLKS - 1
                    nc.vector.tensor_scalar(out[:, i, :], src[:, i, :], mv_[:, i, 0:1], rstd[:, i:i + 1],
                                            ALU.subtract, ALU.mult).then_inc(signal.sem, 1)
                    dve.wait_ge(signal.sem, signal.upto(b, n))

                dve.wait_ge(x_loaded.sem, x_loaded.upto(b, 16))
                normalise(x_in, mv, xh, 0, normed, 1)
                normalise(xh, mv2, xh2, 1, normed, 2)
                nc.vector.tensor_tensor(xsum[:], x_in[:], xh[:], ALU.add).then_inc(normed.sem, 1)
                dve.wait_ge(normed.sem, normed.upto(b, 3))
                dve.sem_inc(x_used.sem, 1)
                for i in range(BLKS):
                    dve.wait_ge(ksquares.sem, ksquares.upto(b, i + 1))
                    link(nc.vector.reduce_sum(tmp[:], ksq[:].rearrange("p (h d) -> p h d", d=RD), axis=AX_X))
                    nc.vector.tensor_scalar(kn2[:], tmp[:], NORM_MIN2, None, ALU.max).then_inc(var_ready.sem, 1)
                    dve.wait_ge(r0_ready.sem, r0_ready.upto(b, 3 + i))
                    refine_rsqrt(nc, link, tmp[:], kn2[:], r0[:], rstd[:])
                    if i:
                        dve.wait_ge(kturned.sem, kturned.upto(b, i))
                    nc.vector.tensor_tensor(ktok[:].rearrange("p (h d) -> p h d", d=RD),
                                            pm[:].rearrange("p (h d) -> p h d", d=RD),
                                            bcast(rstd[:], 2, RD), ALU.mult).then_inc(knormed.sem, 1)
                dve.wait_ge(proj_out.sem, proj_out.upto(b, 2 * RHP))
                dve.wait_ge(k_out.sem, k_out.upto(b, BLKS))
                for lv in range(LEVELS):
                    h = 1 << lv
                    for hp in range(RHP):
                        k = lv * RHP + hp
                        if k >= 2:
                            dve.wait_ge(summed.sem, summed.upto(b, k - 1))
                        for e in range(2):
                            dve.wait_ge(scored.sem, scored.upto(b, 2 * k + e + 1))
                            products = pscores[:, e, 0:P].rearrange("p (c t) -> p c t", t=HALF)
                            mask = masks[:, lv, :].rearrange("p (a t) -> p a t", a=2)
                            nc.vector.tensor_tensor(PM[:, k % 2, e, :, :].rearrange("p c (a t) -> p c a t", a=2),
                                                    bcast(products, 2, 2), bcast(mask, 1, 2),
                                                    ALU.mult).then_inc(masked.sem, 1)
                        if lv:
                            dve.wait_ge(decayed.sem, decayed.upto(b, k - RHP + 1))
                        q_right = Q[:, hp, 0:T].rearrange("p (m s r) -> p m s r", s=2, r=h)[:, :, 1, :]
                        k_left = K[:, hp, :].rearrange("p (m s r) -> p m s r", s=2, r=h)[:, :, 0, :]
                        dve.wait_ge(packed.sem, packed.upto(b, k + 1))
                        dc = decay[lv][:, hp, :].rearrange("p (m s) -> p m s", s=2)
                        link(nc.vector.tensor_tensor(q_right, q_right, bcast(dc[:, :, 0], 2, h), ALU.mult))
                        link(nc.vector.tensor_tensor(k_left, k_left, bcast(dc[:, :, 1], 2, h), ALU.mult))
                        nc.vector.tensor_tensor(decay[lv + 1][:, hp, :], dc[:, :, 0], dc[:, :, 1],
                                                ALU.mult).then_inc(decayed.sem, 1)
                dve.wait_ge(decayed.sem, decayed.upto(b, LEVELS * RHP))
                for hp in range(RHP):
                    dve.wait_ge(ds_ready.sem, ds_ready.upto(b, hp + 1))
                    for c in range(BLKS):
                        step = nc.vector.scalar_tensor_tensor(
                            S[:, hp, c + 1, :], S[:, hp, c, :], decay[LEVELS][:, hp, c:c + 1],
                            psc[hp % 2][:, c * RD:(c + 1) * RD], ALU.mult, ALU.add)
                        if c < BLKS - 1:
                            link(step)
                        else:
                            step.then_inc(state_ready.sem, 1)
                ch.close()
                dve.wait_ge(y_ready.sem, y_ready.upto(b, 1))
                dve.wait_ge(turned_out.sem, turned_out.upto(b, 3))
                nc.vector.tensor_tensor(acc[:, bass.ds(b, 1), :], acc[:, bass.ds(b, 1), :],
                                        pv[:].unsqueeze(1), ALU.add).then_inc(y_added.sem, 1)
                dve.wait_ge(y_added.sem, y_added.upto(b, 1))

        @block.scalar
        def _(act):
            act.wait_ge(loaded.sem, LOADED)
            with act.Fori(0, SEQS) as b:
                ch = Chain(act_chain, act, b)

                def rsqrt_guess(which, src, width):
                    act.wait_ge(var_ready.sem, var_ready.upto(b, which + 1))
                    ch.link(nc.scalar.activation(lnv[:, 0:width], src, ACT.Ln))
                    nc.scalar.activation(r0[:, 0:width], lnv[:, 0:width], ACT.Exp, scale=-0.5).then_inc(r0_ready.sem, 1)

                rsqrt_guess(0, var[:, 0, :], BLKS)
                rsqrt_guess(1, var[:, 1, :], BLKS)
                act.wait_ge(turned.sem, turned.upto(b, 1))
                nc.scalar.copy(xst[:, bass.ds(b, 1), :], pm[:].unsqueeze(1)).then_inc(turned_out.sem, 1)
                act.wait_ge(turned.sem, turned.upto(b, 2))
                nc.scalar.activation(xnT[:], pv[:], ACT.Identity, bias=beta[:, 0:1], scale=gamma[:, 0:1]).then_inc(turned_out.sem, 1)
                act.wait_ge(turned.sem, turned.upto(b, 3))
                nc.scalar.copy(acc[:, bass.ds(b, 1), :], psc[0][:].unsqueeze(1)).then_inc(turned_out.sem, 1)
                for hp in range(RHP):
                    act.wait_ge(proj.sem, proj.upto(b, hp + 1))
                    nc.scalar.copy(Q[:, hp, 1:T + 1], psc[hp % 2][:]).then_inc(proj_out.sem, 1)
                for i in range(BLKS):
                    act.wait_ge(vproj.sem, vproj.upto(b, i + 1))
                    nc.scalar.copy(Vc[:, i, :], pv[:]).then_inc(v_out.sem, 1)
                for i in range(BLKS):
                    act.wait_ge(kproj.sem, kproj.upto(b, i + 1))
                    nc.scalar.activation(ksq[:], pm[:], ACT.Square).then_inc(ksquares.sem, 1)
                    rsqrt_guess(2 + i, kn2[:], RH)
                    act.wait_ge(kturned.sem, kturned.upto(b, i + 1))
                    nc.scalar.copy(K[:, :, i * P:(i + 1) * P],
                                   pv[:].rearrange("p (h t) -> p h t", t=P)).then_inc(k_out.sem, 1)
                for hp in range(RHP):
                    act.wait_ge(proj.sem, proj.upto(b, RHP + hp + 1))
                    nc.scalar.activation(decay[0][:, hp, :], psc[hp % 2][:], ACT.Sigmoid,
                                         bias=ba[:, hp:hp + 1]).then_inc(proj_out.sem, 1)
                def keep_values(lv):
                    for cp in range(2):
                        n = BLKS + 2 * lv + cp
                        act.wait_ge(vproj.sem, vproj.upto(b, n + 1))
                        if lv >= 2:
                            act.wait_ge(summed.sem, summed.upto(b, (lv - 1) * RHP))
                        nc.scalar.copy(Vl[:, lv % 2, cp, :], pv[:] if cp == 0 else pm[:]).then_inc(v_out.sem, 1)

                keep_values(0)
                act.wait_ge(k_out.sem, k_out.upto(b, BLKS))
                for k in range(LEVELS * RHP):
                    lv, hp = divmod(k, RHP)
                    h = 1 << lv
                    if hp == 1 and lv + 1 < LEVELS:
                        keep_values(lv + 1)
                    if lv:
                        act.wait_ge(decayed.sem, decayed.upto(b, k - RHP + 1))
                    if k >= 2:
                        act.wait_ge(scored.sem, scored.upto(b, 2 * (k - 1)))
                    nc.scalar.copy(Kl[:, k % 2, :].rearrange("p (m r) -> p m r", r=h),
                                   K[:, hp, :].rearrange("p (m s r) -> p m s r", s=2, r=h)[:, :, 0, :]).then_inc(packed.sem, 1)
                for hp in range(RHP):
                    act.wait_ge(kd_turned.sem, kd_turned.upto(b, hp + 1))
                    if hp:
                        act.wait_ge(ds_ready.sem, ds_ready.upto(b, hp))
                    nc.scalar.copy(Kd[:].rearrange("p c k -> p (c k)"), pv[:]).then_inc(kd_out.sem, 1)
                for hp in range(RHP):
                    act.wait_ge(o_ready.sem, o_ready.upto(b, hp + 1))
                    nc.scalar.copy(oT[:, hp, 0:T], po[hp][:]).then_inc(o_out.sem, 1)
                nc.scalar.copy(oT[:, :, T:T + 1], pm[:, 0:RHP].unsqueeze(2)).then_inc(o_out.sem, 1)
                ch.close()

        @block.gpsimd
        def _(pool):
            with pool.Fori(0, SEQS) as b:
                pool.wait_ge(turned_out.sem, turned_out.upto(b, 2))
                for lv in range(LEVELS):
                    h = 1 << lv
                    if lv >= 2:
                        pool.wait_ge(vproj.sem, vproj.upto(b, BLKS + 2 * (lv - 1)))
                    settle(pool, settled.sem)
                    nc.gpsimd.tensor_copy(xleft[:, lv % 2, :, :].rearrange("p c (m r) -> p (c m) r", r=h),
                                          xnT[:].rearrange("p (m s r) -> p m s r", s=2, r=h)[:, :, 0, :]).then_inc(lefts.sem, 1)

        @block.tensor
        def _(pe):
            pe.wait_ge(loaded.sem, LOADED)
            pe.wait_ge(set_up.sem, 1)
            mm = nc.tensor.matmul
            with pe.Fori(0, SEQS) as b:
                for n, (src, bank) in enumerate(((xh, pm), (xh2, pv), (xsum, psc[0]))):
                    pe.wait_ge(normed.sem, normed.upto(b, n + 1))
                    for i in range(BLKS):
                        last = nc.tensor.transpose(bank[:, i * P:(i + 1) * P], src[:, i, :], ident[:])
                    last.then_inc(turned.sem, 1)
                for hp in range(RHP):
                    mm(po[hp][:], zeros[:, 0:P], zeros[:], start=True, stop=False, skip_group_check=True)
                pe.wait_ge(turned_out.sem, turned_out.upto(b, 3))
                for hp in range(RHP):
                    if hp >= 2:
                        pe.wait_ge(proj_out.sem, proj_out.upto(b, hp - 1))
                    mm(psc[hp % 2][:], wq[:, hp * P:(hp + 1) * P], xnT[:], start=True, stop=True).then_inc(proj.sem, 1)
                for i in range(BLKS):
                    if i:
                        pe.wait_ge(v_out.sem, v_out.upto(b, i))
                    mm(pv[:], xnT[:, i * P:(i + 1) * P], wv[:], start=True, stop=True).then_inc(vproj.sem, 1)
                for i in range(BLKS):
                    if i:
                        pe.wait_ge(knormed.sem, knormed.upto(b, i))
                    mm(pm[:], xnT[:, i * P:(i + 1) * P], wk[:], start=True, stop=True).then_inc(kproj.sem, 1)
                    if i < 2:
                        pe.wait_ge(proj_out.sem, proj_out.upto(b, RHP - 1 + i))
                        mm(psc[i][:], wa[:, i * P:(i + 1) * P], xnT[:], start=True, stop=True).then_inc(proj.sem, 1)
                    pe.wait_ge(knormed.sem, knormed.upto(b, i + 1))
                    if i == 0:
                        pe.wait_ge(v_out.sem, v_out.upto(b, BLKS))
                    else:
                        pe.wait_ge(k_out.sem, k_out.upto(b, i))
                    for hp in range(RHP):
                        last = nc.tensor.transpose(pv[:, hp * P:(hp + 1) * P], ktok[:, hp * P:(hp + 1) * P], ident[:])
                    last.then_inc(kturned.sem, 1)
                for hp in range(2, RHP):
                    pe.wait_ge(proj_out.sem, proj_out.upto(b, RHP + hp - 1))
                    mm(psc[hp % 2][:], wa[:, hp * P:(hp + 1) * P], xnT[:], start=True, stop=True).then_inc(proj.sem, 1)

                def values_of(lv):
                    pe.wait_ge(lefts.sem, lefts.upto(b, lv + 1))
                    for cp in range(2):
                        if lv == 0:
                            pe.wait_ge(k_out.sem, k_out.upto(b, BLKS))
                        else:
                            pe.wait_ge(v_out.sem, v_out.upto(b, BLKS + 2 * (lv - 1) + cp + 1))
                        mm((pv if cp == 0 else pm)[:], xleft[:, lv % 2, cp, :], wv[:], start=True, stop=True).then_inc(vproj.sem, 1)

                def gather(k):
                    lv, hp = divmod(k, RHP)
                    h = 1 << lv
                    pe.wait_ge(masked.sem, masked.upto(b, 2 * (k + 1)))
                    pe.wait_ge(v_out.sem, v_out.upto(b, BLKS + 2 * (lv + 1)))
                    settle(pe, settled.sem)
                    for cp in range(2):
                        for e in range(2):
                            out = po[hp][RD * e:RD * e + RD, 2 * P * cp:2 * P * (cp + 1)].rearrange(
                                "p (m s r) -> p m s r", s=2, r=h)[:, :, 1, :]
                            head = 2 * hp + e
                            last = mm(out, Vl[:, lv % 2, cp, head * RD:(head + 1) * RD],
                                      PM[:, k % 2, e, cp, :].rearrange("p (m r) -> p m r", r=h),
                                      start=False, stop=False, skip_group_check=True)
                    last.then_inc(summed.sem, 1)

                values_of(0)
                pe.wait_ge(proj_out.sem, proj_out.upto(b, 2 * RHP))
                for k in range(LEVELS * RHP):
                    lv, hp = divmod(k, RHP)
                    h = 1 << lv
                    if hp == 1 and lv + 1 < LEVELS:
                        values_of(lv + 1)
                    pe.wait_ge(packed.sem, packed.upto(b, k + 1))
                    if lv:
                        pe.wait_ge(decayed.sem, decayed.upto(b, k - RHP + 1))
                    for e in range(2):
                        if k:
                            pe.wait_ge(masked.sem, masked.upto(b, 2 * (k - 1) + e + 1))
                        settle(pe, settled.sem)
                        rows = slice(RD * e, RD * e + RD)
                        for c in range(BLKS):
                            left = Kl[rows, k % 2, HALF * c:HALF * (c + 1)]
                            right = Q[rows, hp, P * c:P * (c + 1)].rearrange("p (m s r) -> p m s r", s=2, r=h)[:, :, 1, :]
                            col = HALF * (c // 2)
                            at = HALF * (c % 2)
                            last = mm(pscores[at:at + HALF, e, col:col + HALF], left, right, start=True, stop=True,
                                      skip_group_check=True)
                        last.then_inc(scored.sem, 1)
                    if k:
                        gather(k - 1)
                gather(LEVELS * RHP - 1)
                pe.wait_ge(decayed.sem, decayed.upto(b, LEVELS * RHP))
                pe.wait_ge(v_out.sem, v_out.upto(b, v_out.per))

                def turn_keys(hp):
                    if hp:
                        pe.wait_ge(kd_out.sem, kd_out.upto(b, hp))
                    for c in range(BLKS):
                        last = nc.tensor.transpose(pv[:, P * c:P * (c + 1)], K[:, hp, P * c:P * (c + 1)], ident[:])
                    last.then_inc(kd_turned.sem, 1)

                turn_keys(0)
                for hp in range(RHP):
                    pe.wait_ge(kd_out.sem, kd_out.upto(b, hp + 1))
                    if hp >= 2:
                        pe.wait_ge(state_ready.sem, state_ready.upto(b, hp - 1))
                    settle(pe, settled.sem)
                    for c in range(BLKS):
                        for e in range(2):
                            head = 2 * hp + e
                            last = mm(psc[hp % 2][RD * e:RD * e + RD, RD * c:RD * (c + 1)], Kd[:, c, RD * e:RD * e + RD],
                                      Vc[:, c, head * RD:(head + 1) * RD], start=True, stop=True, skip_group_check=True)
                    last.then_inc(ds_ready.sem, 1)
                    if hp + 1 < RHP:
                        turn_keys(hp + 1)
                for hp in range(RHP):
                    pe.wait_ge(state_ready.sem, state_ready.upto(b, hp + 1))
                    settle(pe, settled.sem)
                    for e in range(2):
                        rows = slice(RD * e, RD * e + RD)
                        for c in range(1, BLKS):
                            mm(po[hp][rows, P * c:P * (c + 1)], S[rows, hp, c, :], Q[rows, hp, P * c:P * (c + 1)],
                               start=False, stop=(c == BLKS - 1), skip_group_check=True)
                        last = mm(pm[rows, hp:hp + 1], S[rows, hp, BLKS, :], Q[rows, hp, T:T + 1],
                                  start=True, stop=True, skip_group_check=True)
                    last.then_inc(o_ready.sem, 1)
                pe.wait_ge(o_out.sem, o_out.upto(b, RHP + 1))
                for hp in range(RHP):
                    last = mm(pv[:], wo[:, hp, :], oT[:, hp, 1:T + 1], start=(hp == 0), stop=(hp == RHP - 1))
                last.then_inc(y_ready.sem, 1)
                pe.wait_ge(y_added.sem, y_added.upto(b, 1))


def layers(nc, a, xst, ident):
    ctx = ExitStack()
    with ctx:
        def sb(name, shape, dt=F32):
            return ctx.enter_context(nc.sbuf_tensor("l_" + name, shape, dt))

        def sig(name, per=1):
            return Signal(ctx.enter_context(nc.semaphore("l_" + name)), per)

        wqkv = sb("wqkv", [P, 3 * AI])
        wo = sb("wo", [P, AHP, D])
        w1 = sb("w1", [P, 2 * FF])
        w2 = sb("w2", [P, 3, D])
        vecs = sb("vecs", [P, 9])
        b1, b2, ln_g, ln_b = vecs[:, 0:6], vecs[:, 6:7], vecs[:, 7:8], vecs[:, 8:9]
        qk_row = sb("qk_row", [P, 2, AD])
        cos_base = sb("cos_base", [P, 2, BLKS, AD])
        sin_base = sb("sin_base", [P, 2, BLKS, AD])
        cos_t = sb("cos_t", [P, 2, BLKS, AD])
        sin_t = sb("sin_t", [P, 2, BLKS, AD])
        mask_f = sb("mask_f", [P, 2, GH * 2 * WIN])
        mask = sb("mask", [P, 2, GH * 2 * WIN], BF16)
        ident_b = sb("ident_b", [P, P], BF16)
        xs = sb("xs", [P, WIN + T])
        sq = sb("sq", [P, 2, GH * AD])
        ssq, n2, lnv, r0, rr = (sb(n, [P, 2 * GH]) for n in ("ssq", "n2", "lnv", "r0", "rr"))
        nt = sb("nt", [P, 2 * GH])
        qn = sb("qn", [P, 2, GH * AD])
        t1 = sb("t1", [P, 2, GH * AD])
        t2 = sb("t2", [P, 2, GH * AD])
        qT = sb("qT", [P, GHP, P])
        kT = sb("kT", [P, AHP, WIN + T])
        V = sb("V", [P, 2, WPB, AHP * AD])
        mx, rs, rinv = sb("mx", [P, GH]), sb("rs", [P, 2, GH]), sb("rinv", [P, 2, GH])
        sim = sb("sim", [P, GH * 2 * WIN])
        pr = sb("pr", [P, 2, GH * 2 * WIN])
        prT = sb("prT", [P, GHP, P])
        on = sb("on", [P, GH * AD])
        oT = sb("oT", [P, AHP, T])
        x1 = sb("x1", [P, T])
        xs1 = sb("xs1", [P, T + 4])
        stats = sb("stats", [P, BLKS, 6])
        mv = sb("mv", [P, BLKS, 2])
        xh = sb("xh", [P, BLKS, P])
        xnT = sb("xnT", [P, T])
        gl = sb("gl", [P, 3, T])
        hid = sb("hid", [P, 3, T])

        pqk = ctx.enter_context(nc.psum_tensor("l_pqk", [P, 2, T], F32))
        pq_t, pk_t, ps, po, pv, pm = (ctx.enter_context(nc.psum_tensor(f"l_p{i}", [P, T], F32)) for i in range(6))

        def up_banks():
            return [pqk[:, 0, :], pqk[:, 1, :], ps[:], po[:], pq_t[:], pm[:]]

        w_ready = sig("w_ready", 0)
        c_ready = sig("c_ready", 0)
        consts = sig("consts", 0)
        settled = sig("settled", 0)
        tables = sig("tables", 6)
        x_out = sig("x_out")
        xs_ready = sig("xs_ready", 2)
        qk_proj = sig("qk_proj", UNITS)
        squared = sig("squared", UNITS)
        n2_ready = sig("n2_ready", UNITS + 1)
        act_chain = sig("act_chain", UNITS + 1)
        r0_ready = sig("r0_ready", UNITS + 1)
        qn_ready = sig("qn_ready", UNITS)
        rotated = sig("rotated", 4 * UNITS)
        roped = sig("roped", UNITS)
        qk_turned = sig("qk_turned", UNITS)
        qk_out = sig("qk_out", 2 * UNITS)
        v_proj = sig("v_proj", WPB * BLKS)
        v_out = sig("v_out", WPB * BLKS)
        scored = sig("scored", 2 * UNITS)
        sim_ready = sig("sim_ready", UNITS)
        exped = sig("exped", UNITS)
        p_turned = sig("p_turned", UNITS)
        p_out = sig("p_out", UNITS)
        weighed = sig("weighed", 2 * UNITS)
        o_normed = sig("o_normed", UNITS)
        o_turned = sig("o_turned", UNITS)
        o_out = sig("o_out", UNITS)
        y_ready = sig("y_ready")
        x1_ready = sig("x1_ready", 3)
        x1_turned = sig("x1_turned")
        xh_ready = sig("xh_ready", 1)
        xh_turned = sig("xh_turned")
        xn_ready = sig("xn_ready")
        up = sig("up", 6)
        gated = sig("gated", 3)
        hid_ready = sig("hid_ready", 3)
        down = sig("down")
        chain = sig("chain", UNITS * 8 + 2 * BLKS + 3 + BLKS - 1)

        STEPS = UNITS + 3
        W_LAYER = 16 * 8

        block = ctx.enter_context(nc.Block())

        @block.sync
        def _(sp):
            sp.dma_start(cos_base[:], a["rope_cos"]).then_inc(c_ready.sem, 16)
            sp.dma_start(sin_base[:], a["rope_sin"]).then_inc(c_ready.sem, 16)
            sp.dma_start(mask_f[:], a["window_mask"]).then_inc(c_ready.sem, 16)
            with sp.Fori(0, DEPTH) as l:
                sp.wait_ge(x_out.sem, l * SEQS + 1)
                row = bass.ds(l, 1)
                pairs = [
                    (wqkv[:].unsqueeze(1), a["L0_ffn_Wqkv"][row].rearrange("l p n -> p l n")),
                    (qk_row[:, 0:1, :], a["L0_ffn_q_scale"][row].unsqueeze(0).to_broadcast([P, 1, AD])),
                    (qk_row[:, 1:2, :], a["L0_ffn_k_scale"][row].unsqueeze(0).to_broadcast([P, 1, AD])),
                    (wo[:].unsqueeze(1), a["L0_ffn_Wo"][row].rearrange("l (h p) d -> p l h d", p=P)),
                    (w1[:].unsqueeze(1), a["L0_ffn_W1"][row].rearrange("l p n -> p l n")),
                    (w2[:, 0:2, :].unsqueeze(1), a["L0_ffn_W2"][row, 0:256, :].rearrange("l (h p) d -> p l h d", p=P)),
                    (w2[0:FT[2][1], 2:3, :], a["L0_ffn_W2"][row, 256:FF, :].rearrange("l p d -> p l d")),
                    (vecs[:].unsqueeze(1), a["l_vectors"][row].rearrange("l p n -> p l n")),
                ]
                for dst, src in pairs:
                    sp.dma_start(dst, src).then_inc(w_ready.sem, 16)
                assert 16 * len(pairs) == W_LAYER

        @block.gpsimd
        def _(pool):
            pool.wait_ge(c_ready.sem, 48)
            with pool.Fori(0, DEPTH) as l:
                pool.wait_ge(w_ready.sem, l * W_LAYER + W_LAYER)
                for j in range(2):
                    nc.gpsimd.tensor_tensor(cos_t[:, j, :, :], cos_base[:, j, :, :],
                                            bcast(qk_row[:, j, :], 1, BLKS), ALU.mult).then_inc(tables.sem, 1)
                    for lo, hi in ((slice(0, 32), slice(32, 64)), (slice(32, 64), slice(0, 32))):
                        nc.gpsimd.tensor_tensor(sin_t[:, j, :, lo], sin_base[:, j, :, lo],
                                                bcast(qk_row[:, j, hi], 1, BLKS), ALU.mult).then_inc(tables.sem, 1)
                pool.wait_ge(tables.sem, tables.upto(l, 6))
                settle(pool, settled.sem)
                with pool.Fori(0, SEQS) as b:
                    it = l * SEQS + b
                    for u in range(UNITS):
                        m = u // GROUPS
                        pool.wait_ge(qn_ready.sem, qn_ready.upto(it, u + 1))
                        if u:
                            pool.wait_ge(roped.sem, roped.upto(it, u))
                        for j in range(2):
                            src = qn[:, j, :].rearrange("p (h d) -> p h d", d=AD)
                            dst = t2[:, j, :].rearrange("p (h d) -> p h d", d=AD)
                            for lo, hi in ((slice(0, 32), slice(32, 64)), (slice(32, 64), slice(0, 32))):
                                nc.gpsimd.tensor_tensor(dst[:, :, lo], src[:, :, hi], bcast(sin_t[:, j, m, lo], 1, GH),
                                                        ALU.mult).then_inc(rotated.sem, 1)

        @block.vector
        def _(dve):
            nc.vector.memset(xs[:], 0.0)
            nc.vector.memset(xs1[:], 0.0)
            nc.vector.memset(kT[:, :, 0:WIN], 0.0)
            dve.wait_ge(c_ready.sem, 48)
            nc.vector.tensor_copy(mask[:], mask_f[:])
            nc.vector.tensor_copy(ident_b[:], ident[:]).then_inc(consts.sem, 1)
            dve.wait_ge(consts.sem, 1)
            dve.sem_inc(x_out.sem, 1)
            with dve.Fori(0, DEPTH) as l:
                dve.wait_ge(w_ready.sem, l * W_LAYER + W_LAYER)
                dve.wait_ge(tables.sem, tables.upto(l, 6))
                settle(dve, settled.sem)
                with dve.Fori(0, SEQS) as b:
                    it = l * SEQS + b
                    ch = Chain(chain, dve, it)
                    link = ch.link
                    one = bass.ds(b, 1)
                    dve.wait_ge(x_out.sem, it + 1)
                    nc.vector.tensor_copy(xs[0:64, WIN:].unsqueeze(1), xst[0:64, one, :]).then_inc(xs_ready.sem, 1)
                    nc.vector.tensor_copy(xs[64:128, WIN + 1:].unsqueeze(1),
                                          xst[64:128, one, 0:T - 1]).then_inc(xs_ready.sem, 1)

                    def softmax_begin(u):
                        dve.wait_ge(scored.sem, scored.upto(it, 2 * u + 2))
                        scores = ps[:].rearrange("p (h k) -> p h k", k=2 * WIN)
                        link(nc.vector.reduce_max(mx[:], scores, axis=AX_X))
                        if u:
                            dve.wait_ge(exped.sem, exped.upto(it, u))
                        nc.vector.tensor_tensor(sim[:].rearrange("p (h k) -> p h k", k=2 * WIN), scores,
                                                bcast(mx[:], 2, 2 * WIN), ALU.subtract).then_inc(sim_ready.sem, 1)

                    def softmax_sum(u):
                        dve.wait_ge(exped.sem, exped.upto(it, u + 1))
                        link(nc.vector.reduce_sum(rs[:, u % 2, :], pr[:, u % 2, :].rearrange("p (h k) -> p h k", k=2 * WIN),
                                                  axis=AX_X))
                        link(nc.vector.reciprocal(rinv[:, u % 2, :], rs[:, u % 2, :]))

                    def norms(u):
                        dve.wait_ge(squared.sem, squared.upto(it, u + 1))
                        link(nc.vector.reduce_sum(ssq[:], sq[:].rearrange("p j (h d) -> p (j h) d", d=AD), axis=AX_X))
                        nc.vector.tensor_scalar(n2[:], ssq[:], NORM_MIN2, None, ALU.max).then_inc(n2_ready.sem, 1)

                    def rope_begin(u):
                        m = u // GROUPS
                        dve.wait_ge(r0_ready.sem, r0_ready.upto(it, u + 1))
                        refine_rsqrt(nc, link, nt[:], n2[:], r0[:], rr[:])
                        nc.vector.tensor_tensor(qn[:].rearrange("p j (h d) -> p (j h) d", d=AD),
                                                pqk[:].rearrange("p j (h d) -> p (j h) d", d=AD),
                                                bcast(rr[:], 2, AD), ALU.mult).then_inc(qn_ready.sem, 1)
                        dve.wait_ge(qn_ready.sem, qn_ready.upto(it, u + 1))
                        if u:
                            dve.wait_ge(qk_turned.sem, qk_turned.upto(it, u))
                        link(nc.vector.tensor_tensor(t1[:].rearrange("p j (h d) -> p j h d", d=AD),
                                                     qn[:].rearrange("p j (h d) -> p j h d", d=AD),
                                                     bcast(cos_t[:, :, m, :], 2, GH), ALU.mult))

                    def rope_end(u):
                        dve.wait_ge(rotated.sem, rotated.upto(it, 4 * u + 4))
                        nc.vector.tensor_tensor(t1[:], t1[:], t2[:], ALU.add).then_inc(roped.sem, 1)

                    def normalise_out(u):
                        dve.wait_ge(weighed.sem, weighed.upto(it, 2 * u + 2))
                        if u:
                            dve.wait_ge(o_turned.sem, o_turned.upto(it, u))
                        nc.vector.tensor_tensor(on[:].rearrange("p (h d) -> p h d", d=AD),
                                                po[:].rearrange("p (h d) -> p h d", d=AD),
                                                bcast(rinv[:, u % 2, :], 2, AD), ALU.mult).then_inc(o_normed.sem, 1)

                    for s in range(STEPS):
                        if 0 <= s - 1 < UNITS:
                            softmax_begin(s - 1)
                        if s < UNITS:
                            norms(s)
                        if 0 <= s - 1 < UNITS:
                            softmax_sum(s - 1)
                        if s < UNITS:
                            rope_begin(s)
                        if 0 <= s - 2 < UNITS:
                            normalise_out(s - 2)
                        if s < UNITS:
                            rope_end(s)
                    dve.wait_ge(y_ready.sem, y_ready.upto(it, 1))
                    nc.vector.tensor_tensor(xs1[0:64, 0:T].unsqueeze(1), pv[0:64, :].unsqueeze(1), xst[0:64, one, :],
                                            ALU.add).then_inc(x1_ready.sem, 1)
                    nc.vector.tensor_tensor(xs1[64:128, 1:T].unsqueeze(1), pv[64:128, 0:T - 1].unsqueeze(1),
                                            xst[64:128, one, 0:T - 1], ALU.add).then_inc(x1_ready.sem, 1)
                    nc.vector.tensor_tensor(x1[:].unsqueeze(1), pv[:].unsqueeze(1), xst[:, one, :],
                                            ALU.add).then_inc(x1_ready.sem, 1)
                    dve.wait_ge(x1_turned.sem, x1_turned.upto(it, 1))
                    for i in range(BLKS):
                        link(nc.vector.bn_stats(stats[:, i, :], pq_t[:, i * P:(i + 1) * P]))
                        settle(dve, settled.sem)
                        link(nc.vector.bn_aggr(mv[:, i, :], stats[:, i, :]))
                    nc.vector.tensor_scalar(n2[:, 0:BLKS], mv[:, :, 1], LN_EPS, None, ALU.add).then_inc(n2_ready.sem, 1)
                    dve.wait_ge(r0_ready.sem, r0_ready.upto(it, UNITS + 1))
                    refine_rsqrt(nc, link, nt[:, 0:BLKS], n2[:, 0:BLKS], r0[:, 0:BLKS], rr[:, 0:BLKS])
                    for i in range(BLKS):
                        step = nc.vector.tensor_scalar(xh[:, i, :], pq_t[:, i * P:(i + 1) * P], mv[:, i, 0:1],
                                                       rr[:, i:i + 1], ALU.subtract, ALU.mult)
                        if i < BLKS - 1:
                            link(step)
                        else:
                            step.then_inc(xh_ready.sem, 1)
                    banks = up_banks()
                    for j, (at, n) in enumerate(FT):
                        dve.wait_ge(gated.sem, gated.upto(it, j + 1))
                        dve.wait_ge(up.sem, up.upto(it, 2 * j + 2))
                        nc.vector.scalar_tensor_tensor(hid[0:n, j, :], banks[3 + j][0:n, :], b1[0:n, j:j + 1],
                                                       gl[0:n, j, :], ALU.add, ALU.mult).then_inc(hid_ready.sem, 1)
                    dve.wait_ge(down.sem, down.upto(it, 1))
                    dve.wait_ge(x1_ready.sem, x1_ready.upto(it, 3))
                    nc.vector.scalar_tensor_tensor(xst[:, one, :], pv[:].unsqueeze(1), b2[:, 0:1], x1[:].unsqueeze(1),
                                                   ALU.add, ALU.add).then_inc(x_out.sem, 1)
                    ch.close()

        @block.scalar
        def _(act):
            with act.Fori(0, DEPTH) as l:
                act.wait_ge(w_ready.sem, l * W_LAYER + W_LAYER)
                with act.Fori(0, SEQS) as b:
                    it = l * SEQS + b
                    ch = Chain(act_chain, act, it)

                    def rsqrt_guess(n, width):
                        act.wait_ge(n2_ready.sem, n2_ready.upto(it, n + 1))
                        ch.link(nc.scalar.activation(lnv[:, 0:width], n2[:, 0:width], ACT.Ln))
                        nc.scalar.activation(r0[:, 0:width], lnv[:, 0:width], ACT.Exp, scale=-0.5).then_inc(r0_ready.sem, 1)

                    for s in range(STEPS):
                        u = s - 3
                        if 0 <= u < UNITS:
                            m, g = divmod(u, GROUPS)
                            act.wait_ge(o_turned.sem, o_turned.upto(it, u + 1))
                            nc.scalar.copy(oT[:, g * GHP:(g + 1) * GHP, m * P:(m + 1) * P],
                                           pm[:].rearrange("p (h t) -> p h t", t=P)).then_inc(o_out.sem, 1)
                        u = s - 1
                        if 0 <= u < UNITS:
                            m, g = divmod(u, GROUPS)
                            act.wait_ge(qk_turned.sem, qk_turned.upto(it, u + 1))
                            nc.scalar.copy(qT[:].rearrange("p h t -> p (h t)"), pq_t[:]).then_inc(qk_out.sem, 1)
                            nc.scalar.copy(kT[:, g * GHP:(g + 1) * GHP, WIN + m * P:WIN + (m + 1) * P],
                                           pk_t[:].rearrange("p (h t) -> p h t", t=P)).then_inc(qk_out.sem, 1)
                        u = s - 2
                        if 0 <= u < UNITS:
                            act.wait_ge(p_turned.sem, p_turned.upto(it, u + 1))
                            nc.scalar.copy(prT[:].rearrange("p h t -> p (h t)"), pm[:]).then_inc(p_out.sem, 1)
                        if s < UNITS:
                            for w in (2 * s, 2 * s + 1):
                                act.wait_ge(v_proj.sem, v_proj.upto(it, w + 1))
                                nc.scalar.copy(V[:, (w // WPB) % 2, w % WPB, :], pv[:]).then_inc(v_out.sem, 1)
                        u = s - 1
                        if 0 <= u < UNITS:
                            act.wait_ge(sim_ready.sem, sim_ready.upto(it, u + 1))
                            if u >= 2:
                                act.wait_ge(p_turned.sem, p_turned.upto(it, u - 1))
                            nc.scalar.activation(pr[:, u % 2, :], sim[:], ACT.Exp, scale=QK_SCALE).then_inc(exped.sem, 1)
                        if s < UNITS:
                            act.wait_ge(qk_proj.sem, qk_proj.upto(it, s + 1))
                            nc.scalar.activation(sq[:], pqk[:], ACT.Square).then_inc(squared.sem, 1)
                            rsqrt_guess(s, 2 * GH)
                    rsqrt_guess(UNITS, BLKS)
                    act.wait_ge(xh_turned.sem, xh_turned.upto(it, 1))
                    nc.scalar.activation(xnT[:], pk_t[:], ACT.Identity, bias=ln_b[:, 0:1], scale=ln_g[:, 0:1]).then_inc(xn_ready.sem, 1)
                    banks = up_banks()
                    for j, (at, n) in enumerate(FT):
                        act.wait_ge(up.sem, up.upto(it, 2 * j + 1))
                        nc.scalar.activation(gl[0:n, j, :], banks[j][0:n, :], ACT.Gelu, bias=b1[0:n, 3 + j:4 + j]).then_inc(gated.sem, 1)
                    ch.close()

        @block.tensor
        def _(pe):
            mm = nc.tensor.matmul
            pe.wait_ge(consts.sem, 1)
            with pe.Fori(0, DEPTH) as l:
                pe.wait_ge(w_ready.sem, l * W_LAYER + W_LAYER)
                settle(pe, settled.sem)
                with pe.Fori(0, SEQS) as b:
                    it = l * SEQS + b
                    pe.wait_ge(xs_ready.sem, xs_ready.upto(it, 2))

                    def project(u):
                        m, g = divmod(u, GROUPS)
                        if u:
                            pe.wait_ge(qn_ready.sem, qn_ready.upto(it, u))
                        for j in range(2):
                            at = j * AI + g * GH * AD
                            last = mm(pqk[:, j, :], xs[:, WIN + m * P:WIN + (m + 1) * P], wqkv[:, at:at + GH * AD],
                                      start=True, stop=True)
                        last.then_inc(qk_proj.sem, 1)

                    def turn_qk(u):
                        pe.wait_ge(roped.sem, roped.upto(it, u + 1))
                        if u:
                            pe.wait_ge(qk_out.sem, qk_out.upto(it, 2 * u))
                        for j, bank in enumerate((pq_t, pk_t)):
                            for i in range(GHP):
                                last = nc.tensor.transpose(bank[:, i * P:(i + 1) * P], t1[:, j, i * P:(i + 1) * P], ident[:])
                        last.then_inc(qk_turned.sem, 1)

                    def values(w):
                        if w:
                            pe.wait_ge(v_out.sem, v_out.upto(it, w))
                        settle(pe, settled.sem)
                        for e in range(2):
                            cols = wqkv[:, 2 * AI:3 * AI].rearrange("p (h e d) -> p e h d", e=2, d=AD)[:, e, :, :]
                            last = mm(pv[64 * e:64 * e + 64, :], xs[:, WIN * w:WIN * w + 64], cols, start=True, stop=True,
                                      skip_group_check=True)
                        last.then_inc(v_proj.sem, 1)

                    def score(u, e):
                        m, g = divmod(u, GROUPS)
                        if e == 0:
                            pe.wait_ge(qk_out.sem, qk_out.upto(it, 2 * u + 2))
                            if u:
                                pe.wait_ge(sim_ready.sem, sim_ready.upto(it, u))
                            mm(ps[:], ident_b[:], mask[:, 0 if m == 0 else 1, :], start=True, stop=False, skip_group_check=True)
                        else:
                            pe.wait_ge(scored.sem, scored.upto(it, 2 * u + 1))
                            settle(pe, settled.sem)
                        rows = slice(64 * e, 64 * e + 64)
                        for h in range(e, GH, 2):
                            for w in range(WPB):
                                at = (m * WPB + w) * WIN
                                last = mm(ps[WIN * w:WIN * (w + 1), 2 * WIN * h:2 * WIN * (h + 1)],
                                          qT[rows, h // 2, WIN * w:WIN * (w + 1)],
                                          kT[rows, g * GHP + h // 2, at:at + 2 * WIN],
                                          start=False, stop=(h >= GH - 2), skip_group_check=True)
                        last.then_inc(scored.sem, 1)

                    def turn_p(u):
                        pe.wait_ge(exped.sem, exped.upto(it, u + 1))
                        if u:
                            pe.wait_ge(o_out.sem, o_out.upto(it, u))
                        for i in range(GHP):
                            last = nc.tensor.transpose(pm[:, i * P:(i + 1) * P], pr[:, u % 2, i * P:(i + 1) * P], ident[:])
                        last.then_inc(p_turned.sem, 1)

                    def weigh(u, e):
                        m, g = divmod(u, GROUPS)
                        if e == 0:
                            pe.wait_ge(p_out.sem, p_out.upto(it, u + 1))
                            if u:
                                pe.wait_ge(o_normed.sem, o_normed.upto(it, u))
                            pe.wait_ge(v_out.sem, v_out.upto(it, WPB * (m + 1)))
                        else:
                            pe.wait_ge(weighed.sem, weighed.upto(it, 2 * u + 1))
                        settle(pe, settled.sem)
                        rows = slice(64 * e, 64 * e + 64)
                        for h in range(e, GH, 2):
                            hp = g * GHP + h // 2
                            for w in range(WPB):
                                last = mm(po[WIN * w:WIN * (w + 1), AD * h:AD * (h + 1)],
                                          prT[rows, h // 2, WIN * w:WIN * (w + 1)],
                                          V[rows, m % 2, w, AD * hp:AD * (hp + 1)],
                                          start=True, stop=True, skip_group_check=True)
                        last.then_inc(weighed.sem, 1)

                    def turn_o(u):
                        pe.wait_ge(o_normed.sem, o_normed.upto(it, u + 1))
                        pe.wait_ge(p_out.sem, p_out.upto(it, u + 1))
                        for i in range(GHP):
                            last = nc.tensor.transpose(pm[:, i * P:(i + 1) * P], on[:, i * P:(i + 1) * P], ident[:])
                        last.then_inc(o_turned.sem, 1)

                    for s in range(STEPS):
                        if 0 <= s - 3 < UNITS:
                            turn_o(s - 3)
                        if 0 <= s - 1 < UNITS:
                            turn_qk(s - 1)
                        if 0 <= s - 2 < UNITS:
                            turn_p(s - 2)
                        if s < UNITS:
                            values(2 * s)
                        if 0 <= s - 1 < UNITS:
                            score(s - 1, 0)
                        if s < UNITS:
                            values(2 * s + 1)
                        if 0 <= s - 1 < UNITS:
                            score(s - 1, 1)
                        if 0 <= s - 2 < UNITS:
                            weigh(s - 2, 0)
                        if s < UNITS:
                            project(s)
                        if 0 <= s - 2 < UNITS:
                            weigh(s - 2, 1)
                    pe.wait_ge(o_out.sem, o_out.upto(it, UNITS))
                    for i in range(AHP):
                        last = mm(pv[:], wo[:, i, :], oT[:, i, :], start=(i == 0), stop=(i == AHP - 1))
                    last.then_inc(y_ready.sem, 1)
                    pe.wait_ge(x1_ready.sem, x1_ready.upto(it, 2))
                    for i in range(BLKS):
                        last = nc.tensor.transpose(pq_t[:, i * P:(i + 1) * P], xs1[:, i * P:(i + 1) * P], ident[:])
                    last.then_inc(x1_turned.sem, 1)
                    pe.wait_ge(xh_ready.sem, xh_ready.upto(it, 1))
                    for i in range(BLKS):
                        last = nc.tensor.transpose(pk_t[:, i * P:(i + 1) * P], xh[:, i, :], ident[:])
                    last.then_inc(xh_turned.sem, 1)
                    pe.wait_ge(xn_ready.sem, xn_ready.upto(it, 1))
                    banks = up_banks()
                    for j, (at, n) in enumerate(FT):
                        mm(banks[j][0:n, :], w1[:, FF + at:FF + at + n], xnT[:], start=True, stop=True).then_inc(up.sem, 1)
                        mm(banks[3 + j][0:n, :], w1[:, at:at + n], xnT[:], start=True, stop=True).then_inc(up.sem, 1)
                    pe.wait_ge(x1_ready.sem, x1_ready.upto(it, 3))
                    for j, (at, n) in enumerate(FT):
                        pe.wait_ge(hid_ready.sem, hid_ready.upto(it, j + 1))
                        last = mm(pv[:], w2[0:n, j, :], hid[0:n, j, :], start=(j == 0), stop=(j == 2))
                    last.then_inc(down.sem, 1)


def combine(nc, a, xst, acc, ident):
    ctx = ExitStack()
    with ctx:
        res = ctx.enter_context(nc.sbuf_tensor("c_res", [P, 2, T], F32))
        tok = ctx.enter_context(nc.sbuf_tensor("c_tok", [P, 2, T], F32))
        banks = [ctx.enter_context(nc.psum_tensor(f"c_p{i}", [P, T], F32)) for i in range(2)]
        added, turned, copied, stored = (ctx.enter_context(nc.semaphore("c_" + n)) for n in ("added", "turned", "copied", "stored"))
        out_d = a["out"].rearrange("s (b p) d -> s p b d", p=P)
        block = ctx.enter_context(nc.Block())

        @block.vector
        def _(dve):
            for b in range(SEQS):
                if b >= 2:
                    dve.wait_ge(turned, b - 1)
                nc.vector.tensor_tensor(res[:, b % 2, :], xst[:, b, :], acc[:, b, :], ALU.add).then_inc(added, 1)

        @block.tensor
        def _(pe):
            for b in range(SEQS):
                pe.wait_ge(added, b + 1)
                if b >= 2:
                    pe.wait_ge(copied, b - 1)
                for i in range(BLKS):
                    last = nc.tensor.transpose(banks[b % 2][:, i * P:(i + 1) * P], res[:, b % 2, i * P:(i + 1) * P], ident[:])
                last.then_inc(turned, 1)

        @block.scalar
        def _(act):
            for b in range(SEQS):
                act.wait_ge(turned, b + 1)
                if b >= 2:
                    act.wait_ge(stored, 16 * (b - 1))
                nc.scalar.copy(tok[:, b % 2, :], banks[b % 2][:]).then_inc(copied, 1)

        @block.sync
        def _(sp):
            for b in range(SEQS):
                sp.wait_ge(copied, b + 1)
                if b:
                    sp.wait_ge(stored, 16 * b)
                sp.dma_start(out_d[b], tok[:, b % 2, :].rearrange("p (b d) -> p b d", d=D)).then_inc(stored, 16)
            sp.wait_ge(stored, 16 * SEQS)


_INS = ["L0_attn_x", "L0_attn_Wq", "L0_attn_Wk", "L0_attn_Wv", "L0_attn_Wa", "L0_attn_Wo",
        "L0_ffn_Wqkv", "L0_ffn_q_scale", "L0_ffn_k_scale", "L0_ffn_Wo", "L0_ffn_W1", "L0_ffn_W2"]


def vectors(inputs):
    import numpy as np
    ba = np.asarray(inputs["L0_attn_ba"]).reshape(RHP, P)
    r = np.stack([*ba, np.asarray(inputs["L0_attn_gamma"]), np.asarray(inputs["L0_attn_beta"])], 1)
    b1 = np.asarray(inputs["L0_ffn_b1"])
    out = np.zeros((DEPTH, P, 9), b1.dtype)
    for part in range(2):
        for j, (at, n) in enumerate(FT):
            out[:, 0:n, 3 * part + j] = b1[:, part * FF + at:part * FF + at + n]
    for j, name in enumerate(("L0_ffn_b2", "L0_ffn_ln_g", "L0_ffn_ln_b")):
        out[:, :, 6 + j] = np.asarray(inputs[name])
    return {"r_vectors": np.ascontiguousarray(r), "l_vectors": out}


def shape_constants():
    import numpy as np
    f = np.float32
    half = np.arange(0, AD, 2, dtype=f)
    inv_freq = (f(1.0) / np.power(f(10000.0), half / f(AD))).astype(f)
    t = np.arange(T, dtype=f)
    freqs = (t[:, None] * inv_freq[None, :]).astype(f)
    freqs = np.concatenate([freqs, freqs], -1)
    base = ((half + f(0.4 * AD)) / f(1.4 * AD)).astype(f)
    power = ((t - T // 2) / f(WIN // 2)).astype(f)
    scale = np.power(base[None, :], power[:, None]).astype(f)
    scale = np.concatenate([scale, scale], -1)
    sign = np.where(np.arange(AD) < AD // 2, f(-1), f(1))
    cos, sin = np.cos(freqs), np.sin(freqs) * sign
    both = lambda x: np.ascontiguousarray(
        np.stack([x * scale, x / scale]).reshape(2, BLKS, P, AD).transpose(2, 0, 1, 3).astype(f))
    i = np.arange(P) % WIN
    key = np.arange(2 * WIN)
    prev = key[None, :] < WIN
    ok = np.where(prev, key[None, :] >= i[:, None], key[None, :] - WIN <= i[:, None])
    first_window = (np.arange(P) < WIN)[:, None] & prev
    m = np.where(ok, f(0), f(MASKED))
    m0 = np.where(first_window, f(MASKED), m)
    window_mask = np.stack([np.tile(m0, (1, GH)), np.tile(m, (1, GH))], 1).astype(f)
    p, j = np.arange(P) % HALF, np.arange(HALF)
    same = np.stack([(p[:, None] >> lv) == (j[None, :] >> lv) for lv in range(LEVELS)], 1)
    own = (np.arange(P)[:, None] // HALF) == np.arange(2)[None, :]
    level = (own[:, None, :, None] & same[:, :, None, :]).reshape(P, LEVELS, P).astype(f)
    return {"ident": np.eye(P, dtype=f), "level_masks": level, "rope_cos": both(cos), "rope_sin": both(sin),
            "window_mask": window_mask}


def kernel(**inputs):
    import numpy as np
    import concourse.bacc as bacc
    from concourse.bass_utils import run_bass_kernel_spmd

    nc = bacc.Bacc("TRN2", target_bir_lowering=False, num_devices=1)
    arrays, aps = {}, {}
    for name in _INS:
        arrays[name + "_dram"] = np.ascontiguousarray(inputs[name])
    for name, table in {**vectors(inputs), **shape_constants()}.items():
        arrays[name + "_dram"] = table
    for key, x in arrays.items():
        aps[key[:-5]] = nc.dram_tensor(key, x.shape, mybir.dt.from_np(x.dtype), kind="ExternalInput").ap()
    aps["out"] = nc.dram_tensor("out_dram", (SEQS, T, D), F32, kind="ExternalOutput").ap()
    build(nc, aps)
    r = run_bass_kernel_spmd(nc, [arrays], core_ids=[0])
    return r.results[0]["out_dram"]
```

```python
import concourse.bass as bass
from concourse import mybir
from contextlib import ExitStack

F32 = mybir.dt.float32
BF16 = mybir.dt.bfloat16
ALU = mybir.AluOpType
ACT = mybir.ActivationFunctionType
AX_X = mybir.AxisListType.X

SEQS, T, D = 8, 512, 128
P = 128
BLKS = T // P
LN_EPS = 1e-5
NORM_MIN2 = 1e-24

RH, RD = 8, 64
RHP = RH // 2
RI = RH * RD
LEVELS = 7
HALF = P // 2

DEPTH, AH, AD, WIN = 6, 16, 64, 32
AI = AH * AD
AHP = AH // 2
GROUPS = 2
GH = AH // GROUPS
GHP = GH // 2
UNITS = BLKS * GROUPS
WPB = P // WIN
QK_SCALE = 8.0
FF = int(D * 4 * 2 / 3)
FT = [(0, 128), (128, 128), (256, FF - 256)]
MASKED = -1e30


class Counted:

    def __init__(self, sem, per):
        self.sem, self.per = sem, per

    def upto(self, turn, n):
        return turn * self.per + n


def settle(engine, sem):
    engine.sem_inc(sem, 1)


def wait_for(engine, counted, turn, n):
    if isinstance(turn, int) and counted.upto(turn, n) <= 0:
        return
    engine.wait_ge(counted.sem, counted.upto(turn, n))


class Parts:

    def __init__(self, attention, before, ffn, ffn_end):
        self.attention, self.before, self.ffn, self.ffn_end = attention, before, ffn, ffn_end
        self.next = attention

    def has(self, unit):
        return self.attention if unit >= 0 else self.before


class Chain:

    def __init__(self, counter, engine, turn):
        self.counter, self.engine, self.turn, self.n = counter, engine, turn, 0

    def link(self, instruction):
        self.n += 1
        instruction.then_inc(self.counter.sem, 1)
        self.engine.wait_ge(self.counter.sem, self.counter.upto(self.turn, self.n))

    def close(self):
        assert self.n == self.counter.per, (self.n, self.counter.per)


def bcast(ap, axis, n):
    ap = ap.unsqueeze(axis)
    shape = list(ap.shape)
    shape[axis] = n
    return ap.to_broadcast(shape)


def refine_rsqrt(nc, link, tmp, x, r0, out):
    link(nc.vector.tensor_tensor(tmp, r0, r0, ALU.mult))
    link(nc.vector.scalar_tensor_tensor(tmp, x, -0.5, tmp, ALU.mult, ALU.mult))
    link(nc.vector.scalar_tensor_tensor(out, tmp, 1.5, r0, ALU.add, ALU.mult))


def build(nc, a):
    with ExitStack() as ctx:
        def sb(name, shape, dt=F32):
            return ctx.enter_context(nc.sbuf_tensor(name, shape, dt))

        xst = sb("xst", [P, SEQS, T])
        acc = sb("acc", [P, SEQS, T])
        ident = sb("ident", [P, P])
        recurrence(nc, a, xst, acc, ident)
        layers(nc, a, xst, ident)
        combine(nc, a, xst, acc, ident)


def recurrence(nc, a, xst, acc, ident):
    ctx = ExitStack()
    with ctx:
        def sb(name, shape, dt=F32):
            return ctx.enter_context(nc.sbuf_tensor("r_" + name, shape, dt))

        def sig(name, per=1):
            return Counted(ctx.enter_context(nc.semaphore("r_" + name)), per)

        x_in = sb("x_in", [P, BLKS, D])
        xh = sb("xh", [P, BLKS, D])
        xh2 = sb("xh2", [P, BLKS, D])
        xsum = sb("xsum", [P, BLKS, D])
        stats = sb("stats", [P, BLKS, 6])
        mv = sb("mv", [P, BLKS, 2])
        mv2 = sb("mv2", [P, BLKS, 2])
        var = sb("var", [P, 2, BLKS])
        lnv = sb("lnv", [P, RH])
        r0 = sb("r0", [P, RH])
        tmp = sb("tmp", [P, RH])
        rstd = sb("rstd", [P, RH])
        xnT = sb("xnT", [P, T])
        wq, wk, wv, wa = (sb(n, [P, RI]) for n in ("wq", "wk", "wv", "wa"))
        wo = sb("wo", [P, RHP, D])
        vecs = sb("vecs", [P, RHP + 2])
        ba, gamma, beta = vecs[:, 0:RHP], vecs[:, RHP:RHP + 1], vecs[:, RHP + 1:RHP + 2]
        masks = sb("masks", [P, LEVELS, P])
        zeros = sb("zeros", [P, T], BF16)
        Q = sb("Q", [P, RHP, T + 4])
        K = sb("K", [P, RHP, T])
        decay = [sb(f"decay{i}", [P, RHP, T >> i]) for i in range(LEVELS + 1)]
        ksq = sb("ksq", [P, RI])
        kn2 = sb("kn2", [P, RH])
        ktok = sb("ktok", [P, RI])
        Vc = sb("Vc", [P, BLKS, RI])
        xleft = sb("xleft", [P, 2, 2, P])
        Kl = sb("Kl", [P, 2, BLKS * HALF])
        Vl = sb("Vl", [P, 2, 2, RI])
        PM = sb("PM", [P, 2, 2, 2, P])
        Kd = sb("Kd", [P, BLKS, P])
        S = sb("S", [P, RHP, BLKS + 1, RD])
        oT = sb("oT", [P, RHP, T + 4])

        pb = [ctx.enter_context(nc.psum_tensor(f"r_p{i}", [P, T], F32)) for i in range(6)]
        po, pv, pm = pb[0:4], pb[4], pb[5]
        pscores = ctx.enter_context(nc.psum_tensor("r_pscores", [P, 2, T], F32))
        psc = [pscores[:, 0, :], pscores[:, 1, :]]

        loaded = sig("loaded")
        x_loaded = sig("x_loaded", 16)
        x_used = sig("x_used")
        var_ready = sig("var_ready", 2 + BLKS)
        r0_ready = sig("r0_ready", 2 + BLKS)
        act_chain = sig("act_chain", 2 + BLKS)
        normed = sig("normed", 3)
        turned = sig("turned", 3)
        turned_out = sig("turned_out", 3)
        proj = sig("proj", 2 * RHP)
        proj_out = sig("proj_out", 2 * RHP)
        kproj = sig("kproj", BLKS)
        ksquares = sig("ksquares", BLKS)
        knormed = sig("knormed", BLKS)
        kturned = sig("kturned", BLKS)
        k_out = sig("k_out", BLKS)
        vproj = sig("vproj", BLKS + 2 * LEVELS)
        v_out = sig("v_out", BLKS + 2 * LEVELS)
        scored = sig("scored", 2 * LEVELS * RHP)
        masked = sig("masked", 2 * LEVELS * RHP)
        decayed = sig("decayed", LEVELS * RHP)
        summed = sig("summed", LEVELS * RHP)
        kd_turned = sig("kd_turned", RHP)
        kd_out = sig("kd_out", RHP)
        ds_ready = sig("ds_ready", RHP)
        state_ready = sig("state_ready", RHP)
        o_ready = sig("o_ready", RHP)
        o_out = sig("o_out", RHP + 1)
        y_ready = sig("y_ready")
        y_added = sig("y_added")
        lefts = sig("lefts", LEVELS)
        packed = sig("packed", LEVELS * RHP)
        chain_len = 2 * (3 * BLKS + 2) + 4 * BLKS + 2 * LEVELS * RHP + RHP * (BLKS - 1)
        chain = sig("chain", chain_len)
        set_up = sig("set_up")
        settled = sig("settled", 0)

        xin_d = a["L0_attn_x"].rearrange("s (b p) d -> s p b d", p=P)

        block = ctx.enter_context(nc.Block())

        @block.sync
        def _(sp):
            n = 0
            for dst, src in ((wq, a["L0_attn_Wq"]), (wk, a["L0_attn_Wk"]), (wv, a["L0_attn_Wv"]),
                             (wa, a["L0_attn_Wa"]), (ident, a["ident"]), (masks, a["level_masks"]),
                             (vecs, a["r_vectors"]),
                             (wo, a["L0_attn_Wo"].rearrange("(h p) d -> p h d", p=P))):
                sp.dma_start(dst[:], src).then_inc(loaded.sem, 16)
                n += 1
            assert n == 8
            with sp.Fori(0, SEQS) as b:
                sp.wait_ge(x_used.sem, x_used.upto(b, 1))
                sp.dma_start(x_in[:], xin_d[b]).then_inc(x_loaded.sem, 16)

        LOADED = 128

        @block.vector
        def _(dve):
            nc.vector.memset(zeros[:], 0.0)
            nc.vector.memset(Q[:], 0.0)
            nc.vector.memset(S[:], 0.0).then_inc(set_up.sem, 1)
            dve.wait_ge(set_up.sem, 1)
            dve.sem_inc(x_used.sem, 1)
            dve.wait_ge(loaded.sem, LOADED)
            with dve.Fori(0, SEQS) as b:
                ch = Chain(chain, dve, b)
                link = ch.link

                def normalise(src, mv_, out, which, signal, n):
                    for i in range(BLKS):
                        link(nc.vector.bn_stats(stats[:, i, :], src[:, i, :]))
                        settle(dve, settled.sem)
                        link(nc.vector.bn_aggr(mv_[:, i, :], stats[:, i, :]))
                    nc.vector.tensor_scalar(var[:, which, :], mv_[:, :, 1], LN_EPS, None, ALU.add).then_inc(var_ready.sem, 1)
                    dve.wait_ge(r0_ready.sem, r0_ready.upto(b, which + 1))
                    refine_rsqrt(nc, link, tmp[:, 0:BLKS], var[:, which, :], r0[:, 0:BLKS], rstd[:, 0:BLKS])
                    for i in range(BLKS - 1):
                        link(nc.vector.tensor_scalar(out[:, i, :], src[:, i, :], mv_[:, i, 0:1], rstd[:, i:i + 1],
                                                     ALU.subtract, ALU.mult))
                    i = BLKS - 1
                    nc.vector.tensor_scalar(out[:, i, :], src[:, i, :], mv_[:, i, 0:1], rstd[:, i:i + 1],
                                            ALU.subtract, ALU.mult).then_inc(signal.sem, 1)
                    dve.wait_ge(signal.sem, signal.upto(b, n))

                dve.wait_ge(x_loaded.sem, x_loaded.upto(b, 16))
                normalise(x_in, mv, xh, 0, normed, 1)
                normalise(xh, mv2, xh2, 1, normed, 2)
                nc.vector.tensor_tensor(xsum[:], x_in[:], xh[:], ALU.add).then_inc(normed.sem, 1)
                dve.wait_ge(normed.sem, normed.upto(b, 3))
                dve.sem_inc(x_used.sem, 1)
                for i in range(BLKS):
                    dve.wait_ge(ksquares.sem, ksquares.upto(b, i + 1))
                    link(nc.vector.reduce_sum(tmp[:], ksq[:].rearrange("p (h d) -> p h d", d=RD), axis=AX_X))
                    nc.vector.tensor_scalar(kn2[:], tmp[:], NORM_MIN2, None, ALU.max).then_inc(var_ready.sem, 1)
                    dve.wait_ge(r0_ready.sem, r0_ready.upto(b, 3 + i))
                    refine_rsqrt(nc, link, tmp[:], kn2[:], r0[:], rstd[:])
                    if i:
                        dve.wait_ge(kturned.sem, kturned.upto(b, i))
                    nc.vector.tensor_tensor(ktok[:].rearrange("p (h d) -> p h d", d=RD),
                                            pm[:].rearrange("p (h d) -> p h d", d=RD),
                                            bcast(rstd[:], 2, RD), ALU.mult).then_inc(knormed.sem, 1)
                dve.wait_ge(proj_out.sem, proj_out.upto(b, 2 * RHP))
                dve.wait_ge(k_out.sem, k_out.upto(b, BLKS))
                for lv in range(LEVELS):
                    h = 1 << lv
                    for hp in range(RHP):
                        k = lv * RHP + hp
                        if k >= 2:
                            dve.wait_ge(summed.sem, summed.upto(b, k - 1))
                        for e in range(2):
                            dve.wait_ge(scored.sem, scored.upto(b, 2 * k + e + 1))
                            products = pscores[:, e, 0:P].rearrange("p (c t) -> p c t", t=HALF)
                            mask = masks[:, lv, :].rearrange("p (a t) -> p a t", a=2)
                            nc.vector.tensor_tensor(PM[:, k % 2, e, :, :].rearrange("p c (a t) -> p c a t", a=2),
                                                    bcast(products, 2, 2), bcast(mask, 1, 2),
                                                    ALU.mult).then_inc(masked.sem, 1)
                        if lv:
                            dve.wait_ge(decayed.sem, decayed.upto(b, k - RHP + 1))
                        q_right = Q[:, hp, 0:T].rearrange("p (m s r) -> p m s r", s=2, r=h)[:, :, 1, :]
                        k_left = K[:, hp, :].rearrange("p (m s r) -> p m s r", s=2, r=h)[:, :, 0, :]
                        dve.wait_ge(packed.sem, packed.upto(b, k + 1))
                        dc = decay[lv][:, hp, :].rearrange("p (m s) -> p m s", s=2)
                        link(nc.vector.tensor_tensor(q_right, q_right, bcast(dc[:, :, 0], 2, h), ALU.mult))
                        link(nc.vector.tensor_tensor(k_left, k_left, bcast(dc[:, :, 1], 2, h), ALU.mult))
                        nc.vector.tensor_tensor(decay[lv + 1][:, hp, :], dc[:, :, 0], dc[:, :, 1],
                                                ALU.mult).then_inc(decayed.sem, 1)
                dve.wait_ge(decayed.sem, decayed.upto(b, LEVELS * RHP))
                for hp in range(RHP):
                    dve.wait_ge(ds_ready.sem, ds_ready.upto(b, hp + 1))
                    for c in range(BLKS):
                        step = nc.vector.scalar_tensor_tensor(
                            S[:, hp, c + 1, :], S[:, hp, c, :], decay[LEVELS][:, hp, c:c + 1],
                            psc[hp % 2][:, c * RD:(c + 1) * RD], ALU.mult, ALU.add)
                        if c < BLKS - 1:
                            link(step)
                        else:
                            step.then_inc(state_ready.sem, 1)
                ch.close()
                dve.wait_ge(y_ready.sem, y_ready.upto(b, 1))
                dve.wait_ge(turned_out.sem, turned_out.upto(b, 3))
                nc.vector.tensor_tensor(acc[:, bass.ds(b, 1), :], acc[:, bass.ds(b, 1), :],
                                        pv[:].unsqueeze(1), ALU.add).then_inc(y_added.sem, 1)
                dve.wait_ge(y_added.sem, y_added.upto(b, 1))

        @block.scalar
        def _(act):
            act.wait_ge(loaded.sem, LOADED)
            with act.Fori(0, SEQS) as b:
                ch = Chain(act_chain, act, b)

                nc.scalar.preload_act_table_set("natural_log_exp_and_others")

                def rsqrt_guess(which, src, width):
                    act.wait_ge(var_ready.sem, var_ready.upto(b, which + 1))
                    ch.link(nc.scalar.activation(lnv[:, 0:width], src, ACT.Ln))
                    nc.scalar.activation(r0[:, 0:width], lnv[:, 0:width], ACT.Exp, scale=-0.5).then_inc(r0_ready.sem, 1)

                rsqrt_guess(0, var[:, 0, :], BLKS)
                rsqrt_guess(1, var[:, 1, :], BLKS)
                act.wait_ge(turned.sem, turned.upto(b, 1))
                nc.scalar.copy(xst[:, bass.ds(b, 1), :], pm[:].unsqueeze(1)).then_inc(turned_out.sem, 1)
                act.wait_ge(turned.sem, turned.upto(b, 2))
                nc.scalar.activation(xnT[:], pv[:], ACT.Identity, bias=beta[:, 0:1], scale=gamma[:, 0:1]).then_inc(turned_out.sem, 1)
                act.wait_ge(turned.sem, turned.upto(b, 3))
                nc.scalar.copy(acc[:, bass.ds(b, 1), :], psc[0][:].unsqueeze(1)).then_inc(turned_out.sem, 1)
                for hp in range(RHP):
                    act.wait_ge(proj.sem, proj.upto(b, hp + 1))
                    nc.scalar.copy(Q[:, hp, 1:T + 1], psc[hp % 2][:]).then_inc(proj_out.sem, 1)
                for i in range(BLKS):
                    act.wait_ge(vproj.sem, vproj.upto(b, i + 1))
                    nc.scalar.copy(Vc[:, i, :], pv[:]).then_inc(v_out.sem, 1)
                for i in range(BLKS):
                    act.wait_ge(kproj.sem, kproj.upto(b, i + 1))
                    nc.scalar.activation(ksq[:], pm[:], ACT.Square).then_inc(ksquares.sem, 1)
                    rsqrt_guess(2 + i, kn2[:], RH)
                    act.wait_ge(kturned.sem, kturned.upto(b, i + 1))
                    nc.scalar.copy(K[:, :, i * P:(i + 1) * P],
                                   pv[:].rearrange("p (h t) -> p h t", t=P)).then_inc(k_out.sem, 1)
                for hp in range(RHP):
                    act.wait_ge(proj.sem, proj.upto(b, RHP + hp + 1))
                    nc.scalar.activation(decay[0][:, hp, :], psc[hp % 2][:], ACT.Sigmoid,
                                         bias=ba[:, hp:hp + 1]).then_inc(proj_out.sem, 1)
                def keep_values(lv):
                    for cp in range(2):
                        n = BLKS + 2 * lv + cp
                        act.wait_ge(vproj.sem, vproj.upto(b, n + 1))
                        if lv >= 2:
                            act.wait_ge(summed.sem, summed.upto(b, (lv - 1) * RHP))
                        nc.scalar.copy(Vl[:, lv % 2, cp, :], pv[:] if cp == 0 else pm[:]).then_inc(v_out.sem, 1)

                keep_values(0)
                act.wait_ge(k_out.sem, k_out.upto(b, BLKS))
                for k in range(LEVELS * RHP):
                    lv, hp = divmod(k, RHP)
                    h = 1 << lv
                    if hp == 1 and lv + 1 < LEVELS:
                        keep_values(lv + 1)
                    if lv:
                        act.wait_ge(decayed.sem, decayed.upto(b, k - RHP + 1))
                    if k >= 2:
                        act.wait_ge(scored.sem, scored.upto(b, 2 * (k - 1)))
                    nc.scalar.copy(Kl[:, k % 2, :].rearrange("p (m r) -> p m r", r=h),
                                   K[:, hp, :].rearrange("p (m s r) -> p m s r", s=2, r=h)[:, :, 0, :]).then_inc(packed.sem, 1)
                for hp in range(RHP):
                    act.wait_ge(kd_turned.sem, kd_turned.upto(b, hp + 1))
                    if hp:
                        act.wait_ge(ds_ready.sem, ds_ready.upto(b, hp))
                    nc.scalar.copy(Kd[:].rearrange("p c k -> p (c k)"), pv[:]).then_inc(kd_out.sem, 1)
                for hp in range(RHP):
                    act.wait_ge(o_ready.sem, o_ready.upto(b, hp + 1))
                    nc.scalar.copy(oT[:, hp, 0:T], po[hp][:]).then_inc(o_out.sem, 1)
                nc.scalar.copy(oT[:, :, T:T + 1], pm[:, 0:RHP].unsqueeze(2)).then_inc(o_out.sem, 1)
                ch.close()

        @block.gpsimd
        def _(pool):
            with pool.Fori(0, SEQS) as b:
                pool.wait_ge(turned_out.sem, turned_out.upto(b, 2))
                for lv in range(LEVELS):
                    h = 1 << lv
                    if lv >= 2:
                        pool.wait_ge(vproj.sem, vproj.upto(b, BLKS + 2 * (lv - 1)))
                    settle(pool, settled.sem)
                    nc.gpsimd.tensor_copy(xleft[:, lv % 2, :, :].rearrange("p c (m r) -> p (c m) r", r=h),
                                          xnT[:].rearrange("p (m s r) -> p m s r", s=2, r=h)[:, :, 0, :]).then_inc(lefts.sem, 1)

        @block.tensor
        def _(pe):
            pe.wait_ge(loaded.sem, LOADED)
            pe.wait_ge(set_up.sem, 1)
            mm = nc.tensor.matmul
            with pe.Fori(0, SEQS) as b:
                for n, (src, bank) in enumerate(((xh, pm), (xh2, pv), (xsum, psc[0]))):
                    pe.wait_ge(normed.sem, normed.upto(b, n + 1))
                    for i in range(BLKS):
                        last = nc.tensor.transpose(bank[:, i * P:(i + 1) * P], src[:, i, :], ident[:])
                    last.then_inc(turned.sem, 1)
                for hp in range(RHP):
                    mm(po[hp][:], zeros[:, 0:P], zeros[:], start=True, stop=False, skip_group_check=True)
                pe.wait_ge(turned_out.sem, turned_out.upto(b, 3))
                for hp in range(RHP):
                    if hp >= 2:
                        pe.wait_ge(proj_out.sem, proj_out.upto(b, hp - 1))
                    mm(psc[hp % 2][:], wq[:, hp * P:(hp + 1) * P], xnT[:], start=True, stop=True).then_inc(proj.sem, 1)
                for i in range(BLKS):
                    if i:
                        pe.wait_ge(v_out.sem, v_out.upto(b, i))
                    mm(pv[:], xnT[:, i * P:(i + 1) * P], wv[:], start=True, stop=True).then_inc(vproj.sem, 1)
                for i in range(BLKS):
                    if i:
                        pe.wait_ge(knormed.sem, knormed.upto(b, i))
                    mm(pm[:], xnT[:, i * P:(i + 1) * P], wk[:], start=True, stop=True).then_inc(kproj.sem, 1)
                    if i < 2:
                        pe.wait_ge(proj_out.sem, proj_out.upto(b, RHP - 1 + i))
                        mm(psc[i][:], wa[:, i * P:(i + 1) * P], xnT[:], start=True, stop=True).then_inc(proj.sem, 1)
                    pe.wait_ge(knormed.sem, knormed.upto(b, i + 1))
                    if i == 0:
                        pe.wait_ge(v_out.sem, v_out.upto(b, BLKS))
                    else:
                        pe.wait_ge(k_out.sem, k_out.upto(b, i))
                    for hp in range(RHP):
                        last = nc.tensor.transpose(pv[:, hp * P:(hp + 1) * P], ktok[:, hp * P:(hp + 1) * P], ident[:])
                    last.then_inc(kturned.sem, 1)
                for hp in range(2, RHP):
                    pe.wait_ge(proj_out.sem, proj_out.upto(b, RHP + hp - 1))
                    mm(psc[hp % 2][:], wa[:, hp * P:(hp + 1) * P], xnT[:], start=True, stop=True).then_inc(proj.sem, 1)

                def values_of(lv):
                    pe.wait_ge(lefts.sem, lefts.upto(b, lv + 1))
                    for cp in range(2):
                        if lv == 0:
                            pe.wait_ge(k_out.sem, k_out.upto(b, BLKS))
                        else:
                            pe.wait_ge(v_out.sem, v_out.upto(b, BLKS + 2 * (lv - 1) + cp + 1))
                        mm((pv if cp == 0 else pm)[:], xleft[:, lv % 2, cp, :], wv[:], start=True, stop=True).then_inc(vproj.sem, 1)

                def gather(k):
                    lv, hp = divmod(k, RHP)
                    h = 1 << lv
                    pe.wait_ge(masked.sem, masked.upto(b, 2 * (k + 1)))
                    pe.wait_ge(v_out.sem, v_out.upto(b, BLKS + 2 * (lv + 1)))
                    settle(pe, settled.sem)
                    for cp in range(2):
                        for e in range(2):
                            out = po[hp][RD * e:RD * e + RD, 2 * P * cp:2 * P * (cp + 1)].rearrange(
                                "p (m s r) -> p m s r", s=2, r=h)[:, :, 1, :]
                            head = 2 * hp + e
                            last = mm(out, Vl[:, lv % 2, cp, head * RD:(head + 1) * RD],
                                      PM[:, k % 2, e, cp, :].rearrange("p (m r) -> p m r", r=h),
                                      start=False, stop=False, skip_group_check=True)
                    last.then_inc(summed.sem, 1)

                values_of(0)
                pe.wait_ge(proj_out.sem, proj_out.upto(b, 2 * RHP))
                for k in range(LEVELS * RHP):
                    lv, hp = divmod(k, RHP)
                    h = 1 << lv
                    if hp == 1 and lv + 1 < LEVELS:
                        values_of(lv + 1)
                    pe.wait_ge(packed.sem, packed.upto(b, k + 1))
                    if lv:
                        pe.wait_ge(decayed.sem, decayed.upto(b, k - RHP + 1))
                    for e in range(2):
                        if k:
                            pe.wait_ge(masked.sem, masked.upto(b, 2 * (k - 1) + e + 1))
                        settle(pe, settled.sem)
                        rows = slice(RD * e, RD * e + RD)
                        for c in range(BLKS):
                            left = Kl[rows, k % 2, HALF * c:HALF * (c + 1)]
                            right = Q[rows, hp, P * c:P * (c + 1)].rearrange("p (m s r) -> p m s r", s=2, r=h)[:, :, 1, :]
                            col = HALF * (c // 2)
                            at = HALF * (c % 2)
                            last = mm(pscores[at:at + HALF, e, col:col + HALF], left, right, start=True, stop=True,
                                      skip_group_check=True)
                        last.then_inc(scored.sem, 1)
                    if k:
                        gather(k - 1)
                gather(LEVELS * RHP - 1)
                pe.wait_ge(decayed.sem, decayed.upto(b, LEVELS * RHP))
                pe.wait_ge(v_out.sem, v_out.upto(b, v_out.per))

                def turn_keys(hp):
                    if hp:
                        pe.wait_ge(kd_out.sem, kd_out.upto(b, hp))
                    for c in range(BLKS):
                        last = nc.tensor.transpose(pv[:, P * c:P * (c + 1)], K[:, hp, P * c:P * (c + 1)], ident[:])
                    last.then_inc(kd_turned.sem, 1)

                turn_keys(0)
                for hp in range(RHP):
                    pe.wait_ge(kd_out.sem, kd_out.upto(b, hp + 1))
                    if hp >= 2:
                        pe.wait_ge(state_ready.sem, state_ready.upto(b, hp - 1))
                    settle(pe, settled.sem)
                    for c in range(BLKS):
                        for e in range(2):
                            head = 2 * hp + e
                            last = mm(psc[hp % 2][RD * e:RD * e + RD, RD * c:RD * (c + 1)], Kd[:, c, RD * e:RD * e + RD],
                                      Vc[:, c, head * RD:(head + 1) * RD], start=True, stop=True, skip_group_check=True)
                    last.then_inc(ds_ready.sem, 1)
                    if hp + 1 < RHP:
                        turn_keys(hp + 1)
                for hp in range(RHP):
                    pe.wait_ge(state_ready.sem, state_ready.upto(b, hp + 1))
                    settle(pe, settled.sem)
                    for e in range(2):
                        rows = slice(RD * e, RD * e + RD)
                        for c in range(1, BLKS):
                            mm(po[hp][rows, P * c:P * (c + 1)], S[rows, hp, c, :], Q[rows, hp, P * c:P * (c + 1)],
                               start=False, stop=(c == BLKS - 1), skip_group_check=True)
                        last = mm(pm[rows, hp:hp + 1], S[rows, hp, BLKS, :], Q[rows, hp, T:T + 1],
                                  start=True, stop=True, skip_group_check=True)
                    last.then_inc(o_ready.sem, 1)
                pe.wait_ge(o_out.sem, o_out.upto(b, RHP + 1))
                for hp in range(RHP):
                    last = mm(pv[:], wo[:, hp, :], oT[:, hp, 1:T + 1], start=(hp == 0), stop=(hp == RHP - 1))
                last.then_inc(y_ready.sem, 1)
                pe.wait_ge(y_added.sem, y_added.upto(b, 1))


def layers(nc, a, xst, ident):
    ctx = ExitStack()
    with ctx:
        def sb(name, shape, dt=F32):
            return ctx.enter_context(nc.sbuf_tensor("l_" + name, shape, dt))

        def sig(name, per=1):
            return Counted(ctx.enter_context(nc.semaphore("l_" + name)), per)

        wqkv = sb("wqkv", [P, 3 * AI])
        wo = sb("wo", [P, AHP, D])
        w1 = sb("w1", [P, 2 * FF])
        w2 = sb("w2", [P, 3, D])
        vecs = sb("vecs", [P, 9])
        b1, b2, ln_g, ln_b = vecs[:, 0:6], vecs[:, 6:7], vecs[:, 7:8], vecs[:, 8:9]
        qk_rows = sb("qk_rows", [P, DEPTH, 2, AD])
        cos_base = sb("cos_base", [P, 2, BLKS, AD])
        sin_base = sb("sin_base", [P, 2, BLKS, AD])
        cos_t = sb("cos_t", [P, 2, BLKS, AD])
        sin_t = sb("sin_t", [P, 2, BLKS, AD])
        mask_f = sb("mask_f", [P, 2, GH * 2 * WIN])
        mask = sb("mask", [P, 2, GH * 2 * WIN], BF16)
        ident_b = sb("ident_b", [P, P], BF16)
        xs = sb("xs", [P, WIN + T])
        sq = sb("sq", [P, 2, GH * AD])
        ssq, n2, lnv, r0, rr, nt = (sb(n, [P, 2 * GH]) for n in ("ssq", "n2", "lnv", "r0", "rr", "nt"))
        qn = sb("qn", [P, 2, GH * AD])
        t1 = sb("t1", [P, 2, GH * AD])
        t2 = sb("t2", [P, 2, GH * AD])
        qT = sb("qT", [P, GHP, P])
        kT = sb("kT", [P, AHP, WIN + T])
        V = sb("V", [P, 2, WPB, AHP * AD])
        mx, rs, rinv = sb("mx", [P, GH]), sb("rs", [P, 2, GH]), sb("rinv", [P, 2, GH])
        sim = sb("sim", [P, GH * 2 * WIN])
        pr = sb("pr", [P, 2, GH * 2 * WIN])
        prT = sb("prT", [P, GHP, P])
        on = sb("on", [P, GH * AD])
        oT = sb("oT", [P, AHP, T])
        x1 = sb("x1", [P, T])
        xs1 = sb("xs1", [P, T])
        stats = sb("stats", [P, BLKS, 6])
        mv = sb("mv", [P, BLKS, 2])
        fn2, flnv, fr0, frr, fnt = (sb(n, [P, BLKS]) for n in ("fn2", "flnv", "fr0", "frr", "fnt"))
        xh = sb("xh", [P, BLKS, P])
        xnT = sb("xnT", [P, T])
        gpre = sb("gpre", [P, 3, T])
        gl = sb("gl", [P, 3, T])
        hid = sb("hid", [P, 3, T])

        pqk = ctx.enter_context(nc.psum_tensor("l_pqk", [P, 2, T], F32))
        pta, ptb, ps, po, pv, pf = (ctx.enter_context(nc.psum_tensor(f"l_p{i}", [P, T], F32)) for i in range(6))

        c_ready = sig("c_ready", 0)
        w_ready = sig("w_ready", 0)
        consts = sig("consts", 0)
        settled = sig("settled", 0)
        att_ok = sig("att_ok")
        ffn_ok = sig("ffn_ok")
        tables = sig("tables", 6)
        tables_ok = sig("tables_ok")
        x_out = sig("x_out")
        xs_ready = sig("xs_ready", 2)
        qk_proj = sig("qk_proj", UNITS)
        squared = sig("squared", UNITS)
        ssq_ready = sig("ssq_ready", UNITS)
        n2_ready = sig("n2_ready", UNITS)
        ln_ready = sig("ln_ready", UNITS)
        r0_ready = sig("r0_ready", UNITS)
        refined = sig("refined", 3 * UNITS)
        qn_ready = sig("qn_ready", UNITS)
        cosed = sig("cosed", UNITS)
        rotated = sig("rotated", 4 * UNITS)
        roped = sig("roped", UNITS)
        q_turned, k_turned = sig("q_turned", UNITS), sig("k_turned", UNITS)
        q_out, k_out = sig("q_out", UNITS), sig("k_out", UNITS)
        v_proj = sig("v_proj", WPB * BLKS)
        v_out = sig("v_out", WPB * BLKS)
        scored = sig("scored", 2 * UNITS)
        max_ready = sig("max_ready", UNITS)
        sim_ready = sig("sim_ready", UNITS)
        exped = sig("exped", UNITS)
        sums = sig("sums", 2 * UNITS)
        p_turned = sig("p_turned", UNITS)
        p_out = sig("p_out", UNITS)
        weighed = sig("weighed", 2 * UNITS)
        o_normed = sig("o_normed", UNITS)
        o_turned = sig("o_turned", UNITS)
        o_out = sig("o_out", UNITS)
        y_ready = sig("y_ready")
        x1_ready = sig("x1_ready")
        xs1_ready = sig("xs1_ready", 2)
        x1_turned = sig("x1_turned")
        ln_steps = sig("ln_steps", 2 * BLKS + 3 + BLKS - 1)
        fn2_ready, fln_ready, fr0_ready = sig("fn2_ready"), sig("fln_ready"), sig("fr0_ready")
        xh_ready = sig("xh_ready")
        xh_turned = sig("xh_turned")
        xn_ready = sig("xn_ready")
        up = sig("up", 6)
        g_out = sig("g_out", 3)
        gelued = sig("gelued", 2)
        hid_ready = sig("hid_ready", 3)
        down = sig("down")

        TURNS = DEPTH * SEQS

        def turns(engine, body):
            body(0, Parts(True, False, False, False))
            body(1, Parts(True, True, True, False))
            with engine.Fori(2, TURNS) as it:
                body(it, Parts(True, True, True, True))
            body(TURNS, Parts(False, True, True, True))
            body(TURNS + 1, Parts(False, False, False, True))

        def slot(turn):
            return bass.ds(turn % SEQS, 1)

        block = ctx.enter_context(nc.Block())

        @block.sync
        def _(sp):
            sp.dma_start(cos_base[:], a["rope_cos"]).then_inc(c_ready.sem, 16)
            sp.dma_start(sin_base[:], a["rope_sin"]).then_inc(c_ready.sem, 16)
            sp.dma_start(mask_f[:], a["window_mask"]).then_inc(c_ready.sem, 16)
            for j, name in enumerate(("L0_ffn_q_scale", "L0_ffn_k_scale")):
                sp.dma_start(qk_rows[:, :, j, :], a[name].unsqueeze(0).to_broadcast([P, DEPTH, AD])).then_inc(c_ready.sem, 16)

            def load(l, loads):
                row = bass.ds(l, 1)
                for dst, src in loads(row):
                    sp.dma_start(dst, src).then_inc(w_ready.sem, 16)

            def attention_weights(row):
                cols = 3 * AI // 3
                return [(wqkv[:, i * cols:(i + 1) * cols].unsqueeze(1),
                         a["L0_ffn_Wqkv"][row, :, i * cols:(i + 1) * cols].rearrange("l p n -> p l n")) for i in range(3)]

            def ffn_weights(row):
                return [(wo[:].unsqueeze(1), a["L0_ffn_Wo"][row].rearrange("l (h p) d -> p l h d", p=P)),
                        (w1[:].unsqueeze(1), a["L0_ffn_W1"][row].rearrange("l p n -> p l n")),
                        (w2[:, 0:2, :].unsqueeze(1), a["L0_ffn_W2"][row, 0:256, :].rearrange("l (h p) d -> p l h d", p=P)),
                        (w2[0:FT[2][1], 2:3, :], a["L0_ffn_W2"][row, 256:FF, :].rearrange("l p d -> p l d")),
                        (vecs[:].unsqueeze(1), a["l_vectors"][row].rearrange("l p n -> p l n"))]

            A_DMA, F_DMA = 3 * 16, 5 * 16

            def layer(l):
                load(l, attention_weights)
                sp.wait_ge(w_ready.sem, l * (A_DMA + F_DMA) + A_DMA)
                sp.sem_inc(att_ok.sem, SEQS)
                sp.wait_ge(x_out.sem, (l + 1) * SEQS)
                load(l, ffn_weights)
                sp.wait_ge(w_ready.sem, (l + 1) * (A_DMA + F_DMA))
                sp.sem_inc(ffn_ok.sem, SEQS)

            layer(0)
            if DEPTH > 1:
                with sp.Fori(1, DEPTH) as l:
                    sp.wait_ge(v_proj.sem, l * SEQS * v_proj.per)
                    layer(l)

        @block.gpsimd
        def _(pool):
            pool.wait_ge(c_ready.sem, 80)

            def make_tables(l):
                row = bass.ds(l, 1)
                for j in range(2):
                    nc.gpsimd.tensor_tensor(cos_t[:, j, :, :], cos_base[:, j, :, :],
                                            qk_rows[:, row, j, :].to_broadcast([P, BLKS, AD]),
                                            ALU.mult).then_inc(tables.sem, 1)
                    for lo, hi in ((slice(0, 32), slice(32, 64)), (slice(32, 64), slice(0, 32))):
                        nc.gpsimd.tensor_tensor(sin_t[:, j, :, lo], sin_base[:, j, :, lo],
                                                qk_rows[:, row, j, hi].to_broadcast([P, BLKS, 32]),
                                                ALU.mult).then_inc(tables.sem, 1)
                pool.wait_ge(tables.sem, tables.upto(l, 6))
                pool.sem_inc(tables_ok.sem, SEQS)

            def rotate(it):
                for u in range(UNITS):
                    m = u // GROUPS
                    wait_for(pool, qn_ready, it, u + 1)
                    wait_for(pool, roped, it, u)
                    for j in range(2):
                        src = qn[:, j, :].rearrange("p (h d) -> p h d", d=AD)
                        dst = t2[:, j, :].rearrange("p (h d) -> p h d", d=AD)
                        for lo, hi in ((slice(0, 32), slice(32, 64)), (slice(32, 64), slice(0, 32))):
                            nc.gpsimd.tensor_tensor(dst[:, :, lo], src[:, :, hi], bcast(sin_t[:, j, m, lo], 1, GH),
                                                    ALU.mult).then_inc(rotated.sem, 1)

            make_tables(0)
            rotate(0)
            if SEQS > 1:
                with pool.Fori(1, SEQS) as it:
                    rotate(it)
            if DEPTH > 1:
                with pool.Fori(1, DEPTH) as l:
                    pool.wait_ge(roped.sem, l * SEQS * roped.per)
                    make_tables(l)
                    settle(pool, settled.sem)
                    with pool.Fori(0, SEQS) as b:
                        rotate(l * SEQS + b)

        @block.vector
        def _(dve):
            def chained(instruction, signal, turn, n):
                instruction.then_inc(signal.sem, 1)
                wait_for(dve, signal, turn, n)

            def refine(tmp, x, guess, out, signal, turn, n):
                chained(nc.vector.tensor_tensor(tmp, guess, guess, ALU.mult), signal, turn, n + 1)
                chained(nc.vector.scalar_tensor_tensor(tmp, x, -0.5, tmp, ALU.mult, ALU.mult), signal, turn, n + 2)
                chained(nc.vector.scalar_tensor_tensor(out, tmp, 1.5, guess, ALU.add, ALU.mult), signal, turn, n + 3)

            nc.vector.memset(xs[:], 0.0)
            nc.vector.memset(xs1[:], 0.0)
            nc.vector.memset(kT[:, :, 0:WIN], 0.0)
            dve.wait_ge(c_ready.sem, 80)
            nc.vector.tensor_copy(mask[:], mask_f[:])
            nc.vector.tensor_copy(ident_b[:], ident[:]).then_inc(consts.sem, 1)
            dve.wait_ge(consts.sem, 1)
            dve.sem_inc(x_out.sem, SEQS)
            nc.vector.tensor_copy(xs[0:64, WIN:].unsqueeze(1), xst[0:64, 0:1, :]).then_inc(xs_ready.sem, 1)

            def body(it, parts):
                def next_stream():
                    wait_for(dve, v_proj, it, v_proj.per)
                    dve.wait_ge(x_out.sem, it + 2)
                    nc.vector.tensor_copy(xs[0:64, WIN:].unsqueeze(1), xst[0:64, slot(it + 1), :]).then_inc(xs_ready.sem, 1)

                def softmax_begin(u):
                    wait_for(dve, scored, it, 2 * u + 2)
                    scores = ps[:].rearrange("p (h k) -> p h k", k=2 * WIN)
                    chained(nc.vector.reduce_max(mx[:], scores, axis=AX_X), max_ready, it, u + 1)
                    wait_for(dve, exped, it, u)
                    nc.vector.tensor_tensor(sim[:].rearrange("p (h k) -> p h k", k=2 * WIN), scores,
                                            bcast(mx[:], 2, 2 * WIN), ALU.subtract).then_inc(sim_ready.sem, 1)

                def softmax_sum(u):
                    wait_for(dve, exped, it, u + 1)
                    chained(nc.vector.reduce_sum(rs[:, u % 2, :], pr[:, u % 2, :].rearrange("p (h k) -> p h k", k=2 * WIN),
                                                 axis=AX_X), sums, it, 2 * u + 1)
                    chained(nc.vector.reciprocal(rinv[:, u % 2, :], rs[:, u % 2, :]), sums, it, 2 * u + 2)

                def norms(u):
                    wait_for(dve, squared, it, u + 1)
                    chained(nc.vector.reduce_sum(ssq[:], sq[:].rearrange("p j (h d) -> p (j h) d", d=AD), axis=AX_X),
                            ssq_ready, it, u + 1)
                    nc.vector.tensor_scalar(n2[:], ssq[:], NORM_MIN2, None, ALU.max).then_inc(n2_ready.sem, 1)

                def rope_begin(u):
                    m = u // GROUPS
                    wait_for(dve, r0_ready, it, u + 1)
                    refine(nt[:], n2[:], r0[:], rr[:], refined, it, 3 * u)
                    chained(nc.vector.tensor_tensor(qn[:].rearrange("p j (h d) -> p (j h) d", d=AD),
                                                    pqk[:].rearrange("p j (h d) -> p (j h) d", d=AD),
                                                    bcast(rr[:], 2, AD), ALU.mult), qn_ready, it, u + 1)
                    wait_for(dve, k_turned, it, u)
                    if u == 0:
                        wait_for(dve, tables_ok, it, 1)
                    nc.vector.tensor_tensor(t1[:].rearrange("p j (h d) -> p j h d", d=AD),
                                            qn[:].rearrange("p j (h d) -> p j h d", d=AD),
                                            bcast(cos_t[:, :, m, :], 2, GH), ALU.mult).then_inc(cosed.sem, 1)

                def rope_end(u):
                    wait_for(dve, cosed, it, u + 1)
                    wait_for(dve, rotated, it, 4 * u + 4)
                    nc.vector.tensor_tensor(t1[:], t1[:], t2[:], ALU.add).then_inc(roped.sem, 1)

                def normalise_out(u):
                    wait_for(dve, weighed, it, 2 * u + 2)
                    wait_for(dve, o_turned, it, u)
                    nc.vector.tensor_tensor(on[:].rearrange("p (h d) -> p h d", d=AD),
                                            po[:].rearrange("p (h d) -> p h d", d=AD),
                                            bcast(rinv[:, u % 2, :], 2, AD), ALU.mult).then_inc(o_normed.sem, 1)

                def residual(j):
                    wait_for(dve, y_ready, j, 1)
                    nc.vector.tensor_tensor(x1[:].unsqueeze(1), pf[:].unsqueeze(1), xst[:, slot(j), :],
                                            ALU.add).then_inc(x1_ready.sem, 1)

                def moments(j):
                    wait_for(dve, x1_turned, j, 1)
                    for i in range(BLKS):
                        chained(nc.vector.bn_stats(stats[:, i, :], pf[:, i * P:(i + 1) * P]), ln_steps, j, 2 * i + 1)
                        settle(dve, settled.sem)
                        chained(nc.vector.bn_aggr(mv[:, i, :], stats[:, i, :]), ln_steps, j, 2 * i + 2)
                    nc.vector.tensor_scalar(fn2[:], mv[:, :, 1], LN_EPS, None, ALU.add).then_inc(fn2_ready.sem, 1)

                def normalise(j):
                    wait_for(dve, fr0_ready, j, 1)
                    refine(fnt[:], fn2[:], fr0[:], frr[:], ln_steps, j, 2 * BLKS)
                    for i in range(BLKS):
                        step = nc.vector.tensor_scalar(xh[:, i, :], pf[:, i * P:(i + 1) * P], mv[:, i, 0:1],
                                                       frr[:, i:i + 1], ALU.subtract, ALU.mult)
                        if i < BLKS - 1:
                            chained(step, ln_steps, j, 2 * BLKS + 3 + i + 1)
                        else:
                            step.then_inc(xh_ready.sem, 1)

                def hidden(j, i):
                    n = FT[i][1]
                    wait_for(dve, gelued, j, 2)
                    wait_for(dve, up, j, 3 + i + 1)
                    nc.vector.scalar_tensor_tensor(hid[0:n, i, :], pf[0:n, :], b1[0:n, i:i + 1],
                                                   gl[0:n, i, :], ALU.add, ALU.mult).then_inc(hid_ready.sem, 1)

                def stream_out(j):
                    wait_for(dve, down, j, 1)
                    wait_for(dve, x1_ready, j, 1)
                    nc.vector.scalar_tensor_tensor(xst[:, slot(j), :], pf[:].unsqueeze(1), b2[:, 0:1], x1[:].unsqueeze(1),
                                                   ALU.add, ALU.add).then_inc(x_out.sem, 1)

                for s in range(UNITS):
                    if parts.has(s - 3):
                        normalise_out(s - 3)
                    if parts.has(s - 2):
                        softmax_sum(s - 2)
                    if parts.has(s):
                        norms(s)
                    if s == 0 and parts.ffn_end:
                        hidden(it - 2, 0)
                    if s == 1 and parts.ffn_end:
                        hidden(it - 2, 2)
                    if parts.has(s):
                        rope_begin(s)
                    if s == 5 and parts.ffn:
                        normalise(it - 1)
                    if s == UNITS - 1 and parts.next:
                        next_stream()
                    if parts.has(s - 1):
                        softmax_begin(s - 1)
                    if parts.has(s):
                        rope_end(s)
                    if s == 0 and parts.ffn_end:
                        hidden(it - 2, 1)
                    if s == 1 and parts.ffn_end:
                        stream_out(it - 2)
                    if s == 3 and parts.ffn:
                        residual(it - 1)
                    if s == 4 and parts.ffn:
                        moments(it - 1)

            turns(dve, body)

        @block.scalar
        def _(act):
            act.wait_ge(consts.sem, 1)
            nc.scalar.copy(xs[64:128, WIN + 1:].unsqueeze(1), xst[64:128, 0:1, 0:T - 1]).then_inc(xs_ready.sem, 1)

            def body(it, parts):
                nc.scalar.preload_act_table_set("natural_log_exp_and_others")

                def keep_square(u):
                    wait_for(act, qk_proj, it, u + 1)
                    nc.scalar.activation(sq[:], pqk[:], ACT.Square).then_inc(squared.sem, 1)

                def keep_q(u):
                    wait_for(act, q_turned, it, u + 1)
                    nc.scalar.copy(qT[:].rearrange("p h t -> p (h t)"), pta[:]).then_inc(q_out.sem, 1)

                def keep_k(u):
                    m, g = divmod(u % UNITS, GROUPS)
                    wait_for(act, k_turned, it, u + 1)
                    nc.scalar.copy(kT[:, g * GHP:(g + 1) * GHP, WIN + m * P:WIN + (m + 1) * P],
                                   ptb[:].rearrange("p (h t) -> p h t", t=P)).then_inc(k_out.sem, 1)

                def guess_norm(u):
                    wait_for(act, n2_ready, it, u + 1)
                    nc.scalar.activation(lnv[:], n2[:], ACT.Ln).then_inc(ln_ready.sem, 1)
                    wait_for(act, ln_ready, it, u + 1)
                    nc.scalar.activation(r0[:], lnv[:], ACT.Exp, scale=-0.5).then_inc(r0_ready.sem, 1)

                def keep_values(w):
                    wait_for(act, v_proj, it, w + 1)
                    nc.scalar.copy(V[:, (w // WPB) % 2, w % WPB, :], pv[:]).then_inc(v_out.sem, 1)

                def keep_p(u):
                    wait_for(act, p_turned, it, u + 1)
                    nc.scalar.copy(prT[:].rearrange("p h t -> p (h t)"), pta[:]).then_inc(p_out.sem, 1)

                def keep_o(u):
                    m, g = divmod(u % UNITS, GROUPS)
                    wait_for(act, o_turned, it, u + 1)
                    nc.scalar.copy(oT[:, g * GHP:(g + 1) * GHP, m * P:(m + 1) * P],
                                   ptb[:].rearrange("p (h t) -> p h t", t=P)).then_inc(o_out.sem, 1)

                def exponentials(u):
                    wait_for(act, sim_ready, it, u + 1)
                    wait_for(act, p_turned, it, u - 1)
                    wait_for(act, sums, it, 2 * (u - 1))
                    nc.scalar.activation(pr[:, u % 2, :], sim[:], ACT.Exp, scale=QK_SCALE).then_inc(exped.sem, 1)

                def next_stream():
                    wait_for(act, v_proj, it, v_proj.per)
                    act.wait_ge(x_out.sem, it + 2)
                    nc.scalar.copy(xs[64:128, WIN + 1:].unsqueeze(1), xst[64:128, slot(it + 1), 0:T - 1]).then_inc(xs_ready.sem, 1)

                def shift(j):
                    wait_for(act, x1_ready, j, 1)
                    nc.scalar.copy(xs1[0:64, :], x1[0:64, :]).then_inc(xs1_ready.sem, 1)
                    nc.scalar.copy(xs1[64:128, 1:T], x1[64:128, 0:T - 1]).then_inc(xs1_ready.sem, 1)

                def guess_std(j):
                    wait_for(act, fn2_ready, j, 1)
                    nc.scalar.activation(flnv[:], fn2[:], ACT.Ln).then_inc(fln_ready.sem, 1)
                    wait_for(act, fln_ready, j, 1)
                    nc.scalar.activation(fr0[:], flnv[:], ACT.Exp, scale=-0.5).then_inc(fr0_ready.sem, 1)

                def keep_normed(j):
                    wait_for(act, xh_turned, j, 1)
                    nc.scalar.activation(xnT[:], pf[:], ACT.Identity, bias=ln_b[:, 0:1], scale=ln_g[:, 0:1]).then_inc(xn_ready.sem, 1)

                def keep_gate(j, i):
                    n = FT[i][1]
                    wait_for(act, up, j, i + 1)
                    nc.scalar.activation(gpre[0:n, i, :], pf[0:n, :], ACT.Identity, bias=b1[0:n, 3 + i:4 + i]).then_inc(g_out.sem, 1)

                def gelu(j):
                    n = FT[2][1]
                    wait_for(act, g_out, j, 3)
                    nc.scalar.activation(gl[:, 0:2, :], gpre[:, 0:2, :], ACT.Gelu).then_inc(gelued.sem, 1)
                    nc.scalar.activation(gl[0:n, 2, :], gpre[0:n, 2, :], ACT.Gelu).then_inc(gelued.sem, 1)

                for s in range(UNITS):
                    if parts.has(s):
                        keep_square(s)
                    if parts.has(s - 1):
                        keep_q(s - 1)
                        keep_k(s - 1)
                    if parts.has(s):
                        guess_norm(s)
                        keep_values(2 * s)
                    if s == 6 and parts.ffn:
                        keep_gate(it - 1, 0)
                    if s == 7 and parts.ffn:
                        keep_gate(it - 1, 2)
                    if parts.has(s - 2):
                        keep_p(s - 2)
                    if parts.has(s):
                        keep_values(2 * s + 1)
                    if parts.has(s - 3):
                        keep_o(s - 3)
                    if s == UNITS - 1 and parts.next:
                        next_stream()
                    if parts.has(s - 1):
                        exponentials(s - 1)
                    if s == 3 and parts.ffn:
                        shift(it - 1)
                    if s == 4 and parts.ffn:
                        guess_std(it - 1)
                    if s == 5 and parts.ffn:
                        keep_normed(it - 1)
                    if s == 6 and parts.ffn:
                        keep_gate(it - 1, 1)
                    if s == 7 and parts.ffn:
                        gelu(it - 1)

            turns(act, body)

        @block.tensor
        def _(pe):
            mm = nc.tensor.matmul
            pe.wait_ge(consts.sem, 1)

            def body(it, parts):
                def project(u):
                    m, g = divmod(u, GROUPS)
                    if u == 0:
                        wait_for(pe, att_ok, it, 1)
                        wait_for(pe, xs_ready, it, 2)
                    wait_for(pe, qn_ready, it, u)
                    for j in range(2):
                        at = j * AI + g * GH * AD
                        last = mm(pqk[:, j, :], xs[:, WIN + m * P:WIN + (m + 1) * P], wqkv[:, at:at + GH * AD],
                                  start=True, stop=True)
                    last.then_inc(qk_proj.sem, 1)

                def turn(bank, src, done):
                    for i in range(GHP):
                        last = nc.tensor.transpose(bank[:, i * P:(i + 1) * P], src[:, i * P:(i + 1) * P], ident[:])
                    last.then_inc(done.sem, 1)

                def turn_q(u):
                    wait_for(pe, roped, it, u + 1)
                    wait_for(pe, p_out, it, u - 1)
                    turn(pta, t1[:, 0, :], q_turned)

                def turn_k(u):
                    wait_for(pe, o_out, it, u - 2)
                    turn(ptb, t1[:, 1, :], k_turned)

                def turn_p(u):
                    wait_for(pe, exped, it, u + 1)
                    if parts.has(u + 1):
                        wait_for(pe, q_out, it, u + 2)
                    else:
                        wait_for(pe, p_out, it, u)
                    turn(pta, pr[:, u % 2, :], p_turned)

                def turn_o(u):
                    wait_for(pe, o_normed, it, u + 1)
                    if parts.has(u + 2):
                        wait_for(pe, k_out, it, u + 3)
                    else:
                        wait_for(pe, o_out, it, u)
                    turn(ptb, on[:], o_turned)

                def values(w):
                    wait_for(pe, v_out, it, w)
                    settle(pe, settled.sem)
                    for e in range(2):
                        cols = wqkv[:, 2 * AI:3 * AI].rearrange("p (h e d) -> p e h d", e=2, d=AD)[:, e, :, :]
                        last = mm(pv[64 * e:64 * e + 64, :], xs[:, WIN * w:WIN * w + 64], cols, start=True, stop=True,
                                  skip_group_check=True)
                    last.then_inc(v_proj.sem, 1)

                def score(u, e):
                    m, g = divmod(u % UNITS, GROUPS)
                    if e == 0:
                        wait_for(pe, q_out, it, u + 1)
                        wait_for(pe, k_out, it, u + 1)
                        wait_for(pe, sim_ready, it, u)
                        mm(ps[:], ident_b[:], mask[:, 0 if m == 0 else 1, :], start=True, stop=False, skip_group_check=True)
                    else:
                        wait_for(pe, scored, it, 2 * u + 1)
                        settle(pe, settled.sem)
                    rows = slice(64 * e, 64 * e + 64)
                    for h in range(e, GH, 2):
                        for w in range(WPB):
                            at = (m * WPB + w) * WIN
                            last = mm(ps[WIN * w:WIN * (w + 1), 2 * WIN * h:2 * WIN * (h + 1)],
                                      qT[rows, h // 2, WIN * w:WIN * (w + 1)],
                                      kT[rows, g * GHP + h // 2, at:at + 2 * WIN],
                                      start=False, stop=(h >= GH - 2), skip_group_check=True)
                    last.then_inc(scored.sem, 1)

                def weigh(u, e):
                    m, g = divmod(u % UNITS, GROUPS)
                    if e == 0:
                        wait_for(pe, p_out, it, u + 1)
                        wait_for(pe, o_normed, it, u)
                        wait_for(pe, v_out, it, WPB * (u // GROUPS + 1))
                    else:
                        wait_for(pe, weighed, it, 2 * u + 1)
                    settle(pe, settled.sem)
                    rows = slice(64 * e, 64 * e + 64)
                    for h in range(e, GH, 2):
                        hp = g * GHP + h // 2
                        for w in range(WPB):
                            last = mm(po[WIN * w:WIN * (w + 1), AD * h:AD * (h + 1)],
                                      prT[rows, h // 2, WIN * w:WIN * (w + 1)],
                                      V[rows, m % 2, w, AD * hp:AD * (hp + 1)],
                                      start=True, stop=True, skip_group_check=True)
                    last.then_inc(weighed.sem, 1)

                def project_out(j):
                    wait_for(pe, ffn_ok, j, 1)
                    wait_for(pe, o_out, j, UNITS)
                    pe.wait_ge(x_out.sem, SEQS + j)
                    for i in range(AHP):
                        last = mm(pf[:], wo[:, i, :], oT[:, i, :], start=(i == 0), stop=(i == AHP - 1))
                    last.then_inc(y_ready.sem, 1)

                def turn_x1(j):
                    wait_for(pe, xs1_ready, j, 2)
                    turn(pf, xs1[:], x1_turned)

                def turn_xh(j):
                    wait_for(pe, xh_ready, j, 1)
                    turn(pf, xh[:].rearrange("p b t -> p (b t)"), xh_turned)

                def gate_up(j, i):
                    if i == 0:
                        wait_for(pe, xn_ready, j, 1)
                    else:
                        wait_for(pe, g_out, j, i)
                    at, n = FT[i]
                    mm(pf[0:n, :], w1[:, FF + at:FF + at + n], xnT[:], start=True, stop=True).then_inc(up.sem, 1)

                def value_up(j, i):
                    if i == 0:
                        wait_for(pe, g_out, j, 3)
                    else:
                        wait_for(pe, hid_ready, j, i)
                    at, n = FT[i]
                    mm(pf[0:n, :], w1[:, at:at + n], xnT[:], start=True, stop=True).then_inc(up.sem, 1)

                def project_down(j):
                    wait_for(pe, hid_ready, j, 3)
                    for i, (_, n) in enumerate(FT):
                        last = mm(pf[:], w2[0:n, i, :], hid[0:n, i, :], start=(i == 0), stop=(i == 2))
                    last.then_inc(down.sem, 1)

                for s in range(UNITS):
                    if parts.has(s):
                        project(s)
                    if parts.has(s - 1):
                        turn_q(s - 1)
                        turn_k(s - 1)
                    if parts.has(s):
                        values(2 * s)
                    if s == 0 and parts.ffn_end:
                        value_up(it - 2, 0)
                    if s == 1 and parts.ffn_end:
                        value_up(it - 2, 2)
                    if s == 3 and parts.ffn:
                        project_out(it - 1)
                    if s == 4 and parts.ffn:
                        turn_x1(it - 1)
                    if s == 6 and parts.ffn:
                        gate_up(it - 1, 0)
                    if s == 7 and parts.ffn:
                        gate_up(it - 1, 2)
                    if parts.has(s - 1):
                        score(s - 1, 0)
                    if parts.has(s - 2):
                        turn_p(s - 2)
                    if parts.has(s):
                        values(2 * s + 1)
                    if parts.has(s - 1):
                        score(s - 1, 1)
                    if parts.has(s - 3):
                        turn_o(s - 3)
                    if parts.has(s - 2):
                        weigh(s - 2, 0)
                    if s == 0 and parts.ffn_end:
                        value_up(it - 2, 1)
                    if s == 1 and parts.ffn_end:
                        project_down(it - 2)
                    if s == 5 and parts.ffn:
                        turn_xh(it - 1)
                    if s == 6 and parts.ffn:
                        gate_up(it - 1, 1)
                    if parts.has(s - 2):
                        weigh(s - 2, 1)

            turns(pe, body)


def combine(nc, a, xst, acc, ident):
    ctx = ExitStack()
    with ctx:
        res = ctx.enter_context(nc.sbuf_tensor("c_res", [P, 2, T], F32))
        tok = ctx.enter_context(nc.sbuf_tensor("c_tok", [P, 2, T], F32))
        banks = [ctx.enter_context(nc.psum_tensor(f"c_p{i}", [P, T], F32)) for i in range(2)]
        added, turned, copied, stored = (ctx.enter_context(nc.semaphore("c_" + n)) for n in ("added", "turned", "copied", "stored"))
        out_d = a["out"].rearrange("s (b p) d -> s p b d", p=P)
        block = ctx.enter_context(nc.Block())

        @block.vector
        def _(dve):
            for b in range(SEQS):
                if b >= 2:
                    dve.wait_ge(turned, b - 1)
                nc.vector.tensor_tensor(res[:, b % 2, :], xst[:, b, :], acc[:, b, :], ALU.add).then_inc(added, 1)

        @block.tensor
        def _(pe):
            for b in range(SEQS):
                pe.wait_ge(added, b + 1)
                if b >= 2:
                    pe.wait_ge(copied, b - 1)
                for i in range(BLKS):
                    last = nc.tensor.transpose(banks[b % 2][:, i * P:(i + 1) * P], res[:, b % 2, i * P:(i + 1) * P], ident[:])
                last.then_inc(turned, 1)

        @block.scalar
        def _(act):
            for b in range(SEQS):
                act.wait_ge(turned, b + 1)
                if b >= 2:
                    act.wait_ge(stored, 16 * (b - 1))
                nc.scalar.copy(tok[:, b % 2, :], banks[b % 2][:]).then_inc(copied, 1)

        @block.sync
        def _(sp):
            for b in range(SEQS):
                sp.wait_ge(copied, b + 1)
                if b:
                    sp.wait_ge(stored, 16 * b)
                sp.dma_start(out_d[b], tok[:, b % 2, :].rearrange("p (b d) -> p b d", d=D)).then_inc(stored, 16)
            sp.wait_ge(stored, 16 * SEQS)


_INS = ["L0_attn_x", "L0_attn_Wq", "L0_attn_Wk", "L0_attn_Wv", "L0_attn_Wa", "L0_attn_Wo",
        "L0_ffn_Wqkv", "L0_ffn_q_scale", "L0_ffn_k_scale", "L0_ffn_Wo", "L0_ffn_W1", "L0_ffn_W2"]


def vectors(inputs):
    import numpy as np
    ba = np.asarray(inputs["L0_attn_ba"]).reshape(RHP, P)
    r = np.stack([*ba, np.asarray(inputs["L0_attn_gamma"]), np.asarray(inputs["L0_attn_beta"])], 1)
    b1 = np.asarray(inputs["L0_ffn_b1"])
    out = np.zeros((DEPTH, P, 9), b1.dtype)
    for part in range(2):
        for j, (at, n) in enumerate(FT):
            out[:, 0:n, 3 * part + j] = b1[:, part * FF + at:part * FF + at + n]
    for j, name in enumerate(("L0_ffn_b2", "L0_ffn_ln_g", "L0_ffn_ln_b")):
        out[:, :, 6 + j] = np.asarray(inputs[name])
    return {"r_vectors": np.ascontiguousarray(r), "l_vectors": out}


def shape_constants():
    import numpy as np
    f = np.float32
    half = np.arange(0, AD, 2, dtype=f)
    inv_freq = (f(1.0) / np.power(f(10000.0), half / f(AD))).astype(f)
    t = np.arange(T, dtype=f)
    freqs = (t[:, None] * inv_freq[None, :]).astype(f)
    freqs = np.concatenate([freqs, freqs], -1)
    base = ((half + f(0.4 * AD)) / f(1.4 * AD)).astype(f)
    power = ((t - T // 2) / f(WIN // 2)).astype(f)
    scale = np.power(base[None, :], power[:, None]).astype(f)
    scale = np.concatenate([scale, scale], -1)
    sign = np.where(np.arange(AD) < AD // 2, f(-1), f(1))
    cos, sin = np.cos(freqs), np.sin(freqs) * sign
    both = lambda x: np.ascontiguousarray(
        np.stack([x * scale, x / scale]).reshape(2, BLKS, P, AD).transpose(2, 0, 1, 3).astype(f))
    i = np.arange(P) % WIN
    key = np.arange(2 * WIN)
    prev = key[None, :] < WIN
    ok = np.where(prev, key[None, :] >= i[:, None], key[None, :] - WIN <= i[:, None])
    first_window = (np.arange(P) < WIN)[:, None] & prev
    m = np.where(ok, f(0), f(MASKED))
    m0 = np.where(first_window, f(MASKED), m)
    window_mask = np.stack([np.tile(m0, (1, GH)), np.tile(m, (1, GH))], 1).astype(f)
    p, j = np.arange(P) % HALF, np.arange(HALF)
    same = np.stack([(p[:, None] >> lv) == (j[None, :] >> lv) for lv in range(LEVELS)], 1)
    own = (np.arange(P)[:, None] // HALF) == np.arange(2)[None, :]
    level = (own[:, None, :, None] & same[:, :, None, :]).reshape(P, LEVELS, P).astype(f)
    return {"ident": np.eye(P, dtype=f), "level_masks": level, "rope_cos": both(cos), "rope_sin": both(sin),
            "window_mask": window_mask}


def kernel(**inputs):
    import numpy as np
    import concourse.bacc as bacc
    from concourse.bass_utils import run_bass_kernel_spmd

    nc = bacc.Bacc("TRN2", target_bir_lowering=False, num_devices=1)
    arrays, aps = {}, {}
    for name in _INS:
        arrays[name + "_dram"] = np.ascontiguousarray(inputs[name])
    for name, table in {**vectors(inputs), **shape_constants()}.items():
        arrays[name + "_dram"] = table
    for key, x in arrays.items():
        aps[key[:-5]] = nc.dram_tensor(key, x.shape, mybir.dt.from_np(x.dtype), kind="ExternalInput").ap()
    aps["out"] = nc.dram_tensor("out_dram", (SEQS, T, D), F32, kind="ExternalOutput").ap()
    build(nc, aps)
    r = run_bass_kernel_spmd(nc, [arrays], core_ids=[0])
    return r.results[0]["out_dram"]
```

```python
import concourse.bass as bass
from concourse import mybir
from contextlib import ExitStack

F32 = mybir.dt.float32
BF16 = mybir.dt.bfloat16
ALU = mybir.AluOpType
ACT = mybir.ActivationFunctionType
AX_X = mybir.AxisListType.X

SEQS, T, D = 8, 512, 128
P = 128
BLKS = T // P
LN_EPS = 1e-5
NORM_MIN2 = 1e-24

RH, RD = 8, 64
RHP = RH // 2
RI = RH * RD
LEVELS = 7
HALF = P // 2

DEPTH, AH, AD, WIN = 6, 16, 64, 32
AI = AH * AD
AHP = AH // 2
GROUPS = 2
GH = AH // GROUPS
GHP = GH // 2
UNITS = BLKS * GROUPS
WPB = P // WIN
PAIRS = T // (2 * WIN)
QK_SCALE = 8.0
FF = int(D * 4 * 2 / 3)
FT = [(0, 128), (128, 128), (256, FF - 256)]
MASKED = -1e30


class Counted:

    def __init__(self, sem, per):
        self.sem, self.per = sem, per

    def upto(self, turn, n):
        return turn * self.per + n


def settle(engine, sem):
    engine.sem_inc(sem, 1)


def wait_for(engine, counted, turn, n):
    if isinstance(turn, int) and counted.upto(turn, n) <= 0:
        return
    engine.wait_ge(counted.sem, counted.upto(turn, n))


class Parts:

    def __init__(self, attention, before, ffn, ffn_end):
        self.attention, self.before, self.ffn, self.ffn_end = attention, before, ffn, ffn_end
        self.next = attention

    def has(self, unit):
        return self.attention if unit >= 0 else self.before


def bcast(ap, axis, n):
    ap = ap.unsqueeze(axis)
    shape = list(ap.shape)
    shape[axis] = n
    return ap.to_broadcast(shape)


def build(nc, a):
    with ExitStack() as ctx:
        def sb(name, shape, dt=F32):
            return ctx.enter_context(nc.sbuf_tensor(name, shape, dt))

        xst = sb("xst", [P, SEQS, T])
        acc = sb("acc", [P, SEQS, T])
        ident = sb("ident", [P, P])
        recurrence(nc, a, xst, acc, ident)
        layers(nc, a, xst, ident)
        combine(nc, a, xst, acc, ident)


def recurrence(nc, a, xst, acc, ident):
    ctx = ExitStack()
    with ctx:
        def sb(name, shape, dt=F32):
            return ctx.enter_context(nc.sbuf_tensor("r_" + name, shape, dt))

        def sig(name, per=1):
            return Counted(ctx.enter_context(nc.semaphore("r_" + name)), per)

        def pair(name, shape):
            return [sb(f"{name}{i}", shape) for i in range(2)]

        SLOTS = LEVELS * RHP
        x_in = sb("x_in", [P, BLKS, D])
        xh = sb("xh", [P, BLKS, D])
        xh2 = sb("xh2", [P, BLKS, D])
        xsum = sb("xsum", [P, BLKS, D])
        stats = sb("stats", [P, BLKS, 6])
        mv = sb("mv", [P, BLKS, 2])
        mv2 = sb("mv2", [P, BLKS, 2])
        var = sb("var", [P, 2, BLKS])
        lnv = sb("lnv", [P, RH])
        r0 = sb("r0", [P, RH])
        tmp = sb("tmp", [P, RH])
        rstd = sb("rstd", [P, RH])
        wq, wk, wv, wa = (sb(n, [P, RI]) for n in ("wq", "wk", "wv", "wa"))
        wo = sb("wo", [P, RHP, D])
        vecs = sb("vecs", [P, RHP + 2])
        ba, gamma, beta = vecs[:, 0:RHP], vecs[:, RHP:RHP + 1], vecs[:, RHP + 1:RHP + 2]
        masks = sb("masks", [P, LEVELS, P])
        zeros = sb("zeros", [P, T], BF16)
        xnT = pair("xnT", [P, T])
        Q = pair("Q", [P, RHP, T + 4])
        K = pair("K", [P, RHP, T])
        Vc = pair("Vc", [P, BLKS, RI])
        decay = [sb(f"decay{i}", [P, RHP, T >> i]) for i in range(LEVELS + 1)]
        ksq = sb("ksq", [P, RI])
        kn2 = sb("kn2", [P, RH])
        ktok = sb("ktok", [P, RI])
        xleft = sb("xleft", [P, 2, 2, P])
        Kl = sb("Kl", [P, 2, BLKS * HALF])
        Vl = sb("Vl", [P, 2, 2, RI])
        PM = sb("PM", [P, 2, 2, 2, P])
        Kd = sb("Kd", [P, 2, BLKS, P])
        S = sb("S", [P, RHP, BLKS + 1, RD])
        oT = sb("oT", [P, RHP, T + 4])

        pb = [ctx.enter_context(nc.psum_tensor(f"r_p{i}", [P, T], F32)) for i in range(6)]
        po, pv, pm = pb[0:4], pb[4], pb[5]
        pscores = ctx.enter_context(nc.psum_tensor("r_pscores", [P, 2, T], F32))
        psc = [pscores[:, 0, :], pscores[:, 1, :]]

        loaded = sig("loaded", 0)
        x_loaded = sig("x_loaded", 16)
        x_used = sig("x_used")
        front_steps = sig("front_steps", 2 * (3 * BLKS + 2) + 4 * BLKS)
        var_ready = sig("var_ready", 2 + BLKS)
        ln_ready = sig("ln_ready", 2 + BLKS)
        r0_ready = sig("r0_ready", 2 + BLKS)
        normed = sig("normed", 3)
        turned = sig("turned", 3)
        turned_out = sig("turned_out", 3)
        proj = sig("proj", 2 * RHP)
        proj_out = sig("proj_out", 2 * RHP)
        kproj = sig("kproj", BLKS)
        ksquares = sig("ksquares", BLKS)
        knormed = sig("knormed", BLKS)
        kturned = sig("kturned", BLKS)
        k_out = sig("k_out", BLKS)
        vproj = sig("vproj", BLKS)
        v_out = sig("v_out", BLKS)
        lefts = sig("lefts", LEVELS)
        vl_proj = sig("vl_proj", 2 * LEVELS)
        vl_out = sig("vl_out", 2 * LEVELS)
        packed = sig("packed", SLOTS)
        scored = sig("scored", 2 * SLOTS)
        masked = sig("masked", 2 * SLOTS)
        decaying = sig("decaying", 2 * SLOTS)
        decayed = sig("decayed", SLOTS)
        summed = sig("summed", SLOTS)
        kd_turned = sig("kd_turned", RHP)
        kd_out = sig("kd_out", RHP)
        ds_ready = sig("ds_ready", RHP)
        state_steps = sig("state_steps", RHP * (BLKS - 1))
        state_ready = sig("state_ready", RHP)
        o_ready = sig("o_ready", RHP)
        o_out = sig("o_out", RHP + 1)
        y_ready = sig("y_ready")
        y_added = sig("y_added")
        set_up = sig("set_up", 0)
        settled = sig("settled", 0)

        LOADED = 8 * 16
        TURN_AT = {4: 0, 5: 1, 6: 2}
        KPROJ_AT = {7 + 3 * i: i for i in range(BLKS)}
        KNORM_AT = {8 + 3 * i: i for i in range(BLKS)}
        KTURN_AT = {9 + 3 * i: i for i in range(BLKS)}
        Q_AT = {19 + i: i for i in range(RHP)}
        LAST_AT = {SLOTS - BLKS + i: i for i in range(BLKS)}

        xin_d = a["L0_attn_x"].rearrange("s (b p) d -> s p b d", p=P)

        def sequences(engine, front, level, end):
            def one(b, parity, more):
                for k in range(SLOTS):
                    level(b, parity, k)
                    if more:
                        front(b + 1, 1 - parity, k)
                end(b, parity, more)

            for k in range(SLOTS):
                front(0, 0, k)
            one(0, 0, True)
            with engine.Fori(0, SEQS // 2 - 1) as i:
                one(i * 2 + 1, 1, True)
                one(i * 2 + 2, 0, True)
            one(SEQS - 1, 1, False)

        def halves(ap, h, side):
            return ap.rearrange("p (m s r) -> p m s r", s=2, r=h)[:, :, side, :]

        block = ctx.enter_context(nc.Block())

        @block.sync
        def _(sp):
            loads = [(wq, a["L0_attn_Wq"]), (wk, a["L0_attn_Wk"]), (wv, a["L0_attn_Wv"]),
                     (wa, a["L0_attn_Wa"]), (ident, a["ident"]), (masks, a["level_masks"]), (vecs, a["r_vectors"]),
                     (wo, a["L0_attn_Wo"].rearrange("(h p) d -> p h d", p=P))]
            assert LOADED == 16 * len(loads)
            for dst, src in loads:
                sp.dma_start(dst[:], src).then_inc(loaded.sem, 16)
            with sp.Fori(0, SEQS) as b:
                sp.wait_ge(x_used.sem, x_used.upto(b, 1))
                sp.dma_start(x_in[:], xin_d[b]).then_inc(x_loaded.sem, 16)

        @block.vector
        def _(dve):
            for q in Q:
                nc.vector.memset(q[:], 0.0)
            nc.vector.memset(zeros[:], 0.0)
            nc.vector.memset(S[:], 0.0).then_inc(set_up.sem, 1)
            dve.wait_ge(set_up.sem, 1)
            dve.sem_inc(x_used.sem, 1)
            dve.wait_ge(loaded.sem, LOADED)

            def chained(instruction, counted, turn, n):
                instruction.then_inc(counted.sem, 1)
                wait_for(dve, counted, turn, n)

            def refine(b, n, width, x, out):
                t, g = tmp[:, 0:width], r0[:, 0:width]
                chained(nc.vector.tensor_tensor(t, g, g, ALU.mult), front_steps, b, n + 1)
                chained(nc.vector.scalar_tensor_tensor(t, x, -0.5, t, ALU.mult, ALU.mult), front_steps, b, n + 2)
                chained(nc.vector.scalar_tensor_tensor(out, t, 1.5, g, ALU.add, ALU.mult), front_steps, b, n + 3)

            NORM_STEPS = 3 * BLKS + 2

            def moments(b, src, mv_, which):
                for i in range(BLKS):
                    chained(nc.vector.bn_stats(stats[:, i, :], src[:, i, :]), front_steps, b, which * NORM_STEPS + 2 * i + 1)
                    settle(dve, settled.sem)
                    chained(nc.vector.bn_aggr(mv_[:, i, :], stats[:, i, :]), front_steps, b, which * NORM_STEPS + 2 * i + 2)
                nc.vector.tensor_scalar(var[:, which, :], mv_[:, :, 1], LN_EPS, None, ALU.add).then_inc(var_ready.sem, 1)

            def normalise(b, src, mv_, out, which):
                dve.wait_ge(r0_ready.sem, r0_ready.upto(b, which + 1))
                at = which * NORM_STEPS + 2 * BLKS
                refine(b, at, BLKS, var[:, which, :], rstd[:, 0:BLKS])
                for i in range(BLKS):
                    step = nc.vector.tensor_scalar(out[:, i, :], src[:, i, :], mv_[:, i, 0:1], rstd[:, i:i + 1],
                                                   ALU.subtract, ALU.mult)
                    if i < BLKS - 1:
                        chained(step, front_steps, b, at + 3 + i + 1)
                    else:
                        step.then_inc(normed.sem, 1)

            def front(b, parity, k):
                if k == 0:
                    dve.wait_ge(x_loaded.sem, x_loaded.upto(b, 16))
                    wait_for(dve, turned, b, 0)
                    moments(b, x_in, mv, 0)
                if k == 1:
                    normalise(b, x_in, mv, xh, 0)
                if k == 2:
                    dve.wait_ge(normed.sem, normed.upto(b, 1))
                    moments(b, xh, mv2, 1)
                if k == 3:
                    normalise(b, xh, mv2, xh2, 1)
                    nc.vector.tensor_tensor(xsum[:], x_in[:], xh[:], ALU.add).then_inc(normed.sem, 1)
                    dve.wait_ge(normed.sem, normed.upto(b, 3))
                    dve.sem_inc(x_used.sem, 1)
                if k in KPROJ_AT:
                    i = KPROJ_AT[k]
                    dve.wait_ge(ksquares.sem, ksquares.upto(b, i + 1))
                    chained(nc.vector.reduce_sum(tmp[:], ksq[:].rearrange("p (h d) -> p h d", d=RD), axis=AX_X),
                            front_steps, b, 2 * NORM_STEPS + 4 * i + 1)
                    nc.vector.tensor_scalar(kn2[:], tmp[:], NORM_MIN2, None, ALU.max).then_inc(var_ready.sem, 1)
                if k in KNORM_AT:
                    i = KNORM_AT[k]
                    dve.wait_ge(r0_ready.sem, r0_ready.upto(b, 3 + i))
                    refine(b, 2 * NORM_STEPS + 4 * i + 1, RH, kn2[:], rstd[:])
                    wait_for(dve, kturned, b, i)
                    nc.vector.tensor_tensor(ktok[:].rearrange("p (h d) -> p h d", d=RD),
                                            pm[:].rearrange("p (h d) -> p h d", d=RD),
                                            bcast(rstd[:], 2, RD), ALU.mult).then_inc(knormed.sem, 1)

            def level(b, parity, k):
                lv, hp = divmod(k, RHP)
                h = 1 << lv
                if k == 0:
                    dve.wait_ge(proj_out.sem, proj_out.upto(b, 2 * RHP))
                    dve.wait_ge(k_out.sem, k_out.upto(b, BLKS))
                wait_for(dve, summed, b, k - 1)
                for e in range(2):
                    dve.wait_ge(scored.sem, scored.upto(b, 2 * k + e + 1))
                    products = pscores[:, e, 0:P].rearrange("p (c t) -> p c t", t=HALF)
                    mask = masks[:, lv, :].rearrange("p (a t) -> p a t", a=2)
                    nc.vector.tensor_tensor(PM[:, k % 2, e, :, :].rearrange("p c (a t) -> p c a t", a=2),
                                            bcast(products, 2, 2), bcast(mask, 1, 2), ALU.mult).then_inc(masked.sem, 1)
                if lv:
                    dve.wait_ge(decayed.sem, decayed.upto(b, k - RHP + 1))
                dve.wait_ge(packed.sem, packed.upto(b, k + 1))
                q_right, k_left = halves(Q[parity][:, hp, 0:T], h, 1), halves(K[parity][:, hp, :], h, 0)
                dc = decay[lv][:, hp, :].rearrange("p (m s) -> p m s", s=2)
                nc.vector.tensor_tensor(q_right, q_right, bcast(dc[:, :, 0], 2, h), ALU.mult).then_inc(decaying.sem, 1)
                nc.vector.tensor_tensor(k_left, k_left, bcast(dc[:, :, 1], 2, h), ALU.mult).then_inc(decaying.sem, 1)
                dve.wait_ge(decaying.sem, decaying.upto(b, 2 * k + 2))
                nc.vector.tensor_tensor(decay[lv + 1][:, hp, :], dc[:, :, 0], dc[:, :, 1], ALU.mult).then_inc(decayed.sem, 1)
                if k == 0 and not (isinstance(b, int) and b == 0):
                    add_result(b - 1)

            def add_result(b):
                dve.wait_ge(y_ready.sem, y_ready.upto(b, 1))
                dve.wait_ge(turned_out.sem, turned_out.upto(b, 3))
                nc.vector.tensor_tensor(acc[:, bass.ds(b, 1), :], acc[:, bass.ds(b, 1), :],
                                        po[3][:].unsqueeze(1), ALU.add).then_inc(y_added.sem, 1)

            def end(b, parity, more):
                dve.wait_ge(decayed.sem, decayed.upto(b, SLOTS))
                for hp in range(RHP):
                    dve.wait_ge(ds_ready.sem, ds_ready.upto(b, hp + 1))
                    for c in range(BLKS):
                        step = nc.vector.scalar_tensor_tensor(
                            S[:, hp, c + 1, :], S[:, hp, c, :], decay[LEVELS][:, hp, c:c + 1],
                            psc[hp % 2][:, c * RD:(c + 1) * RD], ALU.mult, ALU.add)
                        if c < BLKS - 1:
                            chained(step, state_steps, b, hp * (BLKS - 1) + c + 1)
                        else:
                            step.then_inc(state_ready.sem, 1)
                if not more:
                    add_result(b)

            sequences(dve, front, level, end)

        @block.scalar
        def _(act):
            act.wait_ge(loaded.sem, LOADED)

            def rsqrt_guess(b, which, src, width):
                act.wait_ge(var_ready.sem, var_ready.upto(b, which + 1))
                nc.scalar.activation(lnv[:, 0:width], src, ACT.Ln).then_inc(ln_ready.sem, 1)
                act.wait_ge(ln_ready.sem, ln_ready.upto(b, which + 1))
                nc.scalar.activation(r0[:, 0:width], lnv[:, 0:width], ACT.Exp, scale=-0.5).then_inc(r0_ready.sem, 1)

            def front(b, parity, k):
                one = bass.ds(b, 1)
                if k == 0:
                    nc.scalar.preload_act_table_set("natural_log_exp_and_others")
                    rsqrt_guess(b, 0, var[:, 0, :], BLKS)
                if k == 2:
                    rsqrt_guess(b, 1, var[:, 1, :], BLKS)
                if k in TURN_AT:
                    which = TURN_AT[k]
                    act.wait_ge(turned.sem, turned.upto(b, which + 1))
                    if which == 0:
                        nc.scalar.copy(xst[:, one, :], pm[:].unsqueeze(1)).then_inc(turned_out.sem, 1)
                    elif which == 1:
                        nc.scalar.activation(xnT[parity][:], pm[:], ACT.Identity, bias=beta,
                                             scale=gamma).then_inc(turned_out.sem, 1)
                    else:
                        nc.scalar.copy(acc[:, one, :], pm[:].unsqueeze(1)).then_inc(turned_out.sem, 1)
                if k in KPROJ_AT:
                    i = KPROJ_AT[k]
                    act.wait_ge(kproj.sem, kproj.upto(b, i + 1))
                    nc.scalar.activation(ksq[:], pm[:], ACT.Square).then_inc(ksquares.sem, 1)
                if k in KNORM_AT:
                    rsqrt_guess(b, 2 + KNORM_AT[k], kn2[:], RH)
                if k in KTURN_AT:
                    i = KTURN_AT[k]
                    act.wait_ge(kturned.sem, kturned.upto(b, i + 1))
                    nc.scalar.copy(K[parity][:, :, i * P:(i + 1) * P],
                                   pm[:].rearrange("p (h t) -> p h t", t=P)).then_inc(k_out.sem, 1)
                if k in Q_AT:
                    hp = Q_AT[k]
                    act.wait_ge(proj.sem, proj.upto(b, hp + 1))
                    nc.scalar.copy(Q[parity][:, hp, 1:T + 1], pm[:]).then_inc(proj_out.sem, 1)
                if k in LAST_AT:
                    i = LAST_AT[k]
                    act.wait_ge(vproj.sem, vproj.upto(b, i + 1))
                    nc.scalar.copy(Vc[parity][:, i, :], pv[:]).then_inc(v_out.sem, 1)
                    act.wait_ge(proj.sem, proj.upto(b, RHP + i + 1))
                    nc.scalar.activation(decay[0][:, i, :], pm[:], ACT.Sigmoid, bias=ba[:, i:i + 1]).then_inc(proj_out.sem, 1)

            def keep_left_values(b, lv, cp):
                act.wait_ge(vl_proj.sem, vl_proj.upto(b, 2 * lv + cp + 1))
                if lv >= 2:
                    act.wait_ge(summed.sem, summed.upto(b, (lv - 1) * RHP))
                nc.scalar.copy(Vl[:, lv % 2, cp, :], pv[:]).then_inc(vl_out.sem, 1)

            def pack(b, parity, k):
                lv, hp = divmod(k, RHP)
                h = 1 << lv
                if lv:
                    act.wait_ge(decayed.sem, decayed.upto(b, k - RHP + 1))
                wait_for(act, scored, b, 2 * (k - 1))
                nc.scalar.copy(Kl[:, k % 2, :].rearrange("p (m r) -> p m r", r=h),
                               halves(K[parity][:, hp, :], h, 0)).then_inc(packed.sem, 1)

            def level(b, parity, k):
                lv, hp = divmod(k, RHP)
                if k == 0:
                    act.wait_ge(k_out.sem, k_out.upto(b, BLKS))
                    pack(b, parity, 0)
                if k + 1 < SLOTS:
                    pack(b, parity, k + 1)
                if hp in (1, 2) and lv + 1 < LEVELS:
                    keep_left_values(b, lv + 1, hp - 1)
                if k == 0:
                    keep_left_values(b, 0, 0)
                    keep_left_values(b, 0, 1)

            def end(b, parity, more):
                for hp in range(RHP):
                    act.wait_ge(kd_turned.sem, kd_turned.upto(b, hp + 1))
                    wait_for(act, ds_ready, b, hp - 1)
                    nc.scalar.copy(Kd[:, hp % 2, :, :].rearrange("p c k -> p (c k)"),
                                   (pv if hp % 2 == 0 else pm)[:]).then_inc(kd_out.sem, 1)
                for hp in range(RHP):
                    act.wait_ge(o_ready.sem, o_ready.upto(b, hp + 1))
                    nc.scalar.copy(oT[:, hp, 0:T], po[hp][:]).then_inc(o_out.sem, 1)
                nc.scalar.copy(oT[:, :, T:T + 1], pm[:, 0:RHP].unsqueeze(2)).then_inc(o_out.sem, 1)

            sequences(act, front, level, end)

        @block.gpsimd
        def _(pool):
            def nothing(b, parity, k):
                pass

            def level(b, parity, k):
                lv, hp = divmod(k, RHP)
                if hp:
                    return
                if lv == 0:
                    pool.wait_ge(turned_out.sem, turned_out.upto(b, 2))
                wait_for(pool, vl_proj, b, 2 * max(lv - 1, 0))
                settle(pool, settled.sem)
                nc.gpsimd.tensor_copy(xleft[:, lv % 2, :, :].rearrange("p c (m r) -> p (c m) r", r=1 << lv),
                                      halves(xnT[parity][:], 1 << lv, 0)).then_inc(lefts.sem, 1)

            sequences(pool, nothing, level, lambda b, parity, more: None)

        @block.tensor
        def _(pe):
            pe.wait_ge(loaded.sem, LOADED)
            pe.wait_ge(set_up.sem, 1)
            mm = nc.tensor.matmul

            def front(b, parity, k):
                x = xnT[parity]
                if k in TURN_AT:
                    which = TURN_AT[k]
                    pe.wait_ge(normed.sem, normed.upto(b, which + 1))
                    if which:
                        pe.wait_ge(turned_out.sem, turned_out.upto(b, which))
                    for i in range(BLKS):
                        last = nc.tensor.transpose(pm[:, i * P:(i + 1) * P], (xh, xh2, xsum)[which][:, i, :], ident[:])
                    last.then_inc(turned.sem, 1)
                if k in KPROJ_AT:
                    i = KPROJ_AT[k]
                    if i:
                        pe.wait_ge(k_out.sem, k_out.upto(b, i))
                    else:
                        pe.wait_ge(turned_out.sem, turned_out.upto(b, 3))
                    mm(pm[:], x[:, i * P:(i + 1) * P], wk[:], start=True, stop=True).then_inc(kproj.sem, 1)
                if k in KTURN_AT:
                    i = KTURN_AT[k]
                    pe.wait_ge(knormed.sem, knormed.upto(b, i + 1))
                    for hp in range(RHP):
                        last = nc.tensor.transpose(pm[:, hp * P:(hp + 1) * P], ktok[:, hp * P:(hp + 1) * P], ident[:])
                    last.then_inc(kturned.sem, 1)
                if k in Q_AT:
                    hp = Q_AT[k]
                    if hp:
                        pe.wait_ge(proj_out.sem, proj_out.upto(b, hp))
                    else:
                        pe.wait_ge(k_out.sem, k_out.upto(b, BLKS))
                    mm(pm[:], wq[:, hp * P:(hp + 1) * P], x[:], start=True, stop=True).then_inc(proj.sem, 1)
                if k in LAST_AT:
                    i = LAST_AT[k]
                    if i:
                        pe.wait_ge(v_out.sem, v_out.upto(b, i))
                    else:
                        wait_for(pe, vl_out, b, 0)
                    mm(pv[:], x[:, i * P:(i + 1) * P], wv[:], start=True, stop=True).then_inc(vproj.sem, 1)
                    pe.wait_ge(proj_out.sem, proj_out.upto(b, RHP + i))
                    mm(pm[:], wa[:, i * P:(i + 1) * P], x[:], start=True, stop=True).then_inc(proj.sem, 1)

            def left_values(b, lv, cp):
                if cp == 0:
                    pe.wait_ge(lefts.sem, lefts.upto(b, lv + 1))
                wait_for(pe, vl_out, b, 2 * lv + cp)
                mm(pv[:], xleft[:, lv % 2, cp, :], wv[:], start=True, stop=True).then_inc(vl_proj.sem, 1)

            def gather(b, k):
                lv, hp = divmod(k, RHP)
                h = 1 << lv
                if lv == 0:
                    wait_for(pe, o_out, b, 0)
                    if hp == 3:
                        wait_for(pe, y_added, b, 0)
                    mm(po[hp][:], zeros[:, 0:P], zeros[:], start=True, stop=False, skip_group_check=True)
                pe.wait_ge(masked.sem, masked.upto(b, 2 * (k + 1)))
                pe.wait_ge(vl_out.sem, vl_out.upto(b, 2 * (lv + 1)))
                settle(pe, settled.sem)
                for cp in range(2):
                    for e in range(2):
                        out = halves(po[hp][RD * e:RD * e + RD, 2 * P * cp:2 * P * (cp + 1)], h, 1)
                        head = 2 * hp + e
                        last = mm(out, Vl[:, lv % 2, cp, head * RD:(head + 1) * RD],
                                  PM[:, k % 2, e, cp, :].rearrange("p (m r) -> p m r", r=h),
                                  start=False, stop=False, skip_group_check=True)
                last.then_inc(summed.sem, 1)

            def level(b, parity, k):
                lv, hp = divmod(k, RHP)
                h = 1 << lv
                if k == 0:
                    pe.wait_ge(v_out.sem, v_out.upto(b, BLKS))
                    left_values(b, 0, 0)
                    pe.wait_ge(proj_out.sem, proj_out.upto(b, 2 * RHP))
                    wait_for(pe, state_ready, b, 0)
                if hp in (1, 2) and lv + 1 < LEVELS:
                    left_values(b, lv + 1, hp - 1)
                pe.wait_ge(packed.sem, packed.upto(b, k + 1))
                if lv:
                    pe.wait_ge(decayed.sem, decayed.upto(b, k - RHP + 1))
                for e in range(2):
                    wait_for(pe, masked, b, 2 * (k - 1) + e + 1)
                    settle(pe, settled.sem)
                    rows = slice(RD * e, RD * e + RD)
                    for c in range(BLKS):
                        left = Kl[rows, k % 2, HALF * c:HALF * (c + 1)]
                        right = halves(Q[parity][rows, hp, P * c:P * (c + 1)], h, 1)
                        col, at = HALF * (c // 2), HALF * (c % 2)
                        last = mm(pscores[at:at + HALF, e, col:col + HALF], left, right, start=True, stop=True,
                                  skip_group_check=True)
                    last.then_inc(scored.sem, 1)
                if k == 0:
                    left_values(b, 0, 1)
                else:
                    gather(b, k - 1)

            def turn_keys(b, parity, hp):
                bank = pv if hp % 2 == 0 else pm
                if hp >= 2:
                    pe.wait_ge(kd_out.sem, kd_out.upto(b, hp - 1))
                for c in range(BLKS):
                    last = nc.tensor.transpose(bank[:, P * c:P * (c + 1)], K[parity][:, hp, P * c:P * (c + 1)], ident[:])
                last.then_inc(kd_turned.sem, 1)

            def end(b, parity, more):
                gather(b, SLOTS - 1)
                pe.wait_ge(decayed.sem, decayed.upto(b, SLOTS))
                pe.wait_ge(vl_out.sem, vl_out.upto(b, 2 * LEVELS))
                pe.wait_ge(v_out.sem, v_out.upto(b + 1 if more else b, BLKS))
                pe.wait_ge(proj_out.sem, proj_out.upto(b + 1 if more else b, 2 * RHP))
                turn_keys(b, parity, 0)
                turn_keys(b, parity, 1)
                for hp in range(RHP):
                    pe.wait_ge(kd_out.sem, kd_out.upto(b, hp + 1))
                    pe.wait_ge(v_out.sem, v_out.upto(b, BLKS))
                    if hp >= 2:
                        pe.wait_ge(state_ready.sem, state_ready.upto(b, hp - 1))
                    settle(pe, settled.sem)
                    for c in range(BLKS):
                        for e in range(2):
                            head = 2 * hp + e
                            last = mm(psc[hp % 2][RD * e:RD * e + RD, RD * c:RD * (c + 1)],
                                      Kd[:, hp % 2, c, RD * e:RD * e + RD],
                                      Vc[parity][:, c, head * RD:(head + 1) * RD], start=True, stop=True,
                                      skip_group_check=True)
                    last.then_inc(ds_ready.sem, 1)
                    if hp + 2 < RHP:
                        turn_keys(b, parity, hp + 2)
                pe.wait_ge(kd_out.sem, kd_out.upto(b, RHP))
                for hp in range(RHP):
                    pe.wait_ge(state_ready.sem, state_ready.upto(b, hp + 1))
                    settle(pe, settled.sem)
                    for e in range(2):
                        rows = slice(RD * e, RD * e + RD)
                        for c in range(1, BLKS):
                            mm(po[hp][rows, P * c:P * (c + 1)], S[rows, hp, c, :], Q[parity][rows, hp, P * c:P * (c + 1)],
                               start=False, stop=(c == BLKS - 1), skip_group_check=True)
                        last = mm(pm[rows, hp:hp + 1], S[rows, hp, BLKS, :], Q[parity][rows, hp, T:T + 1],
                                  start=True, stop=True, skip_group_check=True)
                    last.then_inc(o_ready.sem, 1)
                pe.wait_ge(o_out.sem, o_out.upto(b, RHP + 1))
                for hp in range(RHP):
                    last = mm(po[3][:], wo[:, hp, :], oT[:, hp, 1:T + 1], start=(hp == 0), stop=(hp == RHP - 1))
                last.then_inc(y_ready.sem, 1)

            sequences(pe, front, level, end)


def layers(nc, a, xst, ident):
    ctx = ExitStack()
    with ctx:
        def sb(name, shape, dt=F32):
            return ctx.enter_context(nc.sbuf_tensor("l_" + name, shape, dt))

        def sig(name, per=1):
            return Counted(ctx.enter_context(nc.semaphore("l_" + name)), per)

        wqkv = sb("wqkv", [P, 3 * AI])
        wo = sb("wo", [P, AHP, D])
        w1 = sb("w1", [P, 2 * FF])
        w2 = sb("w2", [P, 3, D])
        vecs = sb("vecs", [P, 9])
        b1, b2, ln_g, ln_b = vecs[:, 0:6], vecs[:, 6:7], vecs[:, 7:8], vecs[:, 8:9]
        qk_rows = sb("qk_rows", [P, DEPTH, 2, AD])
        cos_base = sb("cos_base", [P, 2, BLKS, AD])
        sin_base = sb("sin_base", [P, 2, BLKS, AD])
        cos_t = sb("cos_t", [P, 2, BLKS, AD])
        sin_t = sb("sin_t", [P, 2, BLKS, AD])
        mask_f = sb("mask_f", [P, 2, GH * 2 * WIN])
        mask = sb("mask", [P, 2, GH * 2 * WIN], BF16)
        ident_b = sb("ident_b", [P, P], BF16)
        xs = sb("xs", [P, WIN + T])
        sq = sb("sq", [P, 2, GH * AD])
        ssq, n2, lnv, r0, rr, nt = (sb(n, [P, 2 * GH]) for n in ("ssq", "n2", "lnv", "r0", "rr", "nt"))
        qn = sb("qn", [P, 2, GH * AD])
        t1 = sb("t1", [P, 2, GH * AD])
        t2 = sb("t2", [P, 2, GH * AD])
        qT = sb("qT", [P, GHP, P])
        kT = sb("kT", [P, AHP, 2, PAIRS + 1, WIN])
        V = sb("V", [P, 2, WPB, AHP * AD])
        mx, rs, rinv = sb("mx", [P, GH]), sb("rs", [P, 2, GH]), sb("rinv", [P, 2, GH])
        sim = sb("sim", [P, GH * 2 * WIN])
        pr = sb("pr", [P, 2, GH * 2 * WIN])
        prT = sb("prT", [P, GHP, P])
        on = sb("on", [P, GH * AD])
        oT = sb("oT", [P, AHP, T])
        x1 = sb("x1", [P, T])
        xs1 = sb("xs1", [P, T])
        stats = sb("stats", [P, BLKS, 6])
        mv = sb("mv", [P, BLKS, 2])
        fn2, flnv, fr0, frr, fnt = (sb(n, [P, BLKS]) for n in ("fn2", "flnv", "fr0", "frr", "fnt"))
        xh = sb("xh", [P, BLKS, P])
        xnT = sb("xnT", [P, T])
        gpre = sb("gpre", [P, 3, T])
        gl = sb("gl", [P, 3, T])
        hid = sb("hid", [P, 3, T])

        pqk = ctx.enter_context(nc.psum_tensor("l_pqk", [P, 2, T], F32))
        pta, ptb, ps, po, pv, pf = (ctx.enter_context(nc.psum_tensor(f"l_p{i}", [P, T], F32)) for i in range(6))

        c_ready = sig("c_ready", 0)
        w_ready = sig("w_ready", 0)
        consts = sig("consts", 0)
        settled = sig("settled", 0)
        att_ok = sig("att_ok")
        ffn_ok = sig("ffn_ok")
        tables = sig("tables", 6)
        tables_ok = sig("tables_ok")
        x_out = sig("x_out")
        xs_ready = sig("xs_ready", 2)
        qk_proj = sig("qk_proj", UNITS)
        squared = sig("squared", UNITS)
        ssq_ready = sig("ssq_ready", UNITS)
        n2_ready = sig("n2_ready", UNITS)
        ln_ready = sig("ln_ready", UNITS)
        r0_ready = sig("r0_ready", UNITS)
        refined = sig("refined", 3 * UNITS)
        qn_ready = sig("qn_ready", UNITS)
        cosed = sig("cosed", UNITS)
        rotated = sig("rotated", 4 * UNITS)
        q_roped, k_roped = sig("q_roped", UNITS), sig("k_roped", UNITS)
        q_turned, k_turned = sig("q_turned", UNITS), sig("k_turned", UNITS)
        q_out, k_out = sig("q_out", UNITS), sig("k_out", UNITS)
        v_proj = sig("v_proj", PAIRS)
        v_out = sig("v_out", 2 * PAIRS)
        v_mixed = sig("v_mixed", 2 * (PAIRS - 1))
        scored = sig("scored", 2 * UNITS)
        max_ready = sig("max_ready", UNITS)
        sim_ready = sig("sim_ready", UNITS)
        exped = sig("exped", UNITS)
        sums = sig("sums", 2 * UNITS)
        p_turned = sig("p_turned", UNITS)
        p_out = sig("p_out", UNITS)
        weighed = sig("weighed", 2 * UNITS)
        o_normed = sig("o_normed", UNITS)
        o_turned = sig("o_turned", UNITS)
        o_out = sig("o_out", UNITS)
        y_ready = sig("y_ready")
        x1_ready = sig("x1_ready")
        xs1_ready = sig("xs1_ready", 2)
        x1_turned = sig("x1_turned")
        ln_steps = sig("ln_steps", 2 * BLKS + 3 + BLKS - 1)
        fn2_ready, fln_ready, fr0_ready = sig("fn2_ready"), sig("fln_ready"), sig("fr0_ready")
        xh_ready = sig("xh_ready")
        xh_turned = sig("xh_turned")
        xn_ready = sig("xn_ready")
        up = sig("up", 6)
        g_out = sig("g_out", 3)
        gelued = sig("gelued", 2)
        hid_ready = sig("hid_ready", 3)
        down = sig("down")

        TURNS = DEPTH * SEQS

        def turns(engine, body):
            body(0, Parts(True, False, False, False))
            body(1, Parts(True, True, True, False))
            with engine.Fori(2, TURNS) as it:
                body(it, Parts(True, True, True, True))
            body(TURNS, Parts(False, True, True, True))
            body(TURNS + 1, Parts(False, False, False, True))

        def slot(turn):
            return bass.ds(turn % SEQS, 1)

        block = ctx.enter_context(nc.Block())

        @block.sync
        def _(sp):
            sp.dma_start(cos_base[:], a["rope_cos"]).then_inc(c_ready.sem, 16)
            sp.dma_start(sin_base[:], a["rope_sin"]).then_inc(c_ready.sem, 16)
            sp.dma_start(mask_f[:], a["window_mask"]).then_inc(c_ready.sem, 16)
            for j, name in enumerate(("L0_ffn_q_scale", "L0_ffn_k_scale")):
                sp.dma_start(qk_rows[:, :, j, :], a[name].unsqueeze(0).to_broadcast([P, DEPTH, AD])).then_inc(c_ready.sem, 16)

            def load(l, loads):
                row = bass.ds(l, 1)
                for dst, src in loads(row):
                    sp.dma_start(dst, src).then_inc(w_ready.sem, 16)

            def attention_weights(row):
                cols = 3 * AI // 3
                return [(wqkv[:, i * cols:(i + 1) * cols].unsqueeze(1),
                         a["L0_ffn_Wqkv"][row, :, i * cols:(i + 1) * cols].rearrange("l p n -> p l n")) for i in range(3)]

            def ffn_weights(row):
                return [(wo[:].unsqueeze(1), a["L0_ffn_Wo"][row].rearrange("l (h p) d -> p l h d", p=P)),
                        (w1[:].unsqueeze(1), a["L0_ffn_W1"][row].rearrange("l p n -> p l n")),
                        (w2[:, 0:2, :].unsqueeze(1), a["L0_ffn_W2"][row, 0:256, :].rearrange("l (h p) d -> p l h d", p=P)),
                        (w2[0:FT[2][1], 2:3, :], a["L0_ffn_W2"][row, 256:FF, :].rearrange("l p d -> p l d")),
                        (vecs[:].unsqueeze(1), a["l_vectors"][row].rearrange("l p n -> p l n"))]

            A_DMA, F_DMA = 3 * 16, 5 * 16

            def layer(l):
                load(l, attention_weights)
                sp.wait_ge(w_ready.sem, l * (A_DMA + F_DMA) + A_DMA)
                sp.sem_inc(att_ok.sem, SEQS)
                sp.wait_ge(x_out.sem, (l + 1) * SEQS)
                load(l, ffn_weights)
                sp.wait_ge(w_ready.sem, (l + 1) * (A_DMA + F_DMA))
                sp.sem_inc(ffn_ok.sem, SEQS)

            layer(0)
            if DEPTH > 1:
                with sp.Fori(1, DEPTH) as l:
                    sp.wait_ge(v_proj.sem, l * SEQS * v_proj.per)
                    layer(l)

        @block.gpsimd
        def _(pool):
            pool.wait_ge(c_ready.sem, 80)

            def make_tables(l):
                row = bass.ds(l, 1)
                for j in range(2):
                    nc.gpsimd.tensor_tensor(cos_t[:, j, :, :], cos_base[:, j, :, :],
                                            qk_rows[:, row, j, :].to_broadcast([P, BLKS, AD]),
                                            ALU.mult).then_inc(tables.sem, 1)
                    for lo, hi in ((slice(0, 32), slice(32, 64)), (slice(32, 64), slice(0, 32))):
                        nc.gpsimd.tensor_tensor(sin_t[:, j, :, lo], sin_base[:, j, :, lo],
                                                qk_rows[:, row, j, hi].to_broadcast([P, BLKS, 32]),
                                                ALU.mult).then_inc(tables.sem, 1)
                pool.wait_ge(tables.sem, tables.upto(l, 6))
                pool.sem_inc(tables_ok.sem, SEQS)

            def rotate(it):
                for u in range(UNITS):
                    m = u // GROUPS
                    pool.wait_ge(qn_ready.sem, qn_ready.upto(it, u + 1))
                    wait_for(pool, q_roped, it, u)
                    wait_for(pool, k_roped, it, u)
                    for j in range(2):
                        src = qn[:, j, :].rearrange("p (h d) -> p h d", d=AD)
                        dst = t2[:, j, :].rearrange("p (h d) -> p h d", d=AD)
                        for lo, hi in ((slice(0, 32), slice(32, 64)), (slice(32, 64), slice(0, 32))):
                            nc.gpsimd.tensor_tensor(dst[:, :, lo], src[:, :, hi], bcast(sin_t[:, j, m, lo], 1, GH),
                                                    ALU.mult).then_inc(rotated.sem, 1)
                    pool.wait_ge(cosed.sem, cosed.upto(it, u + 1))
                    pool.wait_ge(rotated.sem, rotated.upto(it, 4 * u + 4))
                    nc.gpsimd.tensor_tensor(t1[:, 1, :], t1[:, 1, :], t2[:, 1, :], ALU.add).then_inc(k_roped.sem, 1)

            make_tables(0)
            rotate(0)
            if SEQS > 1:
                with pool.Fori(1, SEQS) as it:
                    rotate(it)
            if DEPTH > 1:
                with pool.Fori(1, DEPTH) as l:
                    pool.wait_ge(k_roped.sem, l * SEQS * k_roped.per)
                    make_tables(l)
                    settle(pool, settled.sem)
                    with pool.Fori(0, SEQS) as b:
                        rotate(l * SEQS + b)

        @block.vector
        def _(dve):
            def chained(instruction, signal, turn, n):
                instruction.then_inc(signal.sem, 1)
                wait_for(dve, signal, turn, n)

            def refine(tmp, x, guess, out, signal, turn, n):
                chained(nc.vector.tensor_tensor(tmp, guess, guess, ALU.mult), signal, turn, n + 1)
                chained(nc.vector.scalar_tensor_tensor(tmp, x, -0.5, tmp, ALU.mult, ALU.mult), signal, turn, n + 2)
                chained(nc.vector.scalar_tensor_tensor(out, tmp, 1.5, guess, ALU.add, ALU.mult), signal, turn, n + 3)

            nc.vector.memset(xs[:], 0.0)
            nc.vector.memset(xs1[:], 0.0)
            nc.vector.memset(kT[:, :, 1, 0, :], 0.0)
            dve.wait_ge(c_ready.sem, 80)
            nc.vector.tensor_copy(mask[:], mask_f[:])
            nc.vector.tensor_copy(ident_b[:], ident[:]).then_inc(consts.sem, 1)
            dve.wait_ge(consts.sem, 1)
            dve.sem_inc(x_out.sem, SEQS)
            nc.vector.tensor_copy(xs[0:64, WIN:].unsqueeze(1), xst[0:64, 0:1, :]).then_inc(xs_ready.sem, 1)

            def body(it, parts):
                def next_stream():
                    dve.wait_ge(v_proj.sem, v_proj.upto(it, v_proj.per))
                    dve.wait_ge(x_out.sem, it + 2)
                    nc.vector.tensor_copy(xs[0:64, WIN:].unsqueeze(1), xst[0:64, slot(it + 1), :]).then_inc(xs_ready.sem, 1)

                def softmax_begin(u):
                    dve.wait_ge(scored.sem, scored.upto(it, 2 * u + 2))
                    scores = ps[:].rearrange("p (h k) -> p h k", k=2 * WIN)
                    chained(nc.vector.reduce_max(mx[:], scores, axis=AX_X), max_ready, it, u + 1)
                    wait_for(dve, exped, it, u)
                    nc.vector.tensor_tensor(sim[:].rearrange("p (h k) -> p h k", k=2 * WIN), scores,
                                            bcast(mx[:], 2, 2 * WIN), ALU.subtract).then_inc(sim_ready.sem, 1)

                def softmax_sum(u):
                    dve.wait_ge(exped.sem, exped.upto(it, u + 1))
                    chained(nc.vector.reduce_sum(rs[:, u % 2, :], pr[:, u % 2, :].rearrange("p (h k) -> p h k", k=2 * WIN),
                                                 axis=AX_X), sums, it, 2 * u + 1)
                    chained(nc.vector.reciprocal(rinv[:, u % 2, :], rs[:, u % 2, :]), sums, it, 2 * u + 2)

                def norms(u):
                    dve.wait_ge(squared.sem, squared.upto(it, u + 1))
                    chained(nc.vector.reduce_sum(ssq[:], sq[:].rearrange("p j (h d) -> p (j h) d", d=AD), axis=AX_X),
                            ssq_ready, it, u + 1)
                    nc.vector.tensor_scalar(n2[:], ssq[:], NORM_MIN2, None, ALU.max).then_inc(n2_ready.sem, 1)

                def rope_begin(u):
                    m = u // GROUPS
                    dve.wait_ge(r0_ready.sem, r0_ready.upto(it, u + 1))
                    refine(nt[:], n2[:], r0[:], rr[:], refined, it, 3 * u)
                    chained(nc.vector.tensor_tensor(qn[:].rearrange("p j (h d) -> p (j h) d", d=AD),
                                                    pqk[:].rearrange("p j (h d) -> p (j h) d", d=AD),
                                                    bcast(rr[:], 2, AD), ALU.mult), qn_ready, it, u + 1)
                    wait_for(dve, k_turned, it, u)
                    if u == 0:
                        dve.wait_ge(tables_ok.sem, tables_ok.upto(it, 1))
                    nc.vector.tensor_tensor(t1[:].rearrange("p j (h d) -> p j h d", d=AD),
                                            qn[:].rearrange("p j (h d) -> p j h d", d=AD),
                                            bcast(cos_t[:, :, m, :], 2, GH), ALU.mult).then_inc(cosed.sem, 1)

                def rope_queries(u):
                    dve.wait_ge(cosed.sem, cosed.upto(it, u + 1))
                    dve.wait_ge(rotated.sem, rotated.upto(it, 4 * u + 2))
                    nc.vector.tensor_tensor(t1[:, 0, :], t1[:, 0, :], t2[:, 0, :], ALU.add).then_inc(q_roped.sem, 1)

                def normalise_out(u):
                    dve.wait_ge(weighed.sem, weighed.upto(it, 2 * u + 2))
                    wait_for(dve, o_turned, it, u)
                    nc.vector.tensor_tensor(on[:].rearrange("p (h d) -> p h d", d=AD),
                                            po[:].rearrange("p (h d) -> p h d", d=AD),
                                            bcast(rinv[:, u % 2, :], 2, AD), ALU.mult).then_inc(o_normed.sem, 1)

                def residual(j):
                    dve.wait_ge(y_ready.sem, y_ready.upto(j, 1))
                    nc.vector.tensor_tensor(x1[:].unsqueeze(1), pf[:].unsqueeze(1), xst[:, slot(j), :],
                                            ALU.add).then_inc(x1_ready.sem, 1)

                def moments(j):
                    dve.wait_ge(x1_turned.sem, x1_turned.upto(j, 1))
                    for i in range(BLKS):
                        nc.vector.bn_stats(stats[:, i, :], pf[:, i * P:(i + 1) * P]).then_inc(ln_steps.sem, 1)
                    dve.wait_ge(ln_steps.sem, ln_steps.upto(j, BLKS))
                    settle(dve, settled.sem)
                    for i in range(BLKS):
                        nc.vector.bn_aggr(mv[:, i, :], stats[:, i, :]).then_inc(ln_steps.sem, 1)
                    dve.wait_ge(ln_steps.sem, ln_steps.upto(j, 2 * BLKS))
                    nc.vector.tensor_scalar(fn2[:], mv[:, :, 1], LN_EPS, None, ALU.add).then_inc(fn2_ready.sem, 1)

                def normalise(j):
                    dve.wait_ge(fr0_ready.sem, fr0_ready.upto(j, 1))
                    refine(fnt[:], fn2[:], fr0[:], frr[:], ln_steps, j, 2 * BLKS)
                    for i in range(BLKS):
                        step = nc.vector.tensor_scalar(xh[:, i, :], pf[:, i * P:(i + 1) * P], mv[:, i, 0:1],
                                                       frr[:, i:i + 1], ALU.subtract, ALU.mult)
                        step.then_inc(xh_ready.sem if i == BLKS - 1 else ln_steps.sem, 1)

                def hidden(j, i):
                    n = FT[i][1]
                    dve.wait_ge(gelued.sem, gelued.upto(j, 2))
                    dve.wait_ge(up.sem, up.upto(j, 3 + i + 1))
                    nc.vector.scalar_tensor_tensor(hid[0:n, i, :], pf[0:n, :], b1[0:n, i:i + 1],
                                                   gl[0:n, i, :], ALU.add, ALU.mult).then_inc(hid_ready.sem, 1)

                def stream_out(j):
                    dve.wait_ge(down.sem, down.upto(j, 1))
                    dve.wait_ge(x1_ready.sem, x1_ready.upto(j, 1))
                    nc.vector.scalar_tensor_tensor(xst[:, slot(j), :], pf[:].unsqueeze(1), b2[:, 0:1], x1[:].unsqueeze(1),
                                                   ALU.add, ALU.add).then_inc(x_out.sem, 1)

                for s in range(UNITS):
                    if parts.has(s):
                        norms(s)
                    if s == 1 and parts.ffn_end:
                        hidden(it - 2, 1)
                    if s == 2 and parts.ffn_end:
                        stream_out(it - 2)
                    if s == 4 and parts.ffn:
                        residual(it - 1)
                    if parts.has(s - 3):
                        normalise_out(s - 3)
                    if parts.has(s - 2):
                        softmax_sum(s - 2)
                    if parts.has(s):
                        rope_begin(s)
                    if s == 0 and parts.ffn_end:
                        hidden(it - 2, 0)
                    if s == 1 and parts.ffn_end:
                        hidden(it - 2, 2)
                    if s == 5 and parts.ffn:
                        normalise(it - 1)
                    if s == UNITS - 1 and parts.next:
                        next_stream()
                    if parts.has(s - 1):
                        softmax_begin(s - 1)
                    if parts.has(s):
                        rope_queries(s)
                    if s == 4 and parts.ffn:
                        moments(it - 1)

            turns(dve, body)

        @block.scalar
        def _(act):
            nc.scalar.preload_act_table_set("natural_log_exp_and_others")
            act.wait_ge(consts.sem, 1)
            nc.scalar.copy(xs[64:128, WIN + 1:].unsqueeze(1), xst[64:128, 0:1, 0:T - 1]).then_inc(xs_ready.sem, 1)

            def body(it, parts):
                def keep_square(u):
                    act.wait_ge(qk_proj.sem, qk_proj.upto(it, u + 1))
                    nc.scalar.activation(sq[:], pqk[:], ACT.Square).then_inc(squared.sem, 1)

                def keep_q(u):
                    act.wait_ge(q_turned.sem, q_turned.upto(it, u + 1))
                    nc.scalar.copy(qT[:].rearrange("p h t -> p (h t)"), pta[:]).then_inc(q_out.sem, 1)

                def keep_k(u):
                    m, g = divmod(u % UNITS, GROUPS)
                    act.wait_ge(k_turned.sem, k_turned.upto(it, u + 1))
                    places = slice(2 * m + 1, 2 * m + 3)
                    nc.scalar.copy(kT[:, g * GHP:(g + 1) * GHP, :, places, :],
                                   ptb[:].rearrange("p (h k w t) -> p h w k t", w=2, t=WIN, k=2)).then_inc(k_out.sem, 1)

                def guess_norm(u):
                    act.wait_ge(n2_ready.sem, n2_ready.upto(it, u + 1))
                    nc.scalar.activation(lnv[:], n2[:], ACT.Ln).then_inc(ln_ready.sem, 1)
                    act.wait_ge(ln_ready.sem, ln_ready.upto(it, u + 1))
                    nc.scalar.activation(r0[:], lnv[:], ACT.Exp, scale=-0.5).then_inc(r0_ready.sem, 1)

                def keep_values(k):
                    act.wait_ge(v_proj.sem, v_proj.upto(it, k + 1))
                    for w in (2 * k, 2 * k + 1):
                        nc.scalar.copy(V[:, (w // WPB) % 2, w % WPB, :], pv[:]).then_inc(v_out.sem, 1)

                def mix_values(k):
                    at, before = 2 * k, 2 * k - 1
                    act.wait_ge(v_out.sem, v_out.upto(it, at + 1))
                    for rows in (slice(WIN, 2 * WIN), slice(3 * WIN, 4 * WIN)):
                        nc.scalar.copy(V[rows, (at // WPB) % 2, at % WPB, :],
                                       V[rows, (before // WPB) % 2, before % WPB, :]).then_inc(v_mixed.sem, 1)

                def keep_p(u):
                    act.wait_ge(p_turned.sem, p_turned.upto(it, u + 1))
                    nc.scalar.copy(prT[:].rearrange("p h t -> p (h t)"), pta[:]).then_inc(p_out.sem, 1)

                def keep_o(u):
                    m, g = divmod(u % UNITS, GROUPS)
                    act.wait_ge(o_turned.sem, o_turned.upto(it, u + 1))
                    nc.scalar.copy(oT[:, g * GHP:(g + 1) * GHP, m * P:(m + 1) * P],
                                   ptb[:].rearrange("p (h t) -> p h t", t=P)).then_inc(o_out.sem, 1)

                def exponentials(u):
                    act.wait_ge(sim_ready.sem, sim_ready.upto(it, u + 1))
                    wait_for(act, p_turned, it, u - 1)
                    wait_for(act, sums, it, 2 * (u - 1))
                    nc.scalar.activation(pr[:, u % 2, :], sim[:], ACT.Exp, scale=QK_SCALE).then_inc(exped.sem, 1)

                def next_stream():
                    act.wait_ge(v_proj.sem, v_proj.upto(it, v_proj.per))
                    act.wait_ge(x_out.sem, it + 2)
                    nc.scalar.copy(xs[64:128, WIN + 1:].unsqueeze(1), xst[64:128, slot(it + 1), 0:T - 1]).then_inc(xs_ready.sem, 1)

                def shift(j):
                    act.wait_ge(x1_ready.sem, x1_ready.upto(j, 1))
                    nc.scalar.copy(xs1[0:64, :], x1[0:64, :]).then_inc(xs1_ready.sem, 1)
                    nc.scalar.copy(xs1[64:128, 1:T], x1[64:128, 0:T - 1]).then_inc(xs1_ready.sem, 1)

                def guess_std(j):
                    act.wait_ge(fn2_ready.sem, fn2_ready.upto(j, 1))
                    nc.scalar.activation(flnv[:], fn2[:], ACT.Ln).then_inc(fln_ready.sem, 1)
                    act.wait_ge(fln_ready.sem, fln_ready.upto(j, 1))
                    nc.scalar.activation(fr0[:], flnv[:], ACT.Exp, scale=-0.5).then_inc(fr0_ready.sem, 1)

                def keep_normed(j):
                    act.wait_ge(xh_turned.sem, xh_turned.upto(j, 1))
                    nc.scalar.activation(xnT[:], pf[:], ACT.Identity, bias=ln_b[:, 0:1], scale=ln_g[:, 0:1]).then_inc(xn_ready.sem, 1)

                def keep_gate(j, i):
                    n = FT[i][1]
                    act.wait_ge(up.sem, up.upto(j, i + 1))
                    nc.scalar.activation(gpre[0:n, i, :], pf[0:n, :], ACT.Identity, bias=b1[0:n, 3 + i:4 + i]).then_inc(g_out.sem, 1)

                def gelu(j):
                    n = FT[2][1]
                    act.wait_ge(g_out.sem, g_out.upto(j, 3))
                    nc.scalar.activation(gl[:, 0:2, :], gpre[:, 0:2, :], ACT.Gelu).then_inc(gelued.sem, 1)
                    nc.scalar.activation(gl[0:n, 2, :], gpre[0:n, 2, :], ACT.Gelu).then_inc(gelued.sem, 1)
                    nc.scalar.preload_act_table_set("natural_log_exp_and_others")

                for s in range(UNITS):
                    if parts.has(s):
                        keep_square(s)
                    if parts.has(s - 2):
                        exponentials(s - 2)
                    if s == 7 and parts.ffn:
                        keep_gate(it - 1, 0)
                    if parts.has(s - 4):
                        keep_o(s - 4)
                    if parts.has(s - 1):
                        keep_q(s - 1)
                        keep_k(s - 1)
                    if parts.has(s):
                        guess_norm(s)
                    if s == 5 and parts.ffn:
                        guess_std(it - 1)
                    if parts.has(s):
                        keep_values(s)
                    if s == 0 and parts.ffn_end:
                        gelu(it - 2)
                    if s == 4 and parts.ffn:
                        shift(it - 1)
                    if s == 6 and parts.ffn:
                        keep_normed(it - 1)
                    if s == 7 and parts.ffn:
                        keep_gate(it - 1, 1)
                    if parts.has(s - 2):
                        keep_p(s - 2)
                    if parts.has(s) and s:
                        mix_values(s)
                    if s == UNITS - 1 and parts.next:
                        next_stream()
                    if s == 7 and parts.ffn:
                        keep_gate(it - 1, 2)

            turns(act, body)

        @block.tensor
        def _(pe):
            mm = nc.tensor.matmul
            pe.wait_ge(consts.sem, 1)

            def body(it, parts):
                def project(u):
                    m, g = divmod(u, GROUPS)
                    if u == 0:
                        pe.wait_ge(att_ok.sem, att_ok.upto(it, 1))
                        pe.wait_ge(xs_ready.sem, xs_ready.upto(it, 2))
                    wait_for(pe, qn_ready, it, u)
                    for j in range(2):
                        at = j * AI + g * GH * AD
                        last = mm(pqk[:, j, :], xs[:, WIN + m * P:WIN + (m + 1) * P], wqkv[:, at:at + GH * AD],
                                  start=True, stop=True)
                    last.then_inc(qk_proj.sem, 1)

                def turn(bank, src, done):
                    for i in range(GHP):
                        last = nc.tensor.transpose(bank[:, i * P:(i + 1) * P], src[:, i * P:(i + 1) * P], ident[:])
                    last.then_inc(done.sem, 1)

                def turn_q(u):
                    pe.wait_ge(q_roped.sem, q_roped.upto(it, u + 1))
                    wait_for(pe, p_out, it, u - 1)
                    turn(pta, t1[:, 0, :], q_turned)

                def turn_k(u):
                    pe.wait_ge(k_roped.sem, k_roped.upto(it, u + 1))
                    wait_for(pe, o_out, it, u - 2)
                    turn(ptb, t1[:, 1, :], k_turned)

                def turn_p(u):
                    pe.wait_ge(exped.sem, exped.upto(it, u + 1))
                    if parts.has(u + 1):
                        pe.wait_ge(q_out.sem, q_out.upto(it, u + 2))
                    else:
                        wait_for(pe, p_out, it, u)
                    turn(pta, pr[:, u % 2, :], p_turned)

                def turn_o(u):
                    pe.wait_ge(o_normed.sem, o_normed.upto(it, u + 1))
                    if parts.has(u + 2):
                        pe.wait_ge(k_out.sem, k_out.upto(it, u + 3))
                    else:
                        wait_for(pe, o_out, it, u)
                    turn(ptb, on[:], o_turned)

                def values(k):
                    wait_for(pe, v_out, it, 2 * k)
                    settle(pe, settled.sem)
                    for e in range(2):
                        cols = wqkv[:, 2 * AI:3 * AI].rearrange("p (h e d) -> p e h d", e=2, d=AD)[:, e, :, :]
                        last = mm(pv[64 * e:64 * e + 64, :], xs[:, WIN + 64 * k:WIN + 64 * (k + 1)], cols, start=True, stop=True,
                                  skip_group_check=True)
                    last.then_inc(v_proj.sem, 1)

                def score(u, e):
                    m, g = divmod(u % UNITS, GROUPS)
                    if e == 0:
                        pe.wait_ge(q_out.sem, q_out.upto(it, u + 1))
                        pe.wait_ge(k_out.sem, k_out.upto(it, u + 1))
                        wait_for(pe, sim_ready, it, u)
                        mm(ps[:], ident_b[:], mask[:, 0 if m == 0 else 1, :], start=True, stop=False, skip_group_check=True)
                    else:
                        pe.wait_ge(scored.sem, scored.upto(it, 2 * u + 1))
                        settle(pe, settled.sem)
                    rows = slice(64 * e, 64 * e + 64)
                    for h in range(e, GH, 2):
                        for w in range(WPB):
                            k = (m * WPB + w) // 2
                            keys = kT[rows, g * GHP + h // 2, :, :, :].rearrange("p s k t -> p (s k) t")
                            places = slice(k + 1, k + 1 + PAIRS + 1, PAIRS) if w % 2 == 0 else slice(k + 1, k + 1 + PAIRS + 2, PAIRS + 1)
                            last = mm(ps[WIN * w:WIN * (w + 1), 2 * WIN * h:2 * WIN * (h + 1)],
                                      qT[rows, h // 2, WIN * w:WIN * (w + 1)],
                                      keys[:, places, :],
                                      start=False, stop=(h >= GH - 2), skip_group_check=True)
                    last.then_inc(scored.sem, 1)

                def weigh(u, e):
                    m, g = divmod(u % UNITS, GROUPS)
                    if e == 0:
                        pe.wait_ge(p_out.sem, p_out.upto(it, u + 1))
                        wait_for(pe, o_normed, it, u)
                        pe.wait_ge(v_out.sem, v_out.upto(it, WPB * (u // GROUPS + 1)))
                        pe.wait_ge(v_mixed.sem, v_mixed.upto(it if u >= 0 else it - 1, WPB * (m + 1) - 2))
                    else:
                        pe.wait_ge(weighed.sem, weighed.upto(it, 2 * u + 1))
                    settle(pe, settled.sem)
                    rows = slice(64 * e, 64 * e + 64)
                    for h in range(e, GH, 2):
                        hp = g * GHP + h // 2
                        for w in range(WPB):
                            last = mm(po[WIN * w:WIN * (w + 1), AD * h:AD * (h + 1)],
                                      prT[rows, h // 2, WIN * w:WIN * (w + 1)],
                                      V[rows, m % 2, w, AD * hp:AD * (hp + 1)],
                                      start=True, stop=True, skip_group_check=True)
                    last.then_inc(weighed.sem, 1)

                def project_out(j, quarter):
                    if quarter == 0:
                        pe.wait_ge(ffn_ok.sem, ffn_ok.upto(j, 1))
                        pe.wait_ge(o_out.sem, o_out.upto(j, UNITS - 1))
                        pe.wait_ge(x_out.sem, SEQS + j)
                    if quarter == 2:
                        pe.wait_ge(o_out.sem, o_out.upto(j, UNITS))
                    for i in range(quarter * AHP // 4, (quarter + 1) * AHP // 4):
                        last = mm(pf[:], wo[:, i, :], oT[:, i, :], start=(i == 0), stop=(i == AHP - 1),
                                  skip_group_check=True)
                    if quarter == 3:
                        last.then_inc(y_ready.sem, 1)

                def turn_x1(j):
                    pe.wait_ge(xs1_ready.sem, xs1_ready.upto(j, 2))
                    turn(pf, xs1[:], x1_turned)

                def turn_xh(j):
                    pe.wait_ge(xh_ready.sem, xh_ready.upto(j, 1))
                    turn(pf, xh[:].rearrange("p b t -> p (b t)"), xh_turned)

                def gate_up(j, i):
                    if i == 0:
                        pe.wait_ge(xn_ready.sem, xn_ready.upto(j, 1))
                    else:
                        pe.wait_ge(g_out.sem, g_out.upto(j, i))
                    at, n = FT[i]
                    mm(pf[0:n, :], w1[:, FF + at:FF + at + n], xnT[:], start=True, stop=True).then_inc(up.sem, 1)

                def value_up(j, i):
                    if i == 0:
                        pe.wait_ge(g_out.sem, g_out.upto(j, 3))
                    else:
                        pe.wait_ge(hid_ready.sem, hid_ready.upto(j, i))
                    at, n = FT[i]
                    mm(pf[0:n, :], w1[:, at:at + n], xnT[:], start=True, stop=True).then_inc(up.sem, 1)

                def project_down(j):
                    pe.wait_ge(hid_ready.sem, hid_ready.upto(j, 3))
                    for i, (_, n) in enumerate(FT):
                        last = mm(pf[:], w2[0:n, i, :], hid[0:n, i, :], start=(i == 0), stop=(i == 2))
                    last.then_inc(down.sem, 1)

                for s in range(UNITS):
                    if parts.has(s):
                        project(s)
                    if s == 1 and parts.ffn_end:
                        value_up(it - 2, 1)
                    if s == 2 and parts.ffn_end:
                        project_down(it - 2)
                    if s in (3, 4) and parts.ffn:
                        project_out(it - 1, 2 * (s - 3) + 1)
                    if s == 7 and parts.ffn:
                        gate_up(it - 1, 0)
                    if parts.has(s - 3):
                        weigh(s - 3, 0)
                    if parts.has(s - 4):
                        turn_o(s - 4)
                    if parts.has(s - 3):
                        weigh(s - 3, 1)
                    if parts.has(s - 1):
                        turn_q(s - 1)
                        turn_k(s - 1)
                    if parts.has(s):
                        values(s)
                    if s == 0 and parts.ffn_end:
                        value_up(it - 2, 0)
                    if s == 1 and parts.ffn_end:
                        value_up(it - 2, 2)
                    if s in (2, 3) and parts.ffn:
                        project_out(it - 1, 2 * (s - 2))
                    if s == 6 and parts.ffn:
                        turn_xh(it - 1)
                    if s == 7 and parts.ffn:
                        gate_up(it - 1, 1)
                    if parts.has(s - 1):
                        score(s - 1, 0)
                    if parts.has(s - 2):
                        turn_p(s - 2)
                    if parts.has(s - 1):
                        score(s - 1, 1)
                    if s == 4 and parts.ffn:
                        turn_x1(it - 1)
                    if s == 7 and parts.ffn:
                        gate_up(it - 1, 2)

            turns(pe, body)


def combine(nc, a, xst, acc, ident):
    ctx = ExitStack()
    with ctx:
        res = ctx.enter_context(nc.sbuf_tensor("c_res", [P, 2, T], F32))
        tok = ctx.enter_context(nc.sbuf_tensor("c_tok", [P, 2, T], F32))
        banks = [ctx.enter_context(nc.psum_tensor(f"c_p{i}", [P, T], F32)) for i in range(2)]
        added, turned, copied, stored = (ctx.enter_context(nc.semaphore("c_" + n)) for n in ("added", "turned", "copied", "stored"))
        out_d = a["out"].rearrange("s (b p) d -> s p b d", p=P)
        block = ctx.enter_context(nc.Block())

        @block.vector
        def _(dve):
            for b in range(SEQS):
                if b >= 2:
                    dve.wait_ge(turned, b - 1)
                nc.vector.tensor_tensor(res[:, b % 2, :], xst[:, b, :], acc[:, b, :], ALU.add).then_inc(added, 1)

        @block.tensor
        def _(pe):
            for b in range(SEQS):
                pe.wait_ge(added, b + 1)
                if b >= 2:
                    pe.wait_ge(copied, b - 1)
                for i in range(BLKS):
                    last = nc.tensor.transpose(banks[b % 2][:, i * P:(i + 1) * P], res[:, b % 2, i * P:(i + 1) * P], ident[:])
                last.then_inc(turned, 1)

        @block.scalar
        def _(act):
            for b in range(SEQS):
                act.wait_ge(turned, b + 1)
                if b >= 2:
                    act.wait_ge(stored, 16 * (b - 1))
                nc.scalar.copy(tok[:, b % 2, :], banks[b % 2][:]).then_inc(copied, 1)

        @block.sync
        def _(sp):
            for b in range(SEQS):
                sp.wait_ge(copied, b + 1)
                if b:
                    sp.wait_ge(stored, 16 * b)
                sp.dma_start(out_d[b], tok[:, b % 2, :].rearrange("p (b d) -> p b d", d=D)).then_inc(stored, 16)
            sp.wait_ge(stored, 16 * SEQS)


_INS = ["L0_attn_x", "L0_attn_Wq", "L0_attn_Wk", "L0_attn_Wv", "L0_attn_Wa", "L0_attn_Wo",
        "L0_ffn_Wqkv", "L0_ffn_q_scale", "L0_ffn_k_scale", "L0_ffn_Wo", "L0_ffn_W1", "L0_ffn_W2"]


def vectors(inputs):
    import numpy as np
    ba = np.asarray(inputs["L0_attn_ba"]).reshape(RHP, P)
    r = np.stack([*ba, np.asarray(inputs["L0_attn_gamma"]), np.asarray(inputs["L0_attn_beta"])], 1)
    b1 = np.asarray(inputs["L0_ffn_b1"])
    out = np.zeros((DEPTH, P, 9), b1.dtype)
    for part in range(2):
        for j, (at, n) in enumerate(FT):
            out[:, 0:n, 3 * part + j] = b1[:, part * FF + at:part * FF + at + n]
    for j, name in enumerate(("L0_ffn_b2", "L0_ffn_ln_g", "L0_ffn_ln_b")):
        out[:, :, 6 + j] = np.asarray(inputs[name])
    return {"r_vectors": np.ascontiguousarray(r), "l_vectors": out}


def shape_constants():
    import numpy as np
    f = np.float32
    half = np.arange(0, AD, 2, dtype=f)
    inv_freq = (f(1.0) / np.power(f(10000.0), half / f(AD))).astype(f)
    t = np.arange(T, dtype=f)
    freqs = (t[:, None] * inv_freq[None, :]).astype(f)
    freqs = np.concatenate([freqs, freqs], -1)
    base = ((half + f(0.4 * AD)) / f(1.4 * AD)).astype(f)
    power = ((t - T // 2) / f(WIN // 2)).astype(f)
    scale = np.power(base[None, :], power[:, None]).astype(f)
    scale = np.concatenate([scale, scale], -1)
    sign = np.where(np.arange(AD) < AD // 2, f(-1), f(1))
    cos, sin = np.cos(freqs), np.sin(freqs) * sign
    both = lambda x: np.ascontiguousarray(
        np.stack([x * scale, x / scale]).reshape(2, BLKS, P, AD).transpose(2, 0, 1, 3).astype(f))
    i = np.arange(P) % WIN
    even = (np.arange(P) // WIN) % 2 == 0
    key = np.arange(2 * WIN)
    prev = (key[None, :] < WIN) != even[:, None]
    ok = np.where(prev, key[None, :] % WIN >= i[:, None], key[None, :] % WIN <= i[:, None])
    first_window = (np.arange(P) < WIN)[:, None] & prev
    m = np.where(ok, f(0), f(MASKED))
    m0 = np.where(first_window, f(MASKED), m)
    window_mask = np.stack([np.tile(m0, (1, GH)), np.tile(m, (1, GH))], 1).astype(f)
    p, j = np.arange(P) % HALF, np.arange(HALF)
    same = np.stack([(p[:, None] >> lv) == (j[None, :] >> lv) for lv in range(LEVELS)], 1)
    own = (np.arange(P)[:, None] // HALF) == np.arange(2)[None, :]
    level = (own[:, None, :, None] & same[:, :, None, :]).reshape(P, LEVELS, P).astype(f)
    return {"ident": np.eye(P, dtype=f), "level_masks": level, "rope_cos": both(cos), "rope_sin": both(sin),
            "window_mask": window_mask}


def kernel(**inputs):
    import numpy as np
    import concourse.bacc as bacc
    from concourse.bass_utils import run_bass_kernel_spmd

    nc = bacc.Bacc("TRN2", target_bir_lowering=False, num_devices=1)
    arrays, aps = {}, {}
    for name in _INS:
        arrays[name + "_dram"] = np.ascontiguousarray(inputs[name])
    for name, table in {**vectors(inputs), **shape_constants()}.items():
        arrays[name + "_dram"] = table
    for key, x in arrays.items():
        aps[key[:-5]] = nc.dram_tensor(key, x.shape, mybir.dt.from_np(x.dtype), kind="ExternalInput").ap()
    aps["out"] = nc.dram_tensor("out_dram", (SEQS, T, D), F32, kind="ExternalOutput").ap()
    build(nc, aps)
    r = run_bass_kernel_spmd(nc, [arrays], core_ids=[0])
    return r.results[0]["out_dram"]
```
